# Optimizing a Trainium2 kernel written in Bass

```python
import numpy as np
import jax
import jax.numpy as jnp

def _softmax(x, axis=-1):
    return jax.nn.softmax(x, axis=axis)

def _gelu(x):
    return jax.nn.gelu(x, approximate=True)

def _silu(x):
    return jax.nn.silu(x)

def _sigmoid(x):
    return jax.nn.sigmoid(x)

def _layernorm(x, axis=-1, eps=1e-05):
    m = jnp.mean(x, axis=axis, keepdims=True)
    v = jnp.var(x, axis=axis, keepdims=True)
    return (x - m) / jnp.sqrt(v + eps)

def _scatter_add(tgt, idx, src, axis=0):
    return tgt.at[idx].add(src)

def _segment_sum(src, seg, n):
    return jax.ops.segment_sum(src, seg, n)
kernel_name = 'mk_vit_tower_cls_d4_tok_img768_r4_821ad7'

def setup_inputs(seed: int=0):
    np.random.seed(seed)
    _w = jnp.asarray

    def _rec_inputs():
        import jax
        import jax.numpy as jnp
        _rk = jax.random.key(seed)
        x = 7.57192e-06 + 1.00007 * jax.random.normal(jax.random.fold_in(_rk, 1), (32, 3, 112, 112), jnp.float32)
        cls_tok = 0.02 * jax.random.normal(jax.random.fold_in(_rk, 5), (1, 1, 192), jnp.float32)
        return (x, cls_tok)
    x, cls_tok = _rec_inputs()

    def _L0_tok_setup():
        import jax, jax.numpy as jnp
        import numpy as np
        PATCH = 16

        def _shift2d(x, shift):
            l, r, t, b = shift
            H, W = (x.shape[2], x.shape[3])
            xp = jnp.pad(x, ((0, 0), (0, 0), (max(t, 0), max(b, 0)), (max(l, 0), max(r, 0))))
            h0 = max(-t, 0)
            w0 = max(-l, 0)
            return xp[:, :, h0:h0 + H, w0:w0 + W]
        key = jax.random.key(seed)
        k1, k2 = jax.random.split(key)
        B, C, H, W = (64, 3, 224, 224)
        dim = 192
        patch_dim = PATCH * PATCH * 5 * C
        x = jax.random.normal(k1, (B, C, H, W), dtype=jnp.float32)
        ln_weight = jnp.ones((patch_dim,), dtype=jnp.float32)
        ln_bias = jnp.zeros((patch_dim,), dtype=jnp.float32)
        proj_weight = jax.random.normal(k2, (dim, patch_dim), dtype=jnp.float32) * patch_dim ** (-0.5)
        proj_bias = jnp.zeros((dim,), dtype=jnp.float32)
        return {'x': x, 'ln_weight': ln_weight, 'ln_bias': ln_bias, 'proj_weight': proj_weight, 'proj_bias': proj_bias}
    _L0_tok_all = _L0_tok_setup()
    _L0_tok_in = {k: v for k, v in _L0_tok_all.items() if k in ('ln_weight', 'ln_bias', 'proj_weight', 'proj_bias')}
    del _L0_tok_all

    def _L0_attn_setup():
        import jax, jax.numpy as jnp
        import numpy as np
        from jax import lax
        B_SZ, L, D, N, R = (1, 1024, 192, 16, 48)

        def _soft_clamp(x, lo=0.0001, hi=10.0):
            center = (hi + lo) / 2.0
            half_range = (hi - lo) / 2.0
            return center + half_range * jnp.tanh((x - center) / half_range)
        key = jax.random.key(seed)
        ks = jax.random.split(key, 6)
        x = jax.random.normal(ks[0], (B_SZ, L, D), jnp.float32)
        A_log = jnp.log(jnp.broadcast_to(jnp.arange(1, N + 1, dtype=jnp.float32), (D, N)))
        D_param = jnp.ones((D,), jnp.float32)
        W_bc = jax.random.normal(ks[1], (D, 2 * N), jnp.float32) / np.sqrt(D).astype(np.float32)
        W_dt = jax.random.normal(ks[2], (D, R), jnp.float32) / np.sqrt(D).astype(np.float32)
        W_dtp = jax.random.normal(ks[3], (R, D), jnp.float32) / np.sqrt(R).astype(np.float32)
        dt = jax.random.uniform(ks[4], (D,), jnp.float32, 0.001, 0.1)
        dt = jnp.clip(dt, 0.0001)
        b_dt = dt + jnp.log(-jnp.expm1(-dt))
        rms_scale = jnp.ones((D,), jnp.float32)
        return {'x': x, 'A_log': A_log, 'D_param': D_param, 'W_bc': W_bc, 'W_dt': W_dt, 'W_dtp': W_dtp, 'b_dt': b_dt, 'rms_scale': rms_scale}
    _L0_attn_all = _L0_attn_setup()
    _L0_attn_in = {k: v for k, v in _L0_attn_all.items() if k in ('A_log', 'D_param', 'W_bc', 'W_dt', 'W_dtp', 'b_dt', 'rms_scale')}
    del _L0_attn_all

    def _L0_ffn_setup():
        import jax, jax.numpy as jnp
        import numpy as np
        H = 192
        R = 64
        E = 8
        B, S = (8, 512)
        key = jax.random.key(seed)
        ks = jax.random.split(key, 10)
        s_in = 1.0 / np.sqrt(H)
        s_r = 1.0 / np.sqrt(R)
        return {'x': jax.random.normal(ks[0], (B, S, H), dtype=jnp.float32), 'enc_w': jax.random.uniform(ks[1], (H, R), jnp.float32, -s_in, s_in), 'enc_b': jax.random.uniform(ks[2], (R,), jnp.float32, -s_in, s_in), 'sw_w': jax.random.uniform(ks[3], (R, E), jnp.float32, -s_r, s_r), 'sw_b': jax.random.uniform(ks[4], (E,), jnp.float32, -s_r, s_r), 'w1': jax.random.uniform(ks[5], (E, H, R), jnp.float32, -s_in, s_in), 'b1': jax.random.uniform(ks[6], (E, R), jnp.float32, -s_in, s_in), 'w2': jax.random.uniform(ks[7], (E, R, H), jnp.float32, -s_r, s_r), 'b2': jax.random.uniform(ks[8], (E, H), jnp.float32, -s_r, s_r)}
    _L0_ffn_all = _L0_ffn_setup()
    _L0_ffn_in = {k: v for k, v in _L0_ffn_all.items() if k in ('enc_w', 'enc_b', 'sw_w', 'sw_b', 'w1', 'b1', 'w2', 'b2')}
    del _L0_ffn_all

    def _L1_attn_setup():
        import jax, jax.numpy as jnp
        import numpy as np
        key = jax.random.key(seed)
        ks = jax.random.split(key, 4)
        B, S, D = (8, 512, 192)
        lim = (6.0 / (D + D)) ** 0.5
        Z = jax.random.normal(ks[0], (B, S, D), dtype=jnp.float32)
        Wq = jax.random.uniform(ks[1], (D, D), dtype=jnp.float32, minval=-lim, maxval=lim)
        Wk = jax.random.uniform(ks[2], (D, D), dtype=jnp.float32, minval=-lim, maxval=lim)
        Wv = jax.random.uniform(ks[3], (D, D), dtype=jnp.float32, minval=-lim, maxval=lim)
        bq = jnp.zeros((D,), dtype=jnp.float32)
        bk = jnp.zeros((D,), dtype=jnp.float32)
        bv = jnp.zeros((D,), dtype=jnp.float32)
        return {'Z': Z, 'Wq': Wq, 'bq': bq, 'Wk': Wk, 'bk': bk, 'Wv': Wv, 'bv': bv}
    _L1_attn_all = _L1_attn_setup()
    _L1_attn_in = {k: v for k, v in _L1_attn_all.items() if k in ('Wq', 'bq', 'Wk', 'bk', 'Wv', 'bv')}
    del _L1_attn_all

    def _L1_ffn_setup():
        import jax, jax.numpy as jnp
        import numpy as np
        B, N, DIM, HEADS = (4, 256, 192, 12)
        HIDDEN, E, TOPK = (768, 8, 2)
        EPS = 1e-05

        def _layernorm(x, g, b):
            mu = jnp.mean(x, axis=-1, keepdims=True)
            var = jnp.var(x, axis=-1, keepdims=True)
            return (x - mu) * jax.lax.rsqrt(var + EPS) * g + b
        key = jax.random.key(seed)
        ks = jax.random.split(key, 10)
        s = 0.02
        return {'x': jax.random.normal(ks[0], (B, N, DIM), dtype=jnp.float32), 'ln1_g': jnp.ones((DIM,), jnp.float32), 'ln1_b': jnp.zeros((DIM,), jnp.float32), 'qkv_w': jax.random.normal(ks[1], (3 * DIM, DIM), jnp.float32) * s, 'proj_w': jax.random.normal(ks[2], (DIM, DIM), jnp.float32) * s, 'proj_b': jnp.zeros((DIM,), jnp.float32), 'ln2_g': jnp.ones((DIM,), jnp.float32), 'ln2_b': jnp.zeros((DIM,), jnp.float32), 'gate_w': jax.random.normal(ks[3], (E, DIM), jnp.float32) * s, 'gate_b': jnp.zeros((E,), jnp.float32), 'w1': jax.random.normal(ks[4], (E, HIDDEN, DIM), jnp.float32) * s, 'b1': jnp.zeros((E, HIDDEN), jnp.float32), 'w2': jax.random.normal(ks[5], (E, DIM, HIDDEN), jnp.float32) * s, 'b2': jnp.zeros((E, DIM), jnp.float32)}
    _L1_ffn_all = _L1_ffn_setup()
    _L1_ffn_in = {k: v for k, v in _L1_ffn_all.items() if k in ('ln1_g', 'ln1_b', 'qkv_w', 'proj_w', 'proj_b', 'ln2_g', 'ln2_b', 'gate_w', 'gate_b', 'w1', 'b1', 'w2', 'b2')}
    del _L1_ffn_all

    def _L2_attn_setup():
        import jax, jax.numpy as jnp
        import numpy as np
        B, N, C, H = (4, 512, 192, 12)
        D = C // H
        EPS = 1e-12

        def _l2norm(t):
            n = jnp.sqrt(jnp.sum(t * t, axis=-1, keepdims=True))
            return t / jnp.maximum(n, EPS)
        key = jax.random.key(seed)
        ks = jax.random.split(key, 8)
        s = 0.02
        return {'x': jax.random.normal(ks[0], (B, N, C), dtype=jnp.float32), 'Wq': jax.random.normal(ks[1], (C, C), dtype=jnp.float32) * s, 'bq': jnp.zeros((C,), dtype=jnp.float32), 'Wkv': jax.random.normal(ks[2], (C, 2 * C), dtype=jnp.float32) * s, 'bkv': jnp.zeros((2 * C,), dtype=jnp.float32), 'Wproj': jax.random.normal(ks[3], (C, C), dtype=jnp.float32) * s, 'bproj': jnp.zeros((C,), dtype=jnp.float32), 'scale': jnp.full((1, H, 1, 1), D ** (-0.5), dtype=jnp.float32)}
    _L2_attn_all = _L2_attn_setup()
    _L2_attn_in = {k: v for k, v in _L2_attn_all.items() if k in ('Wq', 'bq', 'Wkv', 'bkv', 'Wproj', 'bproj', 'scale')}
    del _L2_attn_all

    def _L2_ffn_setup():
        import jax, jax.numpy as jnp
        import numpy as np
        NUM_EXPERTS = 8
        TOP_K = 2
        CAPACITY_FACTOR = 1.25
        MAX_GROUP_SIZE = 1024
        MIN_EXPERT_CAPACITY = 4

        def _moe_forward(x, w_router, wi, wo):
            B, T, D = x.shape
            E = NUM_EXPERTS
            num_tokens = B * T
            G = max(num_tokens // MAX_GROUP_SIZE, E)
            while num_tokens % G != 0 or G % E != 0:
                G += 1
            S = num_tokens // G
            C = max(int(TOP_K * CAPACITY_FACTOR * S / E), MIN_EXPERT_CAPACITY)
            xg = x.reshape(G, S, D)
            logits = jnp.einsum('gsd,de->gse', xg.astype(jnp.float32), w_router.astype(jnp.float32))
            probs = jax.nn.softmax(logits, axis=-1)
            gate, idx = jax.lax.top_k(probs, TOP_K)
            idx_kf = jnp.swapaxes(idx, 1, 2).reshape(G, TOP_K * S)
            mask = jax.nn.one_hot(idx_kf, E, dtype=jnp.int32)
            prio = jnp.cumsum(mask, axis=1) * mask - 1
            prio = jnp.swapaxes(prio.reshape(G, TOP_K, S, E), 1, 2)
            prio_se = prio.max(axis=2)
            gate_se = jnp.einsum('gsk,gske->gse', gate, jax.nn.one_hot(idx, E, dtype=gate.dtype))
            dispatch = jax.nn.one_hot(prio_se, C, dtype=x.dtype)
            combine = dispatch * gate_se[..., None].astype(x.dtype)
            expert_in = jnp.einsum('gsec,gsd->egcd', dispatch, xg)
            h = jax.nn.relu(jnp.einsum('egcd,edf->egcf', expert_in, wi))
            expert_out = jnp.einsum('egcf,efd->egcd', h, wo)
            out = jnp.einsum('gsec,egcd->gsd', combine, expert_out)
            return out.reshape(B, T, D)
        key = jax.random.key(seed)
        k1, k2, k3, k4 = jax.random.split(key, 4)
        B, T, D, F = (8, 256, 192, 768)
        x = jax.random.normal(k1, (B, T, D), jnp.float32)
        w_router = jax.random.normal(k2, (D, NUM_EXPERTS), jnp.float32) * D ** (-0.5)
        wi = jax.random.normal(k3, (NUM_EXPERTS, D, F), jnp.float32) * D ** (-0.5)
        wo = jax.random.normal(k4, (NUM_EXPERTS, F, D), jnp.float32) * F ** (-0.5)
        return {'x': x, 'w_router': w_router, 'wi': wi, 'wo': wo}
    _L2_ffn_all = _L2_ffn_setup()
    _L2_ffn_in = {k: v for k, v in _L2_ffn_all.items() if k in ('w_router', 'wi', 'wo')}
    del _L2_ffn_all

    def _L3_attn_setup():
        import jax, jax.numpy as jnp
        import numpy as np
        import math
        D_MODEL = 192
        D_STATE = 16
        D_CONV = 4
        EXPAND = 2
        N_EXP = 8
        TOP_K = 2
        D_INNER = D_MODEL * EXPAND
        D_FF = 4 * D_MODEL
        B_SZ, T_LEN = (2, 256)
        EPS = 1e-06

        def _rms(x, g):
            return x * jax.lax.rsqrt(jnp.mean(x * x, axis=-1, keepdims=True) + EPS) * g
        key = jax.random.key(seed)
        ks = jax.random.split(key, 12)
        s = 0.02
        x = jax.random.normal(ks[0], (B_SZ, T_LEN, D_MODEL), jnp.float32)
        g_mamba = jnp.ones((D_MODEL,), jnp.float32)
        w_in = jax.random.normal(ks[1], (D_MODEL, 2 * D_INNER), jnp.float32) * s
        conv_w = jax.random.normal(ks[2], (D_INNER, D_CONV), jnp.float32) * s
        conv_b = jnp.zeros((D_INNER,), jnp.float32)
        w_xproj = jax.random.normal(ks[3], (D_INNER, 2 * D_STATE + 1), jnp.float32) * s
        w_dt = jax.random.normal(ks[4], (1, D_INNER), jnp.float32) * s
        b_dt = jnp.full((D_INNER,), math.log(0.001), jnp.float32)
        A_log = jnp.log(jnp.arange(1, D_STATE + 1, dtype=jnp.float32)) * jnp.ones((D_INNER, 1), jnp.float32)
        D_skip = jnp.ones((D_INNER,), jnp.float32)
        w_out = jax.random.normal(ks[5], (D_INNER, D_MODEL), jnp.float32) * s
        g_moe = jnp.ones((D_MODEL,), jnp.float32)
        w_router = jax.random.normal(ks[6], (D_MODEL, N_EXP), jnp.float32) * s
        g_exp = jnp.ones((N_EXP, D_MODEL), jnp.float32)
        w1 = jax.random.normal(ks[7], (N_EXP, D_MODEL, D_FF), jnp.float32) * s
        w3 = jax.random.normal(ks[8], (N_EXP, D_MODEL, D_FF), jnp.float32) * s
        w2 = jax.random.normal(ks[9], (N_EXP, D_FF, D_MODEL), jnp.float32) * s
        return dict(x=x, g_mamba=g_mamba, w_in=w_in, conv_w=conv_w, conv_b=conv_b, w_xproj=w_xproj, w_dt=w_dt, b_dt=b_dt, A_log=A_log, D_skip=D_skip, w_out=w_out, g_moe=g_moe, w_router=w_router, g_exp=g_exp, w1=w1, w3=w3, w2=w2)
    _L3_attn_all = _L3_attn_setup()
    _L3_attn_in = {k: v for k, v in _L3_attn_all.items() if k in ('g_mamba', 'w_in', 'conv_w', 'conv_b', 'w_xproj', 'w_dt', 'b_dt', 'A_log', 'D_skip', 'w_out', 'g_moe', 'w_router', 'g_exp', 'w1', 'w3', 'w2')}
    del _L3_attn_all

    def _L3_ffn_setup():
        import jax, jax.numpy as jnp
        import numpy as np
        D_MODEL = 192
        N_EXPERTS = 16
        FFN_HIDDEN = 768
        TOP_K = 4
        key = jax.random.key(seed)
        k0, k1, k2, k3, k4 = jax.random.split(key, 5)
        scale = 0.02
        hidden_states = jax.random.normal(k0, (2, 128, D_MODEL), dtype=jnp.float32)
        router_w = jax.random.normal(k1, (N_EXPERTS, D_MODEL), dtype=jnp.float32) * scale
        w1 = jax.random.normal(k2, (N_EXPERTS, FFN_HIDDEN, D_MODEL), dtype=jnp.float32) * scale
        v1 = jax.random.normal(k3, (N_EXPERTS, FFN_HIDDEN, D_MODEL), dtype=jnp.float32) * scale
        w2 = jax.random.normal(k4, (N_EXPERTS, D_MODEL, FFN_HIDDEN), dtype=jnp.float32) * scale
        return {'hidden_states': hidden_states, 'router_w': router_w, 'w1': w1, 'v1': v1, 'w2': w2}
    _L3_ffn_all = _L3_ffn_setup()
    _L3_ffn_in = {k: v for k, v in _L3_ffn_all.items() if k in ('router_w', 'w1', 'v1', 'w2')}
    del _L3_ffn_all
    return {'x': x, 'cls_tok': cls_tok, 'L0_tok_ln_weight': _L0_tok_in['ln_weight'], 'L0_tok_ln_bias': _L0_tok_in['ln_bias'], 'L0_tok_proj_weight': _L0_tok_in['proj_weight'], 'L0_tok_proj_bias': _L0_tok_in['proj_bias'], 'L0_attn_A_log': _L0_attn_in['A_log'], 'L0_attn_D_param': _L0_attn_in['D_param'], 'L0_attn_W_bc': _L0_attn_in['W_bc'], 'L0_attn_W_dt': _L0_attn_in['W_dt'], 'L0_attn_W_dtp': _L0_attn_in['W_dtp'], 'L0_attn_b_dt': _L0_attn_in['b_dt'], 'L0_attn_rms_scale': _L0_attn_in['rms_scale'], 'L0_ffn_enc_w': _L0_ffn_in['enc_w'], 'L0_ffn_enc_b': _L0_ffn_in['enc_b'], 'L0_ffn_sw_w': _L0_ffn_in['sw_w'], 'L0_ffn_sw_b': _L0_ffn_in['sw_b'], 'L0_ffn_w1': _L0_ffn_in['w1'], 'L0_ffn_b1': _L0_ffn_in['b1'], 'L0_ffn_w2': _L0_ffn_in['w2'], 'L0_ffn_b2': _L0_ffn_in['b2'], 'L1_attn_Wq': _L1_attn_in['Wq'], 'L1_attn_bq': _L1_attn_in['bq'], 'L1_attn_Wk': _L1_attn_in['Wk'], 'L1_attn_bk': _L1_attn_in['bk'], 'L1_attn_Wv': _L1_attn_in['Wv'], 'L1_attn_bv': _L1_attn_in['bv'], 'L1_ffn_ln1_g': _L1_ffn_in['ln1_g'], 'L1_ffn_ln1_b': _L1_ffn_in['ln1_b'], 'L1_ffn_qkv_w': _L1_ffn_in['qkv_w'], 'L1_ffn_proj_w': _L1_ffn_in['proj_w'], 'L1_ffn_proj_b': _L1_ffn_in['proj_b'], 'L1_ffn_ln2_g': _L1_ffn_in['ln2_g'], 'L1_ffn_ln2_b': _L1_ffn_in['ln2_b'], 'L1_ffn_gate_w': _L1_ffn_in['gate_w'], 'L1_ffn_gate_b': _L1_ffn_in['gate_b'], 'L1_ffn_w1': _L1_ffn_in['w1'], 'L1_ffn_b1': _L1_ffn_in['b1'], 'L1_ffn_w2': _L1_ffn_in['w2'], 'L1_ffn_b2': _L1_ffn_in['b2'], 'L2_attn_Wq': _L2_attn_in['Wq'], 'L2_attn_bq': _L2_attn_in['bq'], 'L2_attn_Wkv': _L2_attn_in['Wkv'], 'L2_attn_bkv': _L2_attn_in['bkv'], 'L2_attn_Wproj': _L2_attn_in['Wproj'], 'L2_attn_bproj': _L2_attn_in['bproj'], 'L2_attn_scale': _L2_attn_in['scale'], 'L2_ffn_w_router': _L2_ffn_in['w_router'], 'L2_ffn_wi': _L2_ffn_in['wi'], 'L2_ffn_wo': _L2_ffn_in['wo'], 'L3_attn_g_mamba': _L3_attn_in['g_mamba'], 'L3_attn_w_in': _L3_attn_in['w_in'], 'L3_attn_conv_w': _L3_attn_in['conv_w'], 'L3_attn_conv_b': _L3_attn_in['conv_b'], 'L3_attn_w_xproj': _L3_attn_in['w_xproj'], 'L3_attn_w_dt': _L3_attn_in['w_dt'], 'L3_attn_b_dt': _L3_attn_in['b_dt'], 'L3_attn_A_log': _L3_attn_in['A_log'], 'L3_attn_D_skip': _L3_attn_in['D_skip'], 'L3_attn_w_out': _L3_attn_in['w_out'], 'L3_attn_g_moe': _L3_attn_in['g_moe'], 'L3_attn_w_router': _L3_attn_in['w_router'], 'L3_attn_g_exp': _L3_attn_in['g_exp'], 'L3_attn_w1': _L3_attn_in['w1'], 'L3_attn_w3': _L3_attn_in['w3'], 'L3_attn_w2': _L3_attn_in['w2'], 'L3_ffn_router_w': _L3_ffn_in['router_w'], 'L3_ffn_w1': _L3_ffn_in['w1'], 'L3_ffn_v1': _L3_ffn_in['v1'], 'L3_ffn_w2': _L3_ffn_in['w2']}

def reference(x, cls_tok, L0_tok_ln_weight, L0_tok_ln_bias, L0_tok_proj_weight, L0_tok_proj_bias, L0_attn_A_log, L0_attn_D_param, L0_attn_W_bc, L0_attn_W_dt, L0_attn_W_dtp, L0_attn_b_dt, L0_attn_rms_scale, L0_ffn_enc_w, L0_ffn_enc_b, L0_ffn_sw_w, L0_ffn_sw_b, L0_ffn_w1, L0_ffn_b1, L0_ffn_w2, L0_ffn_b2, L1_attn_Wq, L1_attn_bq, L1_attn_Wk, L1_attn_bk, L1_attn_Wv, L1_attn_bv, L1_ffn_ln1_g, L1_ffn_ln1_b, L1_ffn_qkv_w, L1_ffn_proj_w, L1_ffn_proj_b, L1_ffn_ln2_g, L1_ffn_ln2_b, L1_ffn_gate_w, L1_ffn_gate_b, L1_ffn_w1, L1_ffn_b1, L1_ffn_w2, L1_ffn_b2, L2_attn_Wq, L2_attn_bq, L2_attn_Wkv, L2_attn_bkv, L2_attn_Wproj, L2_attn_bproj, L2_attn_scale, L2_ffn_w_router, L2_ffn_wi, L2_ffn_wo, L3_attn_g_mamba, L3_attn_w_in, L3_attn_conv_w, L3_attn_conv_b, L3_attn_w_xproj, L3_attn_w_dt, L3_attn_b_dt, L3_attn_A_log, L3_attn_D_skip, L3_attn_w_out, L3_attn_g_moe, L3_attn_w_router, L3_attn_g_exp, L3_attn_w1, L3_attn_w3, L3_attn_w2, L3_ffn_router_w, L3_ffn_w1, L3_ffn_v1, L3_ffn_w2):
    import jax
    import jax.numpy as jnp

    def _L0_tok_ref(x, ln_weight, ln_bias, proj_weight, proj_bias):
        import jax, jax.numpy as jnp
        import numpy as np
        PATCH = 16

        def _shift2d(x, shift):
            l, r, t, b = shift
            H, W = (x.shape[2], x.shape[3])
            xp = jnp.pad(x, ((0, 0), (0, 0), (max(t, 0), max(b, 0)), (max(l, 0), max(r, 0))))
            h0 = max(-t, 0)
            w0 = max(-l, 0)
            return xp[:, :, h0:h0 + H, w0:w0 + W]
        shifts = ((1, -1, 0, 0), (-1, 1, 0, 0), (0, 0, 1, -1), (0, 0, -1, 1))
        xc = jnp.concatenate([x] + [_shift2d(x, s) for s in shifts], axis=1)
        B, C5, H, W = xc.shape
        p = PATCH
        h, w = (H // p, W // p)
        t = xc.reshape(B, C5, h, p, w, p)
        t = t.transpose(0, 2, 4, 3, 5, 1).reshape(B, h * w, p * p * C5)
        mu = jnp.mean(t, axis=-1, keepdims=True)
        var = jnp.mean(jnp.square(t - mu), axis=-1, keepdims=True)
        tn = (t - mu) * jax.lax.rsqrt(var + 1e-05) * ln_weight + ln_bias
        return jnp.einsum('bnk,dk->bnd', tn, proj_weight) + proj_bias

    def _L0_attn_ref(x, A_log, D_param, W_bc, W_dt, W_dtp, b_dt, rms_scale):
        import jax, jax.numpy as jnp
        import numpy as np
        from jax import lax
        B_SZ, L, D, N, R = (1, 1024, 192, 16, 48)

        def _soft_clamp(x, lo=0.0001, hi=10.0):
            center = (hi + lo) / 2.0
            half_range = (hi - lo) / 2.0
            return center + half_range * jnp.tanh((x - center) / half_range)
        n = A_log.shape[1]
        A = -jnp.exp(A_log)
        bc = x @ W_bc
        B_sel, C_sel = (bc[..., :n], bc[..., n:])
        delta = jax.nn.softplus(x @ W_dt @ W_dtp + b_dt)
        delta = delta * lax.rsqrt(jnp.mean(delta * delta, axis=-1, keepdims=True) + 1e-06) * rms_scale
        delta = _soft_clamp(delta, 0.0001, 10.0)
        dE = delta[..., None]
        half = 0.5 * dE * A
        denom = 1.0 - half
        A_bar = (1.0 + half) / denom
        B_bar = jnp.sqrt(dE) * B_sel[:, :, None, :] / denom
        x_prev = jnp.concatenate([jnp.zeros_like(x[:, :1]), x[:, :-1]], axis=1)
        x_in = 0.5 * (x + x_prev)
        Bx = B_bar * x_in[..., None]

        def op(left, right):
            a_l, b_l = left
            a_r, b_r = right
            return (a_r * a_l, a_r * b_l + b_r)
        _, all_h = lax.associative_scan(op, (A_bar, Bx), axis=1)
        y = jnp.sum(C_sel[:, :, None, :] * all_h, axis=-1)
        return y + D_param * x

    def _L0_ffn_ref(x, enc_w, enc_b, sw_w, sw_b, w1, b1, w2, b2):
        import jax, jax.numpy as jnp
        import numpy as np
        H = 192
        R = 64
        E = 8
        B, S = (8, 512)
        b, s, d = x.shape
        xt = x.reshape(-1, d)
        x_enc = xt @ enc_w + enc_b
        route_prob = jax.nn.softmax(x_enc @ sw_w + sw_b, axis=-1)
        route_prob_max = jnp.max(route_prob, axis=-1)
        routes = jnp.argmax(route_prob, axis=-1)
        onehot = jax.nn.one_hot(routes, E, dtype=xt.dtype)
        h = jnp.einsum('td,edr->ter', xt, w1) + b1[None]
        h = jax.nn.gelu(h, approximate=False)
        h = h * onehot[..., None]
        out = jnp.einsum('ter,erd->td', h, w2) + onehot @ b2
        out = out * route_prob_max[:, None]
        return out.reshape(b, s, d)

    def _L1_attn_ref(Z, Wq, bq, Wk, bk, Wv, bv):
        import jax, jax.numpy as jnp
        import numpy as np
        D = Z.shape[-1]
        scale = 1.0 / D ** 0.5
        Q = jnp.einsum('bsd,ed->bse', Z, Wq) + bq
        K = jnp.einsum('bsd,ed->bse', Z, Wk) + bk
        V = jnp.einsum('bsd,ed->bse', Z, Wv) + bv
        scores = jnp.einsum('bqd,bkd->bqk', Q, K) * scale
        attn = jax.nn.softmax(scores, axis=-1)
        Z_hat = jnp.einsum('bqk,bkd->bqd', attn, V)
        return Z_hat

    def _L1_ffn_ref(x, ln1_g, ln1_b, qkv_w, proj_w, proj_b, ln2_g, ln2_b, gate_w, gate_b, w1, b1, w2, b2):
        import jax, jax.numpy as jnp
        import numpy as np
        B, N, DIM, HEADS = (4, 256, 192, 12)
        HIDDEN, E, TOPK = (768, 8, 2)
        EPS = 1e-05

        def _layernorm(x, g, b):
            mu = jnp.mean(x, axis=-1, keepdims=True)
            var = jnp.var(x, axis=-1, keepdims=True)
            return (x - mu) * jax.lax.rsqrt(var + EPS) * g + b
        b, n, d = x.shape
        hd = d // HEADS
        scale = hd ** (-0.5)
        h = _layernorm(x, ln1_g, ln1_b)
        qkv = h @ qkv_w.T
        qkv = qkv.reshape(b, n, 3, HEADS, hd).transpose(2, 0, 3, 1, 4)
        q, k, v = (qkv[0], qkv[1], qkv[2])
        attn = jax.nn.softmax(jnp.einsum('bhnd,bhmd->bhnm', q, k) * scale, axis=-1)
        a = jnp.einsum('bhnm,bhmd->bhnd', attn, v)
        a = a.transpose(0, 2, 1, 3).reshape(b, n, d)
        a = a @ proj_w.T + proj_b
        x = x + a
        h2 = _layernorm(x, ln2_g, ln2_b)
        t = h2.reshape(-1, d)
        T = t.shape[0]
        logits = t @ gate_w.T + gate_b
        top_val, top_idx = jax.lax.top_k(logits, TOPK)
        score = jax.nn.softmax(top_val, axis=-1)
        cw = jnp.zeros((T, E), t.dtype).at[jnp.arange(T)[:, None], top_idx].add(score)
        out = jnp.zeros_like(t)
        for e in range(E):
            he = jax.nn.gelu(t @ w1[e].T + b1[e], approximate=False)
            ye = he @ w2[e].T + b2[e]
            out = out + cw[:, e:e + 1] * ye
        return x + out.reshape(b, n, d)

    def _L2_attn_ref(x, Wq, bq, Wkv, bkv, Wproj, bproj, scale):
        import jax, jax.numpy as jnp
        import numpy as np
        B, N, C, H = (4, 512, 192, 12)
        D = C // H
        EPS = 1e-12

        def _l2norm(t):
            n = jnp.sqrt(jnp.sum(t * t, axis=-1, keepdims=True))
            return t / jnp.maximum(n, EPS)
        b, n, c = x.shape
        q = (x @ Wq + bq).reshape(b, n, H, D).transpose(0, 2, 1, 3)
        kv = (x @ Wkv + bkv).reshape(b, n, 2, H, D).transpose(2, 0, 3, 1, 4)
        k, v = (kv[0], kv[1])
        q = _l2norm(q)
        k = _l2norm(k)
        attn = jnp.einsum('bhqd,bhkd->bhqk', q, k) * scale
        attn = jax.nn.softmax(attn, axis=-1)
        out = jnp.einsum('bhqk,bhkd->bhqd', attn, v)
        out = out.transpose(0, 2, 1, 3).reshape(b, n, c)
        return out @ Wproj + bproj

    def _L2_ffn_ref(x, w_router, wi, wo):
        import jax, jax.numpy as jnp
        import numpy as np
        NUM_EXPERTS = 8
        TOP_K = 2
        CAPACITY_FACTOR = 1.25
        MAX_GROUP_SIZE = 1024
        MIN_EXPERT_CAPACITY = 4

        def _moe_forward(x, w_router, wi, wo):
            B, T, D = x.shape
            E = NUM_EXPERTS
            num_tokens = B * T
            G = max(num_tokens // MAX_GROUP_SIZE, E)
            while num_tokens % G != 0 or G % E != 0:
                G += 1
            S = num_tokens // G
            C = max(int(TOP_K * CAPACITY_FACTOR * S / E), MIN_EXPERT_CAPACITY)
            xg = x.reshape(G, S, D)
            logits = jnp.einsum('gsd,de->gse', xg.astype(jnp.float32), w_router.astype(jnp.float32))
            probs = jax.nn.softmax(logits, axis=-1)
            gate, idx = jax.lax.top_k(probs, TOP_K)
            idx_kf = jnp.swapaxes(idx, 1, 2).reshape(G, TOP_K * S)
            mask = jax.nn.one_hot(idx_kf, E, dtype=jnp.int32)
            prio = jnp.cumsum(mask, axis=1) * mask - 1
            prio = jnp.swapaxes(prio.reshape(G, TOP_K, S, E), 1, 2)
            prio_se = prio.max(axis=2)
            gate_se = jnp.einsum('gsk,gske->gse', gate, jax.nn.one_hot(idx, E, dtype=gate.dtype))
            dispatch = jax.nn.one_hot(prio_se, C, dtype=x.dtype)
            combine = dispatch * gate_se[..., None].astype(x.dtype)
            expert_in = jnp.einsum('gsec,gsd->egcd', dispatch, xg)
            h = jax.nn.relu(jnp.einsum('egcd,edf->egcf', expert_in, wi))
            expert_out = jnp.einsum('egcf,efd->egcd', h, wo)
            out = jnp.einsum('gsec,egcd->gsd', combine, expert_out)
            return out.reshape(B, T, D)
        return _moe_forward(x, w_router, wi, wo)

    def _L3_attn_ref(x, g_mamba, w_in, conv_w, conv_b, w_xproj, w_dt, b_dt, A_log, D_skip, w_out, g_moe, w_router, g_exp, w1, w3, w2):
        import jax, jax.numpy as jnp
        import numpy as np
        import math
        D_MODEL = 192
        D_STATE = 16
        D_CONV = 4
        EXPAND = 2
        N_EXP = 8
        TOP_K = 2
        D_INNER = D_MODEL * EXPAND
        D_FF = 4 * D_MODEL
        B_SZ, T_LEN = (2, 256)
        EPS = 1e-06

        def _rms(x, g):
            return x * jax.lax.rsqrt(jnp.mean(x * x, axis=-1, keepdims=True) + EPS) * g
        B, T, _ = x.shape
        residual = x
        h = _rms(x, g_mamba)
        xz = h @ w_in
        x_s, z = jnp.split(xz, 2, axis=-1)
        xpad = jnp.pad(x_s, ((0, 0), (D_CONV - 1, 0), (0, 0)))
        xc = conv_b + sum((xpad[:, k:k + T, :] * conv_w[:, k] for k in range(D_CONV)))
        xc = jax.nn.silu(xc)
        params = xc @ w_xproj
        B_coef = params[..., :D_STATE]
        C_coef = params[..., D_STATE:2 * D_STATE]
        log_dt = params[..., -1:]
        dt = jax.nn.softplus(log_dt @ w_dt + b_dt)
        A = -jnp.exp(A_log)
        dt_e = dt[..., None]
        A_bar = jnp.exp(dt_e * A)
        Bu = dt_e * B_coef[:, :, None, :] * xc[..., None]

        def step(hst, inp):
            Ab, bu, c = inp
            hst = Ab * hst + bu
            return (hst, jnp.einsum('bds,bs->bd', hst, c))
        h0 = jnp.zeros((B, D_INNER, D_STATE), x.dtype)
        _, ys = jax.lax.scan(step, h0, (jnp.swapaxes(A_bar, 0, 1), jnp.swapaxes(Bu, 0, 1), jnp.swapaxes(C_coef, 0, 1)))
        y = jnp.swapaxes(ys, 0, 1)
        y = y + xc * D_skip
        y = y * jax.nn.silu(z)
        x = residual + y @ w_out
        N = B * T
        x_flat = x.reshape(N, D_MODEL)
        h_flat = _rms(x_flat, g_moe)
        scores = h_flat @ w_router
        topk_vals, topk_idx = jax.lax.top_k(scores, TOP_K)
        weights = jax.nn.softmax(topk_vals, axis=-1)
        w_dense = jnp.sum(jax.nn.one_hot(topk_idx, N_EXP, dtype=x.dtype) * weights[..., None], axis=1)
        rms_x = x_flat * jax.lax.rsqrt(jnp.mean(x_flat * x_flat, axis=-1, keepdims=True) + EPS)
        he = rms_x[:, None, :] * g_exp
        a = jnp.einsum('ned,edf->nef', he, w1)
        b = jnp.einsum('ned,edf->nef', he, w3)
        ffn = jnp.einsum('nef,efd->ned', jax.nn.silu(a) * b, w2)
        tok_out = x_flat[:, None, :] + ffn
        out = jnp.einsum('ne,ned->nd', w_dense, tok_out)
        return out.reshape(B, T, D_MODEL)

    def _L3_ffn_ref(hidden_states, router_w, w1, v1, w2):
        import jax, jax.numpy as jnp
        import numpy as np
        D_MODEL = 192
        N_EXPERTS = 16
        FFN_HIDDEN = 768
        TOP_K = 4
        orig_shape = hidden_states.shape
        x = hidden_states.reshape(-1, orig_shape[-1])
        n_experts = router_w.shape[0]
        logits = x @ router_w.T
        probs = jax.nn.softmax(logits.astype(jnp.float32), axis=-1)
        topk_w, topk_idx = jax.lax.top_k(probs, TOP_K)
        topk_w = topk_w / jnp.sum(topk_w, axis=-1, keepdims=True)
        dense_w = jnp.sum(jax.nn.one_hot(topk_idx, n_experts, dtype=x.dtype) * topk_w[..., None].astype(x.dtype), axis=1)
        gate = jnp.einsum('td,eid->tei', x, w1)
        up = jnp.einsum('td,eid->tei', x, v1)
        act = jax.nn.silu(gate) * up
        out = jnp.einsum('tei,edi,te->td', act, w2, dense_w)
        return out.reshape(orig_shape)
    h = _L0_tok_ref(x, L0_tok_ln_weight, L0_tok_ln_bias, L0_tok_proj_weight, L0_tok_proj_bias)
    h = jnp.concatenate([jnp.broadcast_to(cls_tok, (h.shape[0], 1, h.shape[2])), h], axis=1)
    h = h + _L0_attn_ref(_layernorm(h, axis=-1), L0_attn_A_log, L0_attn_D_param, L0_attn_W_bc, L0_attn_W_dt, L0_attn_W_dtp, L0_attn_b_dt, L0_attn_rms_scale)
    h = h + _L0_ffn_ref(_layernorm(h, axis=-1), L0_ffn_enc_w, L0_ffn_enc_b, L0_ffn_sw_w, L0_ffn_sw_b, L0_ffn_w1, L0_ffn_b1, L0_ffn_w2, L0_ffn_b2)
    h = h + _L1_attn_ref(_layernorm(h, axis=-1), L1_attn_Wq, L1_attn_bq, L1_attn_Wk, L1_attn_bk, L1_attn_Wv, L1_attn_bv)
    h = h + _L1_ffn_ref(_layernorm(h, axis=-1), L1_ffn_ln1_g, L1_ffn_ln1_b, L1_ffn_qkv_w, L1_ffn_proj_w, L1_ffn_proj_b, L1_ffn_ln2_g, L1_ffn_ln2_b, L1_ffn_gate_w, L1_ffn_gate_b, L1_ffn_w1, L1_ffn_b1, L1_ffn_w2, L1_ffn_b2)
    h = h + _L2_attn_ref(_layernorm(h, axis=-1), L2_attn_Wq, L2_attn_bq, L2_attn_Wkv, L2_attn_bkv, L2_attn_Wproj, L2_attn_bproj, L2_attn_scale)
    h = h + _L2_ffn_ref(_layernorm(h, axis=-1), L2_ffn_w_router, L2_ffn_wi, L2_ffn_wo)
    h = h + _L3_attn_ref(_layernorm(h, axis=-1), L3_attn_g_mamba, L3_attn_w_in, L3_attn_conv_w, L3_attn_conv_b, L3_attn_w_xproj, L3_attn_w_dt, L3_attn_b_dt, L3_attn_A_log, L3_attn_D_skip, L3_attn_w_out, L3_attn_g_moe, L3_attn_w_router, L3_attn_g_exp, L3_attn_w1, L3_attn_w3, L3_attn_w2)
    h = h + _L3_ffn_ref(_layernorm(h, axis=-1), L3_ffn_router_w, L3_ffn_w1, L3_ffn_v1, L3_ffn_w2)
    return h

_drawn_inputs = setup_inputs


def setup_inputs(seed=0):
    import zlib

    import numpy as np

    out = dict(_drawn_inputs(seed))
    spreads = {'L0_tok_ln_weight': (1.0, 0.2),
     'L0_tok_ln_bias': (0.0, 0.1),
     'L0_tok_proj_bias': (0.0, 0.1),
     'L0_attn_D_param': (1.0, 0.2),
     'L0_attn_rms_scale': (1.0, 0.6),
     'L1_attn_bq': (0.0, 0.62),
     'L1_attn_bk': (0.0, 2.0),
     'L1_attn_bv': (0.0, 0.1),
     'L1_ffn_ln1_g': (1.0, 0.6),
     'L1_ffn_ln1_b': (0.0, 0.8),
     'L1_ffn_proj_b': (0.0, 0.1),
     'L1_ffn_ln2_g': (1.0, 0.6),
     'L1_ffn_ln2_b': (0.0, 0.8),
     'L1_ffn_gate_b': (0.0, 0.476),
     'L1_ffn_b1': (0.0, 0.8),
     'L1_ffn_b2': (0.0, 0.325),
     'L2_attn_bq': (0.0, 2.0),
     'L2_attn_bkv': (0.0, 0.8),
     'L2_attn_bproj': (0.0, 0.269),
     'L2_attn_scale': (0.25, 0.6),
     'L3_attn_g_mamba': (1.0, 0.6),
     'L3_attn_conv_b': (0.0, 0.8),
     'L3_attn_b_dt': (-6.907755374908447, 0.6),
     'L3_attn_D_skip': (1.0, 0.6),
     'L3_attn_g_moe': (1.0, 0.6),
     'L3_attn_g_exp': (1.0, 0.6)}
    factors = {'L0_ffn_enc_w': 2.878,
     'L0_ffn_enc_b': 8.0,
     'L0_ffn_sw_w': 2.876,
     'L0_ffn_sw_b': 4.782,
     'L0_ffn_w1': 3.01,
     'L0_ffn_b1': 8.0,
     'L0_ffn_w2': 2.85,
     'L0_ffn_b2': 7.034,
     'L1_ffn_qkv_w': 8.0,
     'L1_ffn_proj_w': 7.513,
     'L1_ffn_w1': 2.897,
     'L1_ffn_w2': 2.691,
     'L2_attn_Wq': 8.0,
     'L2_attn_Wkv': 8.0,
     'L2_attn_Wproj': 4.938,
     'L3_attn_w_in': 8.0,
     'L3_attn_conv_w': 8.0,
     'L3_attn_w_xproj': 8.0,
     'L3_attn_w_dt': 8.0,
     'L3_attn_A_log': 8.0,
     'L3_attn_w_out': 8.0,
     'L3_attn_w_router': 8.0,
     'L3_attn_w1': 8.0,
     'L3_attn_w3': 8.0,
     'L3_attn_w2': 8.0,
     'L3_ffn_router_w': 8.0,
     'L3_ffn_w1': 8.0,
     'L3_ffn_v1': 8.0,
     'L3_ffn_w2': 8.0}
    for name, (base, spread) in spreads.items():
        noise = np.random.default_rng([zlib.crc32(name.encode()), seed]).standard_normal(out[name].shape)
        drawn = base * np.exp(spread * noise) if base else spread * noise
        out[name] = jnp.asarray(drawn.astype(out[name].dtype))
    for name, factor in factors.items():
        out[name] = (out[name] * factor).astype(out[name].dtype)
    return out
```

```python
from contextlib import ExitStack, contextmanager

import numpy as np

import concourse.bass as bass
from concourse import mybir

F32 = mybir.dt.float32
ALU = mybir.AluOpType
ACT = mybir.ActivationFunctionType
AX = mybir.AxisListType

IMAGES, SEQ, DIM = 32, 50, 192
TOKENS = IMAGES * SEQ
TILE = 2 * SEQ
TILES = TOKENS // TILE
HALF = DIM // 2
CHUNK = 4 * TILE
CHUNKS = TOKENS // CHUNK
PATCH, CHANNELS, SHIFTS, GRID = 16, 3, 5, 7
PATCH_DIM = PATCH * PATCH * CHANNELS * SHIFTS
WINDOW = CHANNELS * (PATCH * PATCH + 4 * PATCH)
WROWS = 120
WCHUNKS = WINDOW // WROWS
HEADS, HEAD = 12, 16
HIDDEN = 768
MASKED = -1.0e30


class Steps:

    def __init__(self, engine, sem):
        self.engine, self.sem, self.done, self.offset = engine, sem, 0, None

    def __call__(self, instruction):
        instruction.then_inc(self.sem, 1)
        self.done += 1
        self.engine.wait_ge(self.sem, self.done if self.offset is None else self.offset + self.done)

    def enter(self, index, per):
        self.per, self.start, self.offset = per, self.done, index * per
        return self

    def leave(self, count):
        assert self.done - self.start == self.per, (self.done - self.start, self.per)
        self.done, self.offset = self.start + count * self.per, None


class Tower:

    def __init__(self, nc, stack, args):
        self.nc, self.stack, self.args, self.sems, self.tensors = nc, stack, args, 0, 0
        sb = self.sbuf
        self.h = sb("h", [TILE, TILES, DIM])
        self.x = sb("x", [TILE, TILES, DIM])
        self.xT = sb("xT", [HALF + 1, 2, TOKENS])
        self.bank = [stack.enter_context(nc.psum_tensor(f"bank{i}", [128, 512], F32)) for i in range(8)]
        self.old, self.theirs, self.new, self.mine = ExitStack(), [], ExitStack(), []
        self.loaded = self.sem("constants_loaded", lasting=True)
        self.loads = []
        self.passed = self.sem("passed", lasting=True)
        self.w = {}
        for name, ap in args.items():
            if name.startswith("c_"):
                self.w[name[2:]] = t = sb(name, list(ap.shape))
                self.loads.append((t, ap))

    def sbuf(self, name, shape, stack=None):
        self.tensors += 1
        return (stack or self.stack).enter_context(self.nc.sbuf_tensor(f"{name}_{self.tensors}", shape, F32))

    def sem(self, name, lasting=False):
        self.sems += 1
        stack = self.stack if lasting else self.new
        sem = stack.enter_context(self.nc.semaphore(f"{name}_{self.sems}"))
        if not lasting:
            self.mine.append(sem)
        return sem

    @contextmanager
    def block(self):
        with self.nc.Block() as block:
            if self.theirs:
                @block.sync
                def _(sp):
                    for sem in self.theirs:
                        sp.sem_clear(sem)
            yield block
        self.old.close()
        self.old, self.theirs = self.new, self.mine
        self.new, self.mine = ExitStack(), []


def flat(ap):
    return ap.rearrange("p a b -> p (a b)")


def embed(t):
    nc = t.nc
    with ExitStack() as st:
        pixels = t.sbuf("pixels", [WROWS, 2, WCHUNKS, TILE], st)
        squares = t.sbuf("squares", [WROWS, 2, WCHUNKS, TILE], st)
        wshift = t.sbuf("wshift", [WROWS, WCHUNKS, SHIFTS, DIM], st)
        wsum = t.sbuf("wsum", [WROWS, WCHUNKS, DIM + 1], st)
        gain = t.sbuf("gain", [WROWS, 2, WCHUNKS, SHIFTS], st)
        share = t.sbuf("share", [WROWS, WCHUNKS], st)
        lift = t.sbuf("lift", [WROWS, 2, TILE], st)
        onesr = t.sbuf("onesr", [WROWS, TILE], st)
        zero = t.sbuf("zero", [1, DIM], st)
        pbias = t.sbuf("pbias", [1, DIM], st)
        rows = t.sbuf("rows", [TILE, 2, DIM], st)
        stats = t.sbuf("pstats", [TILE, TILES, 2], st)
        var = t.sbuf("pvar", [TILE, 4, TILES], st)
        weights_in, pixels_in, cls_in = t.sem("weights_in"), [t.sem("pixels_even"), t.sem("pixels_odd")], t.sem("cls_in")
        wsum_done, squared, multiplied, stored = t.sem("wsum_done"), t.sem("squared"), t.sem("multiplied"), t.sem("stored")
        bias_done, rows_done, lifted, lift_used = t.sem("bias_done"), t.sem("rows_done"), t.sem("lifted"), t.sem("lift_used")
        step, var_done, root_done, h_done = t.sem("step"), t.sem("var_done"), t.sem("root_done"), t.sem("h_done")
        raw, fixed = t.bank[0:2], t.bank[2:4]
        args = t.args

        with t.block() as block:
            @block.sync
            def _(sp):
                sp.dma_start(gain[:], args["ln_gain"]).then_inc(weights_in, 16)
                sp.dma_start(wshift[:], args["w_patch"]).then_inc(weights_in, 16)
                sp.dma_start(share[:], args["share"]).then_inc(weights_in, 16)
                sp.dma_start(pbias[:], args["patch_bias"]).then_inc(weights_in, 16)
                for u in range(2):
                    sp.dma_start(pixels[:, u], args["pixels"][u]).then_inc(pixels_in[u], 16)
                with sp.Fori(0, TILES // 2 - 1) as i:
                    for u in range(2):
                        sp.wait_ge(multiplied, 2 * i + u + 1)
                        sp.dma_start(pixels[:, u], args["pixels"][bass.ds(2 * i + u + 2, 1)]
                                     .rearrange("a p c n -> p (a c) n")).then_inc(pixels_in[u], 16)
                for dst, src in t.loads:
                    sp.dma_start(dst[:], src).then_inc(t.loaded, 16)
                sp.wait_ge(h_done, TILES)
                for image in range(2):
                    sp.dma_start(t.h[SEQ * image:SEQ * image + 1, :, :],
                                 args["cls"].to_broadcast([1, TILES, DIM])).then_inc(cls_in, 16)
                sp.wait_ge(cls_in, 32)
                sp.wait_ge(t.loaded, 16 * len(t.loads))

            @block.vector
            def _(dve):
                one = Steps(dve, step)
                one(nc.vector.memset(zero[:], 0.0))
                nc.vector.memset(onesr[:], 1.0).then_inc(wsum_done, 1)
                one(nc.vector.memset(t.xT[HALF:HALF + 1, :, :], 1.0))
                dve.wait_ge(weights_in, 64)
                for c in range(WCHUNKS):
                    for s in range(SHIFTS):
                        if s == 0:
                            one(nc.vector.tensor_scalar(wsum[:, c, 0:DIM], wshift[:, c, s, :],
                                                        gain[:, 0, c, s:s + 1], None, ALU.mult))
                        else:
                            one(nc.vector.scalar_tensor_tensor(
                                wsum[:, c, 0:DIM], wshift[:, c, s, :], gain[:, 0, c, s:s + 1],
                                wsum[:, c, 0:DIM], ALU.mult, ALU.add))
                nc.vector.tensor_copy(wsum[:, :, DIM:DIM + 1], share[:].unsqueeze(2)).then_inc(wsum_done, 1)
                with dve.Fori(0, WCHUNKS * SHIFTS // 4) as i:
                    for u in range(4):
                        dve.wait_ge(lift_used, 4 * i + u + 1)
                        nc.vector.tensor_scalar(
                            lift[:, u % 2, :], onesr[:],
                            gain[:, 1, :, :].rearrange("p c s -> p (c s)")[:, bass.ds(4 * i + u, 1)],
                            None, ALU.mult).then_inc(lifted, 1)
                dve.wait_ge(bias_done, 1)
                nc.vector.tensor_copy(rows[:, 0, :], fixed[0][0:TILE, 0:DIM])
                one(nc.vector.tensor_copy(rows[:, 1, :], fixed[1][0:TILE, 0:DIM]))
                with dve.Fori(0, TILES // 2) as i:
                    for u in range(2):
                        dve.wait_ge(multiplied, 2 * i + u + 1)
                        nc.vector.tensor_copy(t.h[:, bass.ds(2 * i + u, 1), :],
                                              raw[u][0:TILE, 0:DIM].unsqueeze(1))
                        nc.vector.tensor_copy(stats[:, bass.ds(2 * i + u, 1), :],
                                              raw[u][0:TILE, DIM:DIM + 2].unsqueeze(1)).then_inc(stored, 1)
                dve.wait_ge(stored, TILES + 2)
                mean, second = stats[:, :, 0], stats[:, :, 1]
                one(nc.vector.tensor_tensor(var[:, 0, :], mean, mean, ALU.mult))
                one(nc.vector.tensor_tensor(var[:, 1, :], second, var[:, 0, :], ALU.subtract))
                nc.vector.tensor_scalar(var[:, 2, :], var[:, 1, :], 0.0, 1e-5, ALU.max, ALU.add).then_inc(var_done, 1)
                dve.wait_ge(root_done, 1)
                one(nc.vector.reciprocal(var[:, 1, :], var[:, 3, :]))
                one(nc.vector.tensor_scalar(var[:, 0, :], mean, -1.0, None, ALU.mult))
                with dve.Fori(0, TILES // 2) as i:
                    one.enter(i, 2)
                    for u in range(2):
                        tile = t.h[:, bass.ds(2 * i + u, 1), :]
                        one(nc.vector.scalar_tensor_tensor(tile, rows[:, 0:1, :], var[:, 0, bass.ds(2 * i + u, 1)],
                                                           tile, ALU.mult, ALU.add))
                        nc.vector.scalar_tensor_tensor(tile, tile, var[:, 1, bass.ds(2 * i + u, 1)],
                                                       rows[:, 1:2, :], ALU.mult, ALU.add).then_inc(h_done, 1)
                one.leave(TILES // 2)

            @block.scalar
            def _(act):
                with act.Fori(0, TILES // 2) as i:
                    for u in range(2):
                        act.wait_ge(pixels_in[u], 16 * i + 16)
                        nc.scalar.activation(squares[:, u], pixels[:, u], ACT.Square).then_inc(squared, 1)
                act.wait_ge(var_done, 1)
                nc.scalar.activation(var[:, 3, :], var[:, 2, :], ACT.Sqrt).then_inc(root_done, 1)

            @block.tensor
            def _(pe):
                pe.sem_inc(stored, 2)
                pe.sem_inc(lift_used, 2)
                pe.wait_ge(wsum_done, 2)
                for c in range(WCHUNKS):
                    nc.tensor.matmul(fixed[0][0:TILE, 0:DIM], onesr[:], wsum[:, c, 0:DIM],
                                     start=(c == 0), stop=(c == WCHUNKS - 1))
                nc.tensor.matmul(fixed[1][0:TILE, 0:DIM], onesr[0:1, :], pbias[:], start=True, stop=False)
                flat_w = wshift[:].rearrange("p c s d -> p (c s) d")
                with pe.Fori(0, WCHUNKS * SHIFTS // 4) as i:
                    for u in range(4):
                        pe.wait_ge(lifted, 4 * i + u + 1)
                        nc.tensor.matmul(fixed[1][0:TILE, 0:DIM], lift[:, u % 2, :],
                                         flat_w[:, bass.ds(4 * i + u, 1), :], start=False, stop=False).then_inc(lift_used, 1)
                nc.tensor.matmul(fixed[1][0:TILE, 0:DIM], onesr[0:1, :], zero[:], start=False, stop=True).then_inc(bias_done, 1)
                with pe.Fori(0, TILES // 2) as i:
                    for u in range(2):
                        pe.wait_ge(squared, 2 * i + u + 1)
                        pe.wait_ge(stored, 2 * i + u + 1)
                        for c in range(WCHUNKS):
                            nc.tensor.matmul(raw[u][0:TILE, 0:DIM + 1], pixels[:, u, c, :], wsum[:, c, :],
                                             start=(c == 0), stop=(c == WCHUNKS - 1))
                        for c in range(WCHUNKS):
                            last = nc.tensor.matmul(raw[u][0:TILE, DIM + 1:DIM + 2], squares[:, u, c, :],
                                                    share[:, c:c + 1], start=(c == 0), stop=(c == WCHUNKS - 1))
                        last.then_inc(multiplied, 1)


def normalise(t, src, eps, *, keep=None, centred=True, gain=None, bias=None, feature_major=True):
    nc = t.nc
    with ExitStack() as st:
        bn = t.sbuf("bn", [TILE, TILES, 6], st)
        mv = t.sbuf("mv", [TILE, TILES, 2], st)
        sd = t.sbuf("sd", [TILE, 4, TILES], st)
        xs = t.sbuf("xs", [TILE, 2, DIM], st)
        bn_done, mv_done, step = t.sem("bn_done"), t.sem("mv_done"), t.sem("step")
        var_done, root_done = t.sem("var_done"), t.sem("root_done")
        scaled, turned, kept, copied = t.sem("scaled"), t.sem("turned"), t.sem("kept"), t.sem("copied")
        ident = t.w["ident"]

        with t.block() as block:
            @block.vector
            def _(dve):
                one = Steps(dve, step)
                with dve.Fori(0, TILES // 4) as i:
                    for u in range(4):
                        nc.vector.bn_stats(bn[:, bass.ds(4 * i + u, 1), :],
                                           src[:, bass.ds(4 * i + u, 1), :]).then_inc(bn_done, 1)
                dve.wait_ge(bn_done, TILES)
                for i in range(TILES):
                    nc.vector.bn_aggr(mv[:, i, :], bn[:, i, :]).then_inc(mv_done, 1)
                dve.wait_ge(mv_done, TILES)
                mean, var = mv[:, :, 0], mv[:, :, 1]
                if not centred:
                    one(nc.vector.tensor_tensor(sd[:, 2, :], mean, mean, ALU.mult))
                    one(nc.vector.tensor_tensor(sd[:, 3, :], sd[:, 2, :], var, ALU.add))
                    var = sd[:, 3, :]
                nc.vector.tensor_scalar(sd[:, 0, :], var, eps, None, ALU.add).then_inc(var_done, 1)
                dve.wait_ge(root_done, 1)
                one(nc.vector.reciprocal(sd[:, 2, :], sd[:, 1, :]))
                with dve.Fori(0, TILES // 2) as i:
                    for u in range(2):
                        if feature_major:
                            dve.wait_ge(turned, 2 * i + u + 1)
                        if keep is not None:
                            dve.wait_ge(kept, 2 * i + u + 1)
                        at = bass.ds(2 * i + u, 1)
                        if centred:
                            nc.vector.tensor_scalar(xs[:, u:u + 1, :], src[:, at, :], mv[:, at, 0:1], sd[:, 2, at],
                                                    ALU.subtract, ALU.mult).then_inc(scaled, 1)
                        else:
                            nc.vector.tensor_scalar(xs[:, u:u + 1, :], src[:, at, :], sd[:, 2, at], None,
                                                    ALU.mult).then_inc(scaled, 1)

            @block.gpsimd
            def _(pool):
                if keep is not None:
                    pool.sem_inc(kept, 2)
                    with pool.Fori(0, TILES // 2) as i:
                        for u in range(2):
                            pool.wait_ge(scaled, 2 * i + u + 1)
                            pool.sem_inc(t.passed, 1)
                            nc.gpsimd.tensor_copy(keep[:, bass.ds(2 * i + u, 1), :], xs[:, u:u + 1, :]).then_inc(kept, 1)

            @block.scalar
            def _(act):
                act.wait_ge(var_done, 1)
                nc.scalar.activation(sd[:, 1, :], sd[:, 0, :], ACT.Sqrt).then_inc(root_done, 1)
                if feature_major:
                    act.sem_inc(copied, 2)
                    with act.Fori(0, TILES // 2) as i:
                        for u in range(2):
                            act.wait_ge(turned, 2 * i + u + 3)
                            at = bass.ds(TILE * (2 * i + u), TILE)
                            from_psum = t.bank[u][0:HALF, 0:2 * TILE].rearrange("p (k n) -> p k n", k=2)
                            if gain is None:
                                act.sem_inc(t.passed, 1)
                                nc.scalar.activation(t.xT[0:HALF, :, at], from_psum, ACT.Identity).then_inc(copied, 1)
                            else:
                                for k in range(2):
                                    act.sem_inc(t.passed, 1)
                                    last = nc.scalar.activation(
                                        t.xT[0:HALF, k:k + 1, at], from_psum[:, k:k + 1, :], ACT.Identity,
                                        scale=gain[0:HALF, k:k + 1], bias=bias[0:HALF, k:k + 1] if bias is not None else 0.0)
                                last.then_inc(copied, 1)

            @block.tensor
            def _(pe):
                if feature_major:
                    pe.sem_inc(turned, 2)
                    with pe.Fori(0, TILES // 2) as i:
                        for u in range(2):
                            pe.wait_ge(scaled, 2 * i + u + 1)
                            pe.wait_ge(copied, 2 * i + u + 1)
                            for k in range(2):
                                last = nc.tensor.transpose(t.bank[u][0:HALF, TILE * k:TILE * (k + 1)],
                                                           xs[:, u, HALF * k:HALF * (k + 1)], ident[0:TILE, 0:TILE])
                            last.then_inc(turned, 1)


def store(t, out, src):
    nc = t.nc
    stored = t.sem("out_stored")
    with t.block() as block:
        @block.sync
        def _(sp):
            sp.dma_start(out.rearrange("(t p) d -> p t d", p=TILE), src[:]).then_inc(stored, 16)
            sp.wait_ge(stored, 16)

def softplus(t, z):
    nc = t.nc
    parts, groups = z.shape[0], z.shape[1]
    with ExitStack() as st:
        e, w, l, d = (t.sbuf(n, [parts, groups, CHUNK], st) for n in ("sp_e", "sp_w", "sp_ln", "sp_d"))
        abs_done, exp_done, w_done, ln_done = t.sem("abs_done"), t.sem("exp_done"), t.sem("w_done"), t.sem("ln_done")
        step, out_done = t.sem("step"), t.sem("out_done")
        with t.block() as block:
            @block.scalar
            def _(act):
                nc.scalar.preload_act_table_set("natural_log_exp_and_others")
                with act.Fori(0, CHUNKS) as c:
                    act.wait_ge(out_done, c + 1)
                    act.sem_inc(t.passed, 1)
                    nc.scalar.activation(d[:], z[:, :, bass.ds(CHUNK * c, CHUNK)], ACT.Abs).then_inc(abs_done, 1)
                    act.wait_ge(abs_done, c + 1)
                    nc.scalar.activation(e[:], d[:], ACT.Exp, scale=-1.0).then_inc(exp_done, 1)
                    act.wait_ge(w_done, c + 1)
                    nc.scalar.activation(l[:], w[:], ACT.Ln).then_inc(ln_done, 1)

            @block.vector
            def _(dve):
                one = Steps(dve, step)
                dve.sem_inc(out_done, 1)
                with dve.Fori(0, CHUNKS) as c:
                    one.enter(c, 4)
                    zc = z[:, :, bass.ds(CHUNK * c, CHUNK)]
                    dve.wait_ge(exp_done, c + 1)
                    nc.vector.tensor_scalar(w[:], e[:], 1.0, 1.0 + 2.0 ** -23, ALU.add, ALU.max).then_inc(w_done, 1)
                    dve.wait_ge(w_done, c + 1)
                    one(nc.vector.tensor_scalar(d[:], w[:], -1.0, None, ALU.add))
                    one(nc.vector.reciprocal(d[:], d[:]))
                    one(nc.vector.tensor_tensor(d[:], d[:], e[:], ALU.mult))
                    dve.wait_ge(ln_done, c + 1)
                    one(nc.vector.tensor_tensor(d[:], d[:], l[:], ALU.mult))
                    nc.vector.scalar_tensor_tensor(zc, zc, 0.0, d[:], ALU.max, ALU.add).then_inc(out_done, 1)
                one.leave(CHUNKS)


SLOTS = 4
STATES = 16


def scan(t, u, rate, coef, bc, direct, gain, y, bilinear):
    nc = t.nc
    parts, groups = u.shape[0], u.shape[1]
    jobs = STATES * groups
    with ExitStack() as st:
        a = t.sbuf("a", [parts, SLOTS, CHUNK // SEQ, SEQ], st)
        w2, s, g_ = (t.sbuf(n, [parts, SLOTS, CHUNK], st) for n in ("w2", "s", "g"))
        if bilinear:
            den, r, w1 = (t.sbuf(n, [parts, SLOTS, CHUNK], st) for n in ("den", "r", "w1"))
        den_done, r_done, a_done, w1_done = t.sem("den_done"), t.sem("r_done"), t.sem("a_done"), t.sem("w1_done")
        w2_done, s_done, g_done, summed = t.sem("w2_done"), t.sem("s_done"), t.sem("g_done"), t.sem("summed")
        spread, y_done, a_zero = t.sem("spread"), t.sem("y_done"), t.sem("a_zero")
        bankB, bankC, acc = t.bank[0:2], t.bank[2:4], t.bank[4:4 + groups]
        ident = t.w["ident"]

        with t.block() as block:
            @block.tensor
            def _(pe):
                pe.sem_inc(summed, SLOTS)
                with pe.Fori(0, CHUNKS) as c:
                    at = bass.ds(CHUNK * c, CHUNK)

                    def sum_states(j):
                        n, g = divmod(j, groups)
                        if j == 0:
                            pe.wait_ge(y_done, c + 1)
                        pe.wait_ge(g_done, c * jobs + j + 1 + SLOTS)
                        nc.tensor.matmul(acc[g][0:parts, 0:CHUNK], ident[0:parts, 0:parts], g_[:, j % SLOTS, :],
                                         start=(n == 0), stop=(n == STATES - 1)).then_inc(summed, 1)

                    for n in range(STATES):
                        pe.wait_ge(g_done, c * jobs + (n - 1) * groups + SLOTS)
                        pe.sem_inc(t.passed, 1)
                        for bank, row in ((bankB[n % 2], n), (bankC[n % 2], STATES + n)):
                            last = nc.tensor.matmul(bank[0:parts, 0:CHUNK],
                                                    ident[0:2 * STATES, row:row + 1].to_broadcast([2 * STATES, parts]),
                                                    bc[0:2 * STATES, at], start=True, stop=True)
                        last.then_inc(spread, 1)
                        if n:
                            for g in range(groups):
                                sum_states((n - 1) * groups + g)
                    for g in range(groups):
                        sum_states((STATES - 1) * groups + g)

            @block.scalar
            def _(act):
                act.wait_ge(a_zero, 1)
                act.sem_inc(a_done, SLOTS)
                nc.scalar.preload_act_table(ACT.Exp)
                with act.Fori(0, CHUNKS) as c:
                    at = bass.ds(CHUNK * c, CHUNK)

                    def decay(j):
                        n, g = divmod(j, groups)
                        act.wait_ge(s_done, c * jobs + j + 1)
                        rest = a[:, j % SLOTS, :, 1:SEQ]
                        if bilinear:
                            act.wait_ge(r_done, c * jobs + j + 1 + SLOTS)
                            nc.scalar.activation(rest, r[:, j % SLOTS, :].rearrange("p (b t) -> p b t", t=SEQ)[:, :, 1:SEQ],
                                                 ACT.Identity, scale=2.0, bias=t.w["minus_one"][0:parts, :]).then_inc(a_done, 1)
                        else:
                            act.sem_inc(t.passed, 1)
                            nc.scalar.activation(rest, rate[:, g, at].rearrange("p (b t) -> p b t", t=SEQ)[:, :, 1:SEQ],
                                                 ACT.Exp, scale=coef[:, g, n:n + 1]).then_inc(a_done, 1)

                    for j in range(jobs + 2):
                        if j < jobs and bilinear:
                            n, g = divmod(j, groups)
                            act.wait_ge(r_done, c * jobs + j + 1)
                            act.sem_inc(t.passed, 1)
                            nc.scalar.activation(den[:, j % SLOTS, :], rate[:, g, at], ACT.Identity,
                                                 scale=coef[:, g, n:n + 1], bias=1.0).then_inc(den_done, 1)
                        if j >= 2:
                            decay(j - 2)

            @block.gpsimd
            def _(pool):
                if bilinear:
                    pool.sem_inc(w1_done, SLOTS)
                    with pool.Fori(0, CHUNKS) as c:
                        at = bass.ds(CHUNK * c, CHUNK)
                        for j in range(jobs):
                            pool.wait_ge(r_done, c * jobs + j + 1 + SLOTS)
                            pool.wait_ge(w2_done, c * jobs + j + 1)
                            pool.sem_inc(t.passed, 1)
                            nc.gpsimd.tensor_tensor(w1[:, j % SLOTS, :], u[:, j % groups, at], r[:, j % SLOTS, :],
                                                    ALU.mult).then_inc(w1_done, 1)

            @block.vector
            def _(dve):
                nc.vector.memset(a[:], 0.0).then_inc(a_zero, 1)
                for sem in (r_done, w2_done, s_done, g_done):
                    dve.sem_inc(sem, SLOTS)
                dve.sem_inc(y_done, 1)
                with dve.Fori(0, CHUNKS) as c:
                    at = bass.ds(CHUNK * c, CHUNK)

                    def invert(j):
                        dve.wait_ge(den_done, c * jobs + j + 1)
                        dve.wait_ge(a_done, c * jobs + j + 1)
                        dve.wait_ge(w1_done, c * jobs + j + 1)
                        nc.vector.reciprocal(r[:, j % SLOTS, :], den[:, j % SLOTS, :]).then_inc(r_done, 1)

                    def weigh(j):
                        dve.wait_ge(summed, c * jobs + j + 1)
                        if bilinear:
                            dve.wait_ge(w1_done, c * jobs + j + 1 + SLOTS)
                        n, g = divmod(j, groups)
                        dve.wait_ge(spread, c * STATES + n + 1)
                        src = w1[:, j % SLOTS, :] if bilinear else u[:, g, at]
                        nc.vector.tensor_tensor(w2[:, j % SLOTS, :], src, bankB[n % 2][0:parts, 0:CHUNK],
                                                ALU.mult).then_inc(w2_done, 1)

                    def recur(j):
                        dve.wait_ge(w2_done, c * jobs + j + 1 + SLOTS)
                        dve.wait_ge(a_done, c * jobs + j + 1 + SLOTS)
                        nc.vector.tensor_tensor_scan(s[:, j % SLOTS, :], a[:, j % SLOTS, :, :].rearrange("p b t -> p (b t)"),
                                                     w2[:, j % SLOTS, :], 0.0, ALU.mult, ALU.add).then_inc(s_done, 1)

                    def read(j):
                        dve.wait_ge(s_done, c * jobs + j + 1 + SLOTS)
                        nc.vector.tensor_tensor(g_[:, j % SLOTS, :], s[:, j % SLOTS, :],
                                                bankC[(j // groups) % 2][0:parts, 0:CHUNK], ALU.mult).then_inc(g_done, 1)

                    if bilinear:
                        invert(0)
                        invert(1)
                    for j in range(jobs):
                        if bilinear and j + 2 < jobs:
                            invert(j + 2)
                        weigh(j)
                        if j:
                            read(j - 1)
                        recur(j)
                    read(jobs - 1)
                    dve.wait_ge(summed, c * jobs + jobs + SLOTS)
                    for g in range(groups):
                        last = nc.vector.scalar_tensor_tensor(y[:, g, at], direct[0:parts, g, at], gain[0:parts, g:g + 1],
                                                              acc[g][0:parts, 0:CHUNK], ALU.mult, ALU.add)
                    last.then_inc(y_done, 1)


def add_back(t, y, dst, weights=None):
    nc = t.nc
    parts, groups = y.shape[0], y.shape[1]
    with ExitStack() as st:
        ys = t.sbuf("ys", [parts, 2, groups, TILE], st)
        staged, turned, added = t.sem("staged"), t.sem("turned"), t.sem("added")
        with t.block() as block:
            @block.scalar
            def _(act):
                with act.Fori(0, TILES // 2) as i:
                    for v in range(2):
                        act.wait_ge(turned, 2 * i + v + 1)
                        act.sem_inc(t.passed, 1)
                        nc.scalar.activation(ys[:, v], y[:, :, bass.ds(TILE * (2 * i + v), TILE)],
                                             ACT.Identity).then_inc(staged, 1)

            @block.tensor
            def _(pe):
                pe.sem_inc(turned, 2)
                with pe.Fori(0, TILES // 2) as i:
                    for v in range(2):
                        pe.wait_ge(staged, 2 * i + v + 1)
                        pe.wait_ge(added, 2 * i + v + 1)
                        for g in range(groups):
                            if weights is None:
                                last = nc.tensor.transpose(t.bank[v][0:TILE, parts * g:parts * (g + 1)], ys[:, v, g, :],
                                                           t.w["ident"][0:parts, 0:parts])
                            else:
                                last = nc.tensor.matmul(t.bank[v][0:TILE, 0:DIM], ys[:, v, g, :], weights(g, i),
                                                        start=(g == 0), stop=(g == groups - 1))
                        last.then_inc(turned, 1)

            @block.vector
            def _(dve):
                dve.sem_inc(added, 2)
                with dve.Fori(0, TILES // 2) as i:
                    for v in range(2):
                        dve.wait_ge(turned, 2 * i + v + 3)
                        tile = dst[:, bass.ds(2 * i + v, 1), :]
                        nc.vector.tensor_tensor(tile, tile, t.bank[v][0:TILE, 0:DIM].unsqueeze(1), ALU.add).then_inc(added, 1)


CLAMP_LO, CLAMP_HI = 0.0001, 10.0
CENTRE, REACH = (CLAMP_HI + CLAMP_LO) / 2.0, (CLAMP_HI - CLAMP_LO) / 2.0
RANK = 48


def layer0_mixer(t):
    nc, w = t.nc, t.w
    normalise(t, t.h, 1e-5)
    with ExitStack() as st:
        bc = t.sbuf("bc", [2 * STATES, TOKENS], st)
        rate = t.sbuf("rate", [HALF, 2, TOKENS], st)
        u = t.sbuf("u", [HALF, 2, TOKENS], st)
        coef = t.sbuf("coef", [HALF, 2, STATES], st)
        low = t.sbuf("low", [RANK, TOKENS], st)
        mult, low_done, up, biased, coef_done = t.sem("mult"), t.sem("low_done"), t.sem("up"), t.sem("biased"), t.sem("coef_done")
        with t.block() as block:
            @block.tensor
            def _(pe):
                pe.sem_inc(low_done, 1)
                pe.sem_inc(biased, 1)
                with pe.Fori(0, CHUNKS) as c:
                    at = bass.ds(CHUNK * c, CHUNK)
                    pe.wait_ge(low_done, 2 * c + 1)
                    for k in range(2):
                        nc.tensor.matmul(t.bank[0][0:2 * STATES, 0:CHUNK], w["L0_W_bc"][:, k, :], t.xT[0:HALF, k, at],
                                         start=(k == 0), stop=(k == 1))
                    for k in range(2):
                        last = nc.tensor.matmul(t.bank[1][0:RANK, 0:CHUNK], w["L0_W_dt"][:, k, :], t.xT[0:HALF, k, at],
                                                start=(k == 0), stop=(k == 1))
                    last.then_inc(mult, 1)
                    pe.wait_ge(low_done, 2 * c + 3)
                    pe.wait_ge(biased, 2 * c + 1)
                    for k in range(2):
                        last = nc.tensor.matmul(t.bank[2 + k][0:HALF, 0:CHUNK], w["L0_W_dtp"][:, HALF * k:HALF * (k + 1)],
                                                low[:, at], start=True, stop=True)
                    last.then_inc(up, 1)

            @block.scalar
            def _(act):
                act.sem_inc(t.passed, 1)
                nc.scalar.activation(coef[:], w["L0_A_log"][:], ACT.Exp).then_inc(coef_done, 1)
                with act.Fori(0, CHUNKS) as c:
                    at = bass.ds(CHUNK * c, CHUNK)
                    act.wait_ge(mult, c + 1)
                    act.sem_inc(t.passed, 1)
                    nc.scalar.activation(bc[:, at], t.bank[0][0:2 * STATES, 0:CHUNK], ACT.Identity).then_inc(low_done, 1)
                    act.sem_inc(t.passed, 1)
                    nc.scalar.activation(low[:, at], t.bank[1][0:RANK, 0:CHUNK], ACT.Identity).then_inc(low_done, 1)

            @block.vector
            def _(dve):
                dve.wait_ge(coef_done, 1)
                nc.vector.tensor_scalar(coef[:], coef[:], 0.5, None, ALU.mult)
                with dve.Fori(0, CHUNKS) as c:
                    at = bass.ds(CHUNK * c, CHUNK)
                    dve.wait_ge(up, c + 1)
                    for k in range(2):
                        nc.vector.tensor_scalar(rate[:, k, at], t.bank[2 + k][0:HALF, 0:CHUNK],
                                                w["L0_b_dt"][:, k:k + 1], None, ALU.add).then_inc(biased, 1)
        softplus(t, rate)
        with ExitStack() as inner:
            sq = t.sbuf("sq", [HALF, 2, TOKENS], inner)
            rms = t.sbuf("rms", [HALF, 2, CHUNK], inner)
            squared, meant, eps_done, root, inv = t.sem("squared"), t.sem("meant"), t.sem("eps_done"), t.sem("root"), t.sem("inv")
            scaled, tanh_done, clamped, rooted, summed = t.sem("scaled"), t.sem("tanh_done"), t.sem("clamped"), t.sem("rooted"), t.sem("summed")
            with t.block() as block:
                @block.scalar
                def _(act):
                    nc.scalar.preload_act_table(ACT.Sqrt)
                    with act.Fori(0, CHUNKS) as c:
                        at = bass.ds(CHUNK * c, CHUNK)
                        act.sem_inc(t.passed, 1)
                        nc.scalar.activation(sq[:, :, at], rate[:, :, at], ACT.Square).then_inc(squared, 1)
                        act.wait_ge(eps_done, c + 1)
                        nc.scalar.activation(rms[:, 1, :], rms[:, 0, :], ACT.Sqrt).then_inc(root, 1)
                    act.wait_ge(scaled, 2 * CHUNKS)
                    nc.scalar.activation(sq[:], rate[:], ACT.Tanh, scale=1.0 / REACH,
                                         bias=w["clamp"][0:HALF, :]).then_inc(tanh_done, 1)
                    act.wait_ge(clamped, 1)
                    nc.scalar.activation(sq[:], rate[:], ACT.Sqrt).then_inc(rooted, 1)

                @block.tensor
                def _(pe):
                    with pe.Fori(0, CHUNKS) as c:
                        at = bass.ds(CHUNK * c, CHUNK)
                        pe.wait_ge(squared, c + 1)
                        for k in range(2):
                            last = nc.tensor.matmul(t.bank[0][0:HALF, 0:CHUNK], w["mean"][:], sq[:, k, at],
                                                    start=(k == 0), stop=(k == 1))
                        last.then_inc(meant, 1)

                @block.vector
                def _(dve):
                    for k in range(2):
                        xk = t.xT[0:HALF, k, :].rearrange("p (b t) -> p b t", t=SEQ)
                        uk = u[:, k, :].rearrange("p (b t) -> p b t", t=SEQ)
                        nc.vector.tensor_tensor(uk[:, :, 1:SEQ], xk[:, :, 1:SEQ], xk[:, :, 0:SEQ - 1], ALU.add).then_inc(summed, 1)
                        nc.vector.tensor_copy(uk[:, :, 0:1], xk[:, :, 0:1]).then_inc(summed, 1)
                    with dve.Fori(0, CHUNKS) as c:
                        at = bass.ds(CHUNK * c, CHUNK)
                        dve.wait_ge(meant, c + 1)
                        nc.vector.tensor_scalar(rms[:, 0, :], t.bank[0][0:HALF, 0:CHUNK], 1e-6, None, ALU.add).then_inc(eps_done, 1)
                        dve.wait_ge(root, c + 1)
                        nc.vector.reciprocal(rms[:, 1, :], rms[:, 1, :]).then_inc(inv, 1)
                        dve.wait_ge(inv, c + 1)
                        for k in range(2):
                            nc.vector.scalar_tensor_tensor(rate[:, k, at], rate[:, k, at], w["L0_rms"][:, k:k + 1],
                                                           rms[:, 1, :], ALU.mult, ALU.mult).then_inc(scaled, 1)
                        dve.wait_ge(scaled, 2 * c + 2)
                    dve.wait_ge(tanh_done, 1)
                    nc.vector.tensor_scalar(rate[:], sq[:], REACH, CENTRE, ALU.mult, ALU.add).then_inc(clamped, 1)
                    dve.wait_ge(rooted, 1)
                    dve.wait_ge(summed, 4)
                    nc.vector.scalar_tensor_tensor(flat(u[:]), flat(u[:]), 0.5, flat(sq[:]), ALU.mult, ALU.mult)
        y = rate
        scan(t, u, rate, coef, bc, t.xT, w["L0_D"], y, bilinear=True)
        add_back(t, y, t.h)

def route(t, lhs, gate, experts, picks, masks=None, weights=None, total=None, probs=None):
    nc = t.nc
    size = [TILE, TILES, experts]
    with ExitStack() as st:
        logits, ex, eq, chosen = (t.sbuf(n, size, st) for n in ("logits", "ex", "eq", "chosen"))
        top, best = t.sbuf("top", [TILE, TILES], st), t.sbuf("best", [TILE, TILES], st)
        own = t.sbuf("own", size, st)
        multiplied, shifted, exp_done, step = t.sem("multiplied"), t.sem("shifted"), t.sem("exp_done"), t.sem("step")
        spread = lambda v: v[:].unsqueeze(2).to_broadcast(size)
        first = t.w["first"][0:TILE, 0:experts].unsqueeze(1).to_broadcast(size)
        with t.block() as block:
            @block.tensor
            def _(pe):
                for i in range(TILES):
                    for k in range(len(gate)):
                        last = nc.tensor.matmul(t.bank[0][0:TILE, experts * i:experts * (i + 1)], lhs(i, k), gate[k],
                                                start=(k == 0), stop=(k == len(gate) - 1))
                last.then_inc(multiplied, 1)

            @block.scalar
            def _(act):
                act.wait_ge(shifted, 1)
                nc.scalar.activation(ex[:], own[:], ACT.Exp).then_inc(exp_done, 1)

            @block.vector
            def _(dve):
                one = Steps(dve, step)
                dve.wait_ge(multiplied, 1)
                one(nc.vector.tensor_copy(flat(logits[:]), t.bank[0][0:TILE, 0:TILES * experts]))
                one(nc.vector.tensor_reduce(top[:], logits[:], AX.X, ALU.max))
                nc.vector.tensor_tensor(own[:], logits[:], spread(top), ALU.subtract).then_inc(shifted, 1)
                for j in range(picks):
                    if j:
                        one(nc.vector.scalar_tensor_tensor(flat(logits[:]), flat(mask[:]), MASKED, flat(logits[:]), ALU.mult, ALU.add))
                        one(nc.vector.tensor_reduce(top[:], logits[:], AX.X, ALU.max))
                    mask = masks[j] if masks else (chosen if j == 0 else eq)
                    one(nc.vector.tensor_tensor(eq[:], logits[:], spread(top), ALU.is_equal))
                    one(nc.vector.tensor_tensor(eq[:], eq[:], first, ALU.mult))
                    one(nc.vector.tensor_reduce(best[:], eq[:], AX.X, ALU.max))
                    one(nc.vector.tensor_tensor(mask[:], eq[:], spread(best), ALU.is_equal))
                    if weights is not None and masks and j == 0:
                        one(nc.vector.tensor_copy(chosen[:], mask[:]))
                    elif weights is not None and j:
                        one(nc.vector.tensor_tensor(chosen[:], chosen[:], mask[:], ALU.add))
                dve.wait_ge(exp_done, 1)
                if total is not None:
                    one(nc.vector.tensor_reduce(best[:], ex[:], AX.X, ALU.add))
                    one(nc.vector.reciprocal(total[:], best[:]))
                if probs is not None:
                    one(nc.vector.tensor_tensor(probs[:], ex[:], spread(total), ALU.mult))
                if weights is not None:
                    one(nc.vector.tensor_tensor(ex[:], ex[:], chosen[:], ALU.mult))
                    one(nc.vector.tensor_reduce(best[:], ex[:], AX.X, ALU.add))
                    one(nc.vector.reciprocal(top[:], best[:]))
                    one(nc.vector.tensor_tensor(weights[:], ex[:], spread(top), ALU.mult))


def turn(t, src, dst):
    nc = t.nc
    n = src.shape[2]
    turned = t.sem("turned")
    with t.block() as block:
        @block.tensor
        def _(pe):
            for i in range(TILES):
                nc.tensor.transpose(t.bank[i // 4][0:n, TILE * (i % 4):TILE * (i % 4 + 1)], src[:, i, :],
                                    t.w["ident"][0:TILE, 0:TILE]).then_inc(turned, 1)

        @block.scalar
        def _(act):
            for c in range(CHUNKS):
                act.wait_ge(turned, 4 * c + 4)
                nc.scalar.activation(dst[:, CHUNK * c:CHUNK * (c + 1)], t.bank[c][0:n, 0:CHUNK], ACT.Identity)


L0_CODE, L0_EXPERTS = 64, 8
L0_GROUPS = L0_CODE * L0_EXPERTS // 128


def layer0_ffn(t):
    nc, w = t.nc, t.w
    normalise(t, t.h, 1e-5)
    with ExitStack() as st:
        code = t.sbuf("code", [L0_CODE + 1, TOKENS], st)
        mask = t.sbuf("mask", [TILE, TILES, L0_EXPERTS], st)
        prob = t.sbuf("prob", [TILE, TILES], st)
        gate = t.sbuf("gate", [L0_EXPERTS, 1, TOKENS], st)
        up = t.sbuf("up", [128, L0_GROUPS, CHUNK], st)
        picked = t.sbuf("picked", [128, L0_GROUPS, CHUNK], st)
        ones_done, encoded, code_done = t.sem("ones_done"), t.sem("encoded"), t.sem("code_done")
        with t.block() as block:
            @block.vector
            def _(dve):
                nc.vector.memset(code[L0_CODE:L0_CODE + 1, :], 1.0).then_inc(ones_done, 1)

            @block.tensor
            def _(pe):
                for c in range(CHUNKS):
                    at = slice(CHUNK * c, CHUNK * (c + 1))
                    nc.tensor.matmul(t.bank[c][0:L0_CODE, 0:CHUNK], w["L0_enc"][:, 0, :], t.xT[:, 0, at], start=True, stop=False)
                    nc.tensor.matmul(t.bank[c][0:L0_CODE, 0:CHUNK], w["L0_enc"][0:HALF, 1, :], t.xT[0:HALF, 1, at],
                                     start=False, stop=True).then_inc(encoded, 1)

            @block.scalar
            def _(act):
                for c in range(CHUNKS):
                    act.wait_ge(encoded, c + 1)
                    nc.scalar.activation(code[0:L0_CODE, CHUNK * c:CHUNK * (c + 1)], t.bank[c][0:L0_CODE, 0:CHUNK],
                                         ACT.Identity).then_inc(code_done, 1)
        route(t, lambda i, k: code[:, TILE * i:TILE * (i + 1)], [w["L0_switch"][:]], L0_EXPERTS, 1, masks=[mask], total=prob)
        masked = t.sem("masked")
        with t.block() as block:
            @block.vector
            def _(dve):
                nc.vector.tensor_tensor(mask[:], mask[:], prob[:].unsqueeze(2).to_broadcast([TILE, TILES, L0_EXPERTS]),
                                        ALU.mult).then_inc(masked, 1)
        turn(t, mask, gate[:, 0, :])
        up_done, act_done, spread, pick_done, down, added = (
            t.sem(n) for n in ("up_done", "act_done", "spread", "pick_done", "down", "added"))
        G = L0_GROUPS
        with t.block() as block:
            @block.tensor
            def _(pe):
                pe.sem_inc(down, 4)
                with pe.Fori(0, CHUNKS) as c:
                    at = bass.ds(CHUNK * c, CHUNK)
                    pe.wait_ge(act_done, c * G + G)
                    for m in range(G):
                        for k in range(2):
                            last = nc.tensor.matmul(t.bank[m][:, 0:CHUNK], w["L0_w1"][:, k, 128 * m:128 * (m + 1)],
                                                    t.xT[0:HALF, k, at], start=(k == 0), stop=(k == 1))
                        last.then_inc(up_done, 1)
                    for m in range(G):
                        pe.wait_ge(pick_done, c * G + m + 3)
                        pe.sem_inc(t.passed, 1)
                        nc.tensor.matmul(t.bank[4 + m % 2][:, 0:CHUNK], w["L0_pair"][:, m, :], gate[:, 0, at],
                                         start=True, stop=True).then_inc(spread, 1)
                    pe.wait_ge(pick_done, c * G + G + 4)
                    for j in range(4):
                        pe.wait_ge(added, 4 * c + j + 1)
                        for m in range(G):
                            last = nc.tensor.matmul(t.bank[6 + j % 2][0:TILE, 0:DIM], picked[:, m, TILE * j:TILE * (j + 1)],
                                                    w["L0_w2"][:, m, :], start=(m == 0), stop=(m == G - 1))
                        last.then_inc(down, 1)

            @block.scalar
            def _(act):
                act.sem_inc(act_done, G)
                nc.scalar.preload_act_table(ACT.Gelu)
                with act.Fori(0, CHUNKS) as c:
                    for m in range(G):
                        act.wait_ge(up_done, c * G + m + 1)
                        act.wait_ge(pick_done, c * G + m + 1)
                        nc.scalar.activation(up[:, m, :], t.bank[m][:, 0:CHUNK], ACT.Gelu,
                                             bias=w["L0_b1"][:, m:m + 1]).then_inc(act_done, 1)

            @block.vector
            def _(dve):
                dve.sem_inc(pick_done, G)
                dve.sem_inc(added, 2)
                with dve.Fori(0, CHUNKS) as c:
                    dve.wait_ge(down, 4 * c + 4)
                    for m in range(G):
                        dve.wait_ge(act_done, c * G + m + 1 + G)
                        dve.wait_ge(spread, c * G + m + 1)
                        nc.vector.tensor_tensor(picked[:, m, :], up[:, m, :], t.bank[4 + m % 2][:, 0:CHUNK],
                                                ALU.mult).then_inc(pick_done, 1)
                    for j in range(4):
                        dve.wait_ge(down, 4 * c + j + 1 + 4)
                        tile = t.h[:, bass.ds(4 * c + j, 1), :]
                        nc.vector.tensor_tensor(tile, tile, t.bank[6 + j % 2][0:TILE, 0:DIM].unsqueeze(1), ALU.add).then_inc(added, 1)
        add_back(t, gate, t.h, lambda g, i: w["L0_b2"][:, g, :])


def layer1_mixer(t):
    nc, w = t.nc, t.w
    normalise(t, t.h, 1e-5)
    with ExitStack() as st:
        x = t.sbuf("xtile", [HALF + 1, 2, 2, TILE], st)
        qk = t.sbuf("qk", [HALF, 2, 4, TILE], st)
        v_ = t.sbuf("v", [TILE, 2, DIM], st)
        s = t.sbuf("scores", [TILE, 2, TILE], st)
        p = t.sbuf("probs", [TILE, 2, TILE], st)
        pT = t.sbuf("probsT", [TILE, 2, TILE], st)
        low, tot = t.sbuf("low", [TILE, 2], st), t.sbuf("tot", [TILE, 2], st)
        inv = t.sbuf("inv", [TILE, 2], st)
        staged, projected, qk_done, v_done, scored, masked, low_done, exp_done, turned, pT_done, out_done, inv_done, added = (
            t.sem(n) for n in ("staged", "projected", "qk_done", "v_done", "scored", "masked", "low_done", "exp_done",
                               "turned", "pT_done", "out_done", "inv_done", "added"))
        bankP, bankV, bankS = t.bank[0:2], t.bank[2:4], t.bank[4:6]
        with t.block() as block:
            @block.gpsimd
            def _(pool):
                with pool.Fori(0, TILES // 2) as i:
                    for u in range(2):
                        pool.wait_ge(projected, 2 * i + u + 1)
                        pool.sem_inc(t.passed, 1)
                        nc.gpsimd.tensor_copy(x[:, u], t.xT[:, :, bass.ds(TILE * (2 * i + u), TILE)]).then_inc(staged, 1)

            @block.tensor
            def _(pe):
                pe.sem_inc(projected, 2)
                with pe.Fori(0, TILES // 2) as i:
                    n = lambda u: 2 * i + u + 1
                    for u in range(2):
                        pe.wait_ge(staged, n(u))
                        pe.wait_ge(added, n(u))
                        for m in range(4):
                            nc.tensor.matmul(bankP[u][0:HALF, TILE * m:TILE * (m + 1)], w["L1_wqk"][:, 0, HALF * m:HALF * (m + 1)],
                                             x[:, u, 0, :], start=True, stop=False)
                            nc.tensor.matmul(bankP[u][0:HALF, TILE * m:TILE * (m + 1)], w["L1_wqk"][0:HALF, 1, HALF * m:HALF * (m + 1)],
                                             x[0:HALF, u, 1, :], start=False, stop=True)
                        nc.tensor.matmul(bankV[u][0:TILE, 0:DIM], x[:, u, 0, :], w["L1_wv"][:, 0, :], start=True, stop=False)
                        nc.tensor.matmul(bankV[u][0:TILE, 0:DIM], x[0:HALF, u, 1, :], w["L1_wv"][0:HALF, 1, :],
                                         start=False, stop=True).then_inc(projected, 1)
                    for u in range(2):
                        pe.wait_ge(qk_done, n(u))
                        for k in range(2):
                            last = nc.tensor.matmul(bankS[u][0:TILE, 0:TILE], qk[:, u, k, :], qk[:, u, 2 + k, :],
                                                    start=(k == 0), stop=(k == 1))
                        last.then_inc(scored, 1)
                    for u in range(2):
                        pe.wait_ge(exp_done, n(u))
                        nc.tensor.transpose(bankP[u][0:TILE, 0:TILE], p[:, u, :], w["ident"][0:TILE, 0:TILE]).then_inc(turned, 1)
                    for u in range(2):
                        pe.wait_ge(pT_done, n(u))
                        pe.wait_ge(v_done, n(u))
                        nc.tensor.matmul(bankS[u][0:TILE, TILE:TILE + DIM], pT[:, u, :], v_[:, u, :],
                                         start=True, stop=True).then_inc(out_done, 1)

            @block.scalar
            def _(act):
                nc.scalar.preload_act_table(ACT.Exp)
                with act.Fori(0, TILES // 2) as i:
                    n = lambda u: 2 * i + u + 1
                    for u in range(2):
                        act.wait_ge(projected, n(u) + 2)
                        nc.scalar.activation(qk[:, u], bankP[u][0:HALF, 0:4 * TILE].rearrange("p (m n) -> p m n", m=4),
                                             ACT.Identity).then_inc(qk_done, 1)
                    for u in range(2):
                        act.wait_ge(low_done, n(u))
                        nc.scalar.activation(p[:, u, :], s[:, u, :], ACT.Exp, bias=low[:, u:u + 1],
                                             accum_out=tot[:, u:u + 1]).then_inc(exp_done, 1)
                    for u in range(2):
                        act.wait_ge(turned, n(u))
                        nc.scalar.activation(pT[:, u, :], bankP[u][0:TILE, 0:TILE], ACT.Identity).then_inc(pT_done, 1)

            @block.vector
            def _(dve):
                dve.sem_inc(added, 2)
                with dve.Fori(0, TILES // 2) as i:
                    n = lambda u: 2 * i + u + 1
                    for u in range(2):
                        dve.wait_ge(projected, n(u) + 2)
                        nc.vector.tensor_copy(v_[:, u, :], bankV[u][0:TILE, 0:DIM]).then_inc(v_done, 1)
                    for u in range(2):
                        dve.wait_ge(scored, n(u))
                        nc.vector.scalar_tensor_tensor(s[:, u, :], bankS[u][0:TILE, 0:TILE], DIM ** -0.5,
                                                       w["mask"][:], ALU.mult, ALU.add).then_inc(masked, 1)
                    for u in range(2):
                        dve.wait_ge(masked, n(u))
                        nc.vector.tensor_reduce(low[:, u:u + 1], s[:, u, :], AX.X, ALU.max, negate=True).then_inc(low_done, 1)
                    for u in range(2):
                        dve.wait_ge(exp_done, n(u))
                        nc.vector.reciprocal(inv[:, u:u + 1], tot[:, u:u + 1]).then_inc(inv_done, 1)
                    for u in range(2):
                        dve.wait_ge(inv_done, n(u))
                        dve.wait_ge(out_done, n(u))
                        tile = t.h[:, bass.ds(2 * i + u, 1), :]
                        nc.vector.scalar_tensor_tensor(tile, bankS[u][0:TILE, TILE:TILE + DIM].unsqueeze(1), inv[:, u:u + 1],
                                                       tile, ALU.mult, ALU.add).then_inc(added, 1)


def heads_attention(t, wqkv, wproj, dst, unit):
    nc, w = t.nc, t.w
    GROUPS = HEADS // 4
    with ExitStack() as st:
        x = t.sbuf("xtile", [HALF + 1, 2, 2, TILE], st)
        wide = t.sbuf("wide", [TILE, 2, 2 * HEADS, 2 * HEAD], st)
        sq = t.sbuf("sq", [TILE, 2, 2 * HEADS * HEAD], st)
        norm = t.sbuf("norm", [TILE, 2, 3, 2 * HEADS], st)
        v_ = t.sbuf("v", [TILE, 2, DIM], st)
        qkT = t.sbuf("qkT", [128, 2, 2 * GROUPS, TILE], st)
        s = t.sbuf("scores", [TILE, 2, HEADS, TILE], st)
        pT = t.sbuf("probsT", [TILE, HEADS, TILE], st)
        red = t.sbuf("red", [TILE, 2, 3, HEADS], st)
        a = t.sbuf("a", [TILE, 2, DIM], st)
        aT = t.sbuf("aT", [HALF + 1, 2, 2, TILE], st)
        names = ("zeroed", "staged", "projected", "squared", "summed", "rooted", "q_done", "v_done", "turned", "qkT_done",
                 "scored", "masked", "max_done", "shifted", "exp_done", "probs_turned", "pT_done", "weighed",
                 "a_done", "a_turned", "aT_done", "out_done", "added", "step")
        (zeroed, staged, projected, squared, summed, rooted, q_done, v_done, turned, qkT_done, scored, masked, max_done,
         shifted, exp_done, probs_turned, pT_done, weighed, a_done, a_turned, aT_done, out_done, added, step) = (
            t.sem(n) for n in names)
        bankQ, bankV, bankT, bankS = t.bank[0], t.bank[1], t.bank[2:4], t.bank[4:8]
        ident = w["ident"]
        with t.block() as block:
            @block.gpsimd
            def _(pool):
                nc.gpsimd.memset(wide[:], 0.0).then_inc(zeroed, 1)
                with pool.Fori(0, TILES // 2) as i:
                    for u in range(2):
                        pool.wait_ge(projected, 2 * i + u + 1)
                        pool.sem_inc(t.passed, 1)
                        nc.gpsimd.tensor_copy(x[:, u], t.xT[:, :, bass.ds(TILE * (2 * i + u), TILE)]).then_inc(staged, 1)

            @block.tensor
            def _(pe):
                pe.sem_inc(projected, 2)
                pe.wait_ge(zeroed, 2)
                with pe.Fori(0, TILES // 2) as i:
                    n = lambda u: 2 * i + u + 1
                    for u in range(2):
                        pe.wait_ge(staged, n(u))
                        pe.wait_ge(q_done, n(u))
                        pe.wait_ge(added, n(u))
                        for bank, lo, hi in ((bankQ, 0, 2 * DIM), (bankV, 2 * DIM, 3 * DIM)):
                            nc.tensor.matmul(bank[0:TILE, 0:hi - lo], x[:, u, 0, :], wqkv[:, 0, lo:hi], start=True, stop=False)
                            last = nc.tensor.matmul(bank[0:TILE, 0:hi - lo], x[0:HALF, u, 1, :], wqkv[0:HALF, 1, lo:hi],
                                                    start=False, stop=True)
                        last.then_inc(projected, 1)
                        pe.wait_ge(q_done, n(u) + 1)
                        pe.wait_ge(qkT_done, n(u))
                        for g in range(2 * GROUPS):
                            last = nc.tensor.transpose(bankT[g // GROUPS][:, TILE * (g % GROUPS):TILE * (g % GROUPS + 1)],
                                                       wide[:, u, 4 * g:4 * g + 4, :].rearrange("p h e -> p (h e)"),
                                                       ident[0:TILE, 0:TILE])
                        last.then_inc(turned, 1)
                        pe.wait_ge(qkT_done, n(u) + 1)
                        pe.wait_ge(pT_done, 3 * (2 * i + u) + 3)
                        for g in range(GROUPS):
                            for j in range(4):
                                rows = slice(32 * j, 32 * j + HEAD)
                                last = nc.tensor.matmul(bankS[j][0:TILE, TILE * g:TILE * (g + 1)], qkT[rows, u, g, :],
                                                        qkT[rows, u, GROUPS + g, :], start=True, stop=True)
                        last.then_inc(scored, 1)
                        pe.wait_ge(exp_done, n(u))
                        for g in range(GROUPS):
                            for j in range(4):
                                last = nc.tensor.transpose(bankS[g][0:TILE, TILE * j:TILE * (j + 1)], s[:, u, 4 * g + j, :],
                                                           ident[0:TILE, 0:TILE])
                            last.then_inc(probs_turned, 1)
                        pe.wait_ge(v_done, n(u))
                        for g in range(GROUPS):
                            pe.wait_ge(pT_done, 3 * (2 * i + u) + 3 + g + 1)
                            for j in range(4):
                                head = slice(HEAD * (4 * g + j), HEAD * (4 * g + j + 1))
                                last = nc.tensor.matmul(bankV[0:TILE, head], pT[:, 4 * g + j, :], v_[:, u, head], start=True, stop=True)
                        last.then_inc(weighed, 1)
                        pe.wait_ge(a_done, n(u))
                        for k in range(2):
                            last = nc.tensor.transpose(bankV[0:HALF, DIM + TILE * k:DIM + TILE * (k + 1)],
                                                       a[:, u, HALF * k:HALF * (k + 1)], ident[0:TILE, 0:TILE])
                        last.then_inc(a_turned, 1)
                        pe.wait_ge(aT_done, n(u))
                        nc.tensor.matmul(bankV[0:TILE, 0:DIM], aT[:, u, 0, :], wproj[:, 0, :], start=True, stop=False)
                        nc.tensor.matmul(bankV[0:TILE, 0:DIM], aT[0:HALF, u, 1, :], wproj[0:HALF, 1, :],
                                         start=False, stop=True).then_inc(out_done, 1)

            @block.scalar
            def _(act):
                act.sem_inc(qkT_done, 1)
                act.sem_inc(pT_done, 3)
                with act.Fori(0, TILES // 2) as i:
                    n = lambda u: 2 * i + u + 1
                    for u in range(2):
                        act.wait_ge(projected, n(u) + 2)
                        if unit:
                            nc.scalar.activation(sq[:, u, :], bankQ[0:TILE, 0:2 * DIM], ACT.Square).then_inc(squared, 1)
                            act.wait_ge(summed, n(u))
                            nc.scalar.activation(norm[:, u, 1, :], norm[:, u, 0, :], ACT.Sqrt).then_inc(rooted, 1)
                        act.wait_ge(turned, n(u))
                        for half in range(2):
                            last = nc.scalar.activation(qkT[:, u, GROUPS * half:GROUPS * (half + 1), :],
                                                        bankT[half][:, 0:GROUPS * TILE].rearrange("p (g n) -> p g n", g=GROUPS),
                                                        ACT.Identity)
                        last.then_inc(qkT_done, 1)
                        act.wait_ge(shifted, n(u))
                        nc.scalar.activation(s[:, u], s[:, u], ACT.Exp).then_inc(exp_done, 1)
                        act.wait_ge(weighed, n(u))
                        for g in range(GROUPS):
                            act.wait_ge(probs_turned, 3 * (2 * i + u) + g + 1)
                            nc.scalar.activation(pT[:, 4 * g:4 * g + 4, :], bankS[g][0:TILE, 0:4 * TILE].rearrange("p (j n) -> p j n", j=4),
                                                 ACT.Identity).then_inc(pT_done, 1)
                        act.wait_ge(a_turned, n(u))
                        nc.scalar.activation(aT[0:HALF, u], bankV[0:HALF, DIM:DIM + 2 * TILE].rearrange("p (k n) -> p k n", k=2),
                                             ACT.Identity).then_inc(aT_done, 1)

            @block.vector
            def _(dve):
                one = Steps(dve, step)
                dve.sem_inc(added, 1)
                dve.sem_inc(q_done, 1)
                dve.sem_inc(weighed, 1)
                nc.vector.memset(aT[HALF:HALF + 1], 1.0).then_inc(zeroed, 1)
                dve.wait_ge(zeroed, 2)
                with dve.Fori(0, TILES // 2) as i:
                    one.enter(i, 2 * (6 if unit else 2))
                    n = lambda u: 2 * i + u + 1
                    for u in range(2):
                        narrow = bankQ[0:TILE, 0:2 * DIM].rearrange("p (h e) -> p h e", e=HEAD)
                        if unit:
                            dve.wait_ge(squared, n(u))
                            nc.vector.tensor_reduce(norm[:, u, 2, :], sq[:, u, :].rearrange("p (h e) -> p h e", e=HEAD),
                                                    AX.X, ALU.add).then_inc(step, 1)
                            one.done += 1
                            dve.wait_ge(step, one.offset + one.done)
                            nc.vector.tensor_scalar(norm[:, u, 0, :], norm[:, u, 2, :], 1e-24, None, ALU.max).then_inc(summed, 1)
                            dve.wait_ge(rooted, n(u))
                            one(nc.vector.reciprocal(norm[:, u, 2, :], norm[:, u, 1, :]))
                            one(nc.vector.tensor_tensor(norm[:, u, 2, 0:HEADS], norm[:, u, 2, 0:HEADS], w["L2_scale"][:], ALU.mult))
                            nc.vector.tensor_tensor(wide[:, u, :, 0:HEAD], narrow,
                                                    norm[:, u, 2, :].unsqueeze(2).to_broadcast([TILE, 2 * HEADS, HEAD]),
                                                    ALU.mult).then_inc(q_done, 1)
                        else:
                            dve.wait_ge(projected, n(u) + 2)
                            nc.vector.tensor_copy(wide[:, u, :, 0:HEAD], narrow).then_inc(q_done, 1)
                        nc.vector.tensor_copy(v_[:, u, :], bankV[0:TILE, 0:DIM]).then_inc(v_done, 1)
                        dve.wait_ge(scored, n(u))
                        for j in range(4):
                            last = nc.vector.scalar_tensor_tensor(
                                s[:, u].rearrange("p (g j) n -> p j g n", j=4)[:, j], bankS[j][0:TILE, 0:GROUPS * TILE]
                                .rearrange("p (g n) -> p g n", g=GROUPS), 1.0 if unit else HEAD ** -0.5,
                                w["mask"][:].unsqueeze(1).to_broadcast([TILE, GROUPS, TILE]), ALU.mult, ALU.add)
                            last.then_inc(masked, 1)
                        dve.wait_ge(masked, 4 * (2 * i + u) + 4)
                        one(nc.vector.tensor_reduce(red[:, u, 0, :], s[:, u], AX.X, ALU.max))
                        nc.vector.tensor_tensor(s[:, u], s[:, u], red[:, u, 0, :].unsqueeze(2).to_broadcast([TILE, HEADS, TILE]),
                                                ALU.subtract).then_inc(shifted, 1)
                        dve.wait_ge(exp_done, n(u))
                        one(nc.vector.tensor_reduce(red[:, u, 1, :], s[:, u], AX.X, ALU.add))
                        if unit:
                            one(nc.vector.reciprocal(red[:, u, 2, :], red[:, u, 1, :]))
                        else:
                            nc.vector.reciprocal(red[:, u, 2, :], red[:, u, 1, :]).then_inc(max_done, 1)
                            dve.wait_ge(max_done, n(u))
                        dve.wait_ge(weighed, n(u) + 1)
                        nc.vector.tensor_tensor(a[:, u, :].rearrange("p (h e) -> p h e", e=HEAD),
                                                bankV[0:TILE, 0:DIM].rearrange("p (h e) -> p h e", e=HEAD),
                                                red[:, u, 2, :].unsqueeze(2).to_broadcast([TILE, HEADS, HEAD]),
                                                ALU.mult).then_inc(a_done, 1)
                        dve.wait_ge(out_done, n(u))
                        tile = dst[:, bass.ds(2 * i + u, 1), :]
                        nc.vector.tensor_tensor(tile, tile, bankV[0:TILE, 0:DIM].unsqueeze(1), ALU.add).then_inc(added, 1)
                one.leave(TILES // 2)


def experts(t, name, dst, weights, count, rows, func, gated, row_gain=None):
    nc, w, args = t.nc, t.w, t.args
    M = HIDDEN // 128
    ups = [args[f"{name}_up"]] + ([args[f"{name}_gate"]] if gated else [])
    with ExitStack() as st:
        wu = t.sbuf("wu", [rows, 2, len(ups), 2, HIDDEN], st)
        wd = t.sbuf("wd", [128, 2, M, DIM], st)
        hid = t.sbuf("hid", [128, M, CHUNK], st)
        sa = t.sbuf("sa", [128, 2, CHUNK], st)
        own_gain = t.sbuf("own_gain", [HALF, 2, 2, 1], st)
        gain_done = t.sem("gain_done")
        loaded = [t.sem("loaded_even"), t.sem("loaded_odd")]
        used = [t.sem("used_even"), t.sem("used_odd")]
        scaled = [t.sem("scaled_even"), t.sem("scaled_odd")]
        up_done, silu_done, hid_done, down, y_done, added = (
            t.sem(n) for n in ("up_done", "silu_done", "hid_done", "down", "y_done", "added"))
        bankU, bankG, bankY = t.bank[0:2], t.bank[2:4], t.bank[4:8]
        LOADS = len(ups) + 1

        with t.block() as block:
            @block.sync
            def _(sp):
                def load(v, e):
                    for n, up in enumerate(ups):
                        sp.dma_start(wu[:, v, n], up[e].rearrange("a p k m -> (a p) k m") if isinstance(e, type(bass.ds(0, 1))) else up[e]
                                     ).then_inc(loaded[v], 16)
                    down_e = args[f"{name}_down"][e]
                    sp.dma_start(wd[:, v], down_e.rearrange("a p m d -> (a p) m d") if isinstance(e, type(bass.ds(0, 1))) else down_e
                                 ).then_inc(loaded[v], 16)
                for v in range(2):
                    load(v, v)
                with sp.Fori(0, count // 2 - 1) as i:
                    for v in range(2):
                        sp.wait_ge(used[v], i + 1)
                        load(v, bass.ds(2 * i + v + 2, 1))

            @block.gpsimd
            def _(pool):
                if row_gain is not None:
                    with pool.Fori(0, count // 2) as i:
                        for v in range(2):
                            pool.wait_ge(loaded[v], 16 * LOADS * i + 16 * LOADS)
                            pool.sem_inc(t.passed, 1)
                            nc.gpsimd.tensor_copy(own_gain[:, v, :, :], row_gain[:, :, bass.ds(2 * i + v, 1)]).then_inc(gain_done, 1)
                            pool.wait_ge(gain_done, 2 * i + v + 1)
                            pool.sem_inc(t.passed, 1)
                            for n in range(len(ups)):
                                for k in range(2):
                                    last = nc.gpsimd.tensor_scalar(wu[:, v, n, k, :], wu[:, v, n, k, :],
                                                                   own_gain[:, v, k, :], None, ALU.mult)
                                    last.then_inc(scaled[v], 1)

            @block.tensor
            def _(pe):
                pe.sem_inc(down, M)
                with pe.Fori(0, count // 2) as i:
                    for v in range(2):
                        pe.wait_ge(loaded[v], 16 * LOADS * i + 16 * LOADS)
                        if row_gain is not None:
                            pe.wait_ge(scaled[v], 4 * i + 4)
                        pe.sem_inc(t.passed, 1)
                        with pe.Fori(0, CHUNKS) as c:
                            q = (2 * i + v) * CHUNKS + c
                            at = bass.ds(CHUNK * c, CHUNK)

                            def up(m):
                                pe.wait_ge(hid_done, q * M + m + 1)
                                for n, bank in enumerate((bankU, bankG)[0:len(ups)]):
                                    for k in range(2):
                                        part = rows if k == 0 else HALF
                                        last = nc.tensor.matmul(bank[m % 2][:, 0:CHUNK], wu[0:part, v, n, k, 128 * m:128 * (m + 1)],
                                                                t.xT[0:part, k, at], start=(k == 0), stop=(k == 1))
                                last.then_inc(up_done, 1)

                            def down_(m):
                                pe.wait_ge(hid_done, q * M + m + 3)
                                if m == 0:
                                    pe.wait_ge(added, q + 1)
                                for j in range(4):
                                    last = nc.tensor.matmul(bankY[j][0:TILE, 0:DIM], hid[:, m, TILE * j:TILE * (j + 1)], wd[:, v, m, :],
                                                            start=(m == 0), stop=(m == M - 1))
                                last.then_inc(down, 1)

                            up(0)
                            for m in range(1, M):
                                up(m)
                                down_(m - 1)
                            down_(M - 1)
                        pe.drain().then_inc(used[v], 1)

            @block.scalar
            def _(act):
                nc.scalar.preload_act_table(func)
                if not gated:
                    act.sem_inc(hid_done, 2)
                with act.Fori(0, count * CHUNKS) as q:
                    for m in range(M):
                        act.wait_ge(up_done, q * M + m + 1)
                        if gated:
                            act.wait_ge(hid_done, q * M + m + 1)
                            nc.scalar.activation(sa[:, m % 2, :], bankU[m % 2][:, 0:CHUNK], func).then_inc(silu_done, 1)
                        else:
                            act.wait_ge(down, q * M + m + 1)
                            nc.scalar.activation(hid[:, m, :], bankU[m % 2][:, 0:CHUNK], func).then_inc(hid_done, 1)

            @block.vector
            def _(dve):
                dve.sem_inc(added, 1)
                if gated:
                    dve.sem_inc(hid_done, 2)
                with dve.Fori(0, count) as e:
                    with dve.Fori(0, CHUNKS) as c:
                        q = e * CHUNKS + c
                        if gated:
                            for m in range(M):
                                dve.wait_ge(silu_done, q * M + m + 1)
                                dve.wait_ge(down, q * M + m + 1)
                                nc.vector.tensor_tensor(hid[:, m, :], sa[:, m % 2, :], bankG[m % 2][:, 0:CHUNK],
                                                        ALU.mult).then_inc(hid_done, 1)
                        dve.wait_ge(down, q * M + 2 * M)
                        for j in range(4):
                            tile = dst[:, bass.ds(4 * c + j, 1), :]
                            last = nc.vector.scalar_tensor_tensor(tile, bankY[j][0:TILE, 0:DIM].unsqueeze(1),
                                                                  weights[:, bass.ds(4 * c + j, 1), bass.ds(e, 1)], tile,
                                                                  ALU.mult, ALU.add)
                        last.then_inc(added, 1)


def gates(t, w, rows):
    return [w[0:rows, 0, :], w[0:HALF, 1, :]]


def xT_tile(t, rows):
    return lambda i, k: t.xT[0:rows if k == 0 else HALF, k, TILE * i:TILE * (i + 1)]


def add_into(t, dst, src):
    nc = t.nc
    done = t.sem("added_into")
    with t.block() as block:
        @block.vector
        def _(dve):
            nc.vector.tensor_tensor(flat(dst[:]), flat(dst[:]), flat(src[:]), ALU.add).then_inc(done, 1)


def layer1_ffn(t):
    w = t.w
    normalise(t, t.h, 1e-5, keep=t.x, feature_major=False)
    normalise(t, t.x, 1e-5, gain=w["L1_ln1_g"], bias=w["L1_ln1_b"])
    heads_attention(t, w["L1_qkv"], w["L1_proj"], t.x, unit=False)
    normalise(t, t.x, 1e-5, gain=w["L1_ln2_g"], bias=w["L1_ln2_b"])
    add_into(t, t.h, t.x)
    with ExitStack() as st:
        share = t.sbuf("share8", [TILE, TILES, 8], st)
        shareT = t.sbuf("shareT", [8, 1, TOKENS], st)
        route(t, xT_tile(t, HALF + 1), gates(t, w["L1_gate"], HALF + 1), 8, 2, weights=share)
        turn(t, share, shareT[:, 0, :])
        add_back(t, shareT, t.h, lambda g, i: w["L1_b2"][:, g, :])
        experts(t, "L1", t.h, share, 8, HALF + 1, ACT.Gelu, gated=False)


def layer2_mixer(t):
    normalise(t, t.h, 1e-5)
    heads_attention(t, t.w["L2_qkv"], t.w["L2_proj"], t.h, unit=True)

GROUPS2, SLOTS2, CAPACITY = 8, 64, 62
L2_EXPERTS = 8


def layer2_ffn(t):
    nc, w = t.nc, t.w
    E, M = L2_EXPERTS, HIDDEN // 128
    size = [TILE, TILES, E]
    normalise(t, t.h, 1e-5, keep=t.x)
    with ExitStack() as st:
        combine = t.sbuf("combine", [128, E // 2, TOKENS], st)
        taken = t.sbuf("taken", [HALF, 2, E, GROUPS2, SLOTS2], st)
        with ExitStack() as inner:
            m = [t.sbuf(f"choice{j}", size, inner) for j in range(2)]
            prob, chosen, slot, part = (t.sbuf(n, size, inner) for n in ("prob", "chosen", "slot", "part"))
            total = t.sbuf("total", [TILE, TILES], inner)
            route(t, xT_tile(t, HALF), gates(t, w["L2_gate"], HALF), E, 2, masks=m, total=total, probs=prob)
            ranked, step, slots_done = t.sem("ranked"), t.sem("step"), t.sem("slots_done")
            with t.block() as block:
                view = lambda x, par: x[:].rearrange("p (g a) e -> p g a e", a=2)[:, :, par, :]
                rank = lambda b: t.bank[b][0:TILE, 0:GROUPS2 * E]

                @block.tensor
                def _(pe):
                    for j in range(2):
                        for par in range(2):
                            ahead = [(0, 0), (0, 1), (1, 0), (1, 1)][0:2 * j + par]
                            terms = [(w["before"], view(m[j], par))] + [(w["all"], view(m[a], b)) for a, b in ahead]
                            for n, (lhs, rhs) in enumerate(terms):
                                last = nc.tensor.matmul(rank(2 * j + par).rearrange("p (g e) -> p g e", e=E), lhs[:], rhs,
                                                        start=(n == 0), stop=(n == len(terms) - 1))
                    last.then_inc(ranked, 1)

                @block.vector
                def _(dve):
                    one = Steps(dve, step)
                    one(nc.vector.tensor_tensor(chosen[:], m[0][:], m[1][:], ALU.add))
                    one(nc.vector.tensor_tensor(prob[:], prob[:], chosen[:], ALU.mult))
                    dve.wait_ge(ranked, 1)
                    for j in range(2):
                        for par in range(2):
                            one(nc.vector.tensor_tensor(view((slot, part)[j], par), view(m[j], par),
                                                        rank(2 * j + par).rearrange("p (g e) -> p g e", e=E), ALU.mult))
                    one(nc.vector.tensor_tensor(slot[:], slot[:], part[:], ALU.add))
                    one(nc.vector.tensor_tensor(slot[:], slot[:], chosen[:], ALU.add))
                    nc.vector.tensor_scalar(slot[:], slot[:], -1.0, None, ALU.add).then_inc(slots_done, 1)

            xs = t.sbuf("xs2", [TILE, 2, DIM], inner)
            hot = t.sbuf("hot", [TILE, 2, E, SLOTS2], inner)
            gated = t.sbuf("gated", [TILE, 2, E, SLOTS2], inner)
            staged, hot_done, gated_done, filled, taken_done, turned, combine_done = (
                t.sem(n) for n in ("staged", "hot_done", "gated_done", "filled", "taken_done", "turned", "combine_done"))
            full = [TILE, E, SLOTS2]
            with t.block() as block:
                @block.vector
                def _(dve):
                    with dve.Fori(0, GROUPS2) as g:
                        dve.wait_ge(filled, g + 1)
                        dve.wait_ge(turned, 2 * g + 2)
                        for u in range(2):
                            at = bass.ds(2 * g + u, 1)
                            nc.vector.tensor_tensor(
                                hot[:, u], w["slot"][:].unsqueeze(1).to_broadcast(full),
                                slot[:, at, :].rearrange("p a e -> p (a e)").unsqueeze(2).to_broadcast(full), ALU.is_equal).then_inc(hot_done, 1)
                        for u in range(2):
                            at = bass.ds(2 * g + u, 1)
                            dve.wait_ge(hot_done, 2 * g + u + 1)
                            nc.vector.tensor_tensor(
                                gated[:, u], hot[:, u],
                                prob[:, at, :].rearrange("p a e -> p (a e)").unsqueeze(2).to_broadcast(full), ALU.mult).then_inc(gated_done, 1)

                @block.gpsimd
                def _(pool):
                    with pool.Fori(0, GROUPS2) as g:
                        pool.wait_ge(filled, g + 1)
                        pool.sem_inc(t.passed, 1)
                        nc.gpsimd.tensor_copy(xs[:], t.x[:, bass.ds(2 * g, 2), :]).then_inc(staged, 1)

                @block.tensor
                def _(pe):
                    pe.sem_inc(filled, 1)
                    pe.sem_inc(turned, 2)
                    with pe.Fori(0, GROUPS2) as g:
                        pe.wait_ge(staged, g + 1)
                        pe.wait_ge(hot_done, 2 * g + 2)
                        pe.wait_ge(taken_done, 2 * g + 1)
                        for k in range(2):
                            for u in range(2):
                                last = nc.tensor.matmul(t.bank[k][0:HALF, :], xs[:, u, HALF * k:HALF * (k + 1)],
                                                        hot[:, u].rearrange("p e c -> p (e c)"), start=(u == 0), stop=(u == 1))
                        last.then_inc(filled, 1)
                        for u in range(2):
                            pe.wait_ge(gated_done, 2 * g + u + 1)
                            pe.wait_ge(combine_done, 2 * g + u + 1)
                            for b in range(E // 2):
                                last = nc.tensor.transpose(t.bank[2 + u][:, TILE * b:TILE * (b + 1)],
                                                           gated[:, u, 2 * b:2 * b + 2, :].rearrange("p e c -> p (e c)"),
                                                           w["ident"][0:TILE, 0:TILE])
                            last.then_inc(turned, 1)

                @block.scalar
                def _(act):
                    act.sem_inc(taken_done, 1)
                    act.sem_inc(combine_done, 2)
                    with act.Fori(0, GROUPS2) as g:
                        for k in range(2):
                            act.wait_ge(filled, g + 2)
                            act.sem_inc(t.passed, 1)
                            nc.scalar.activation(taken[:, k, :, bass.ds(g, 1), :].rearrange("p e g c -> p e (g c)"),
                                                 t.bank[k][0:HALF, :].rearrange("p (e c) -> p e c", e=E), ACT.Identity).then_inc(taken_done, 1)
                        for u in range(2):
                            act.wait_ge(turned, 2 * g + u + 3)
                            act.sem_inc(t.passed, 1)
                            nc.scalar.activation(combine[:, :, bass.ds(TILE * (2 * g + u), TILE)],
                                                 t.bank[2 + u][:, 0:4 * TILE].rearrange("p (b n) -> p b n", n=TILE),
                                                 ACT.Identity).then_inc(combine_done, 1)
        given = t.sbuf("given", [128, E // 2, GROUPS2, DIM], st)
        inner = ExitStack()
        wu = t.sbuf("wu2", [HALF, 2, 2, HIDDEN], inner)
        wd = t.sbuf("wd2", [128, 2, M, DIM], inner)
        hid = t.sbuf("hid2", [128, 2, M, GROUPS2 * SLOTS2], inner)
        loaded, used = [t.sem("loaded_even"), t.sem("loaded_odd")], [t.sem("used_even"), t.sem("used_odd")]
        up_done, hid_done, down, given_done = t.sem("up_done"), t.sem("hid_done"), t.sem("down"), t.sem("given_done")
        with t.block() as block:
            @block.sync
            def _(sp):
                for v in range(2):
                    sp.dma_start(wu[:, v], t.args["L2_up"][v]).then_inc(loaded[v], 16)
                    sp.dma_start(wd[:, v], t.args["L2_down"][v]).then_inc(loaded[v], 16)
                with sp.Fori(0, E // 2 - 1) as i:
                    for v in range(2):
                        sp.wait_ge(used[v], i + 1)
                        at = bass.ds(2 * i + v + 2, 1)
                        sp.dma_start(wu[:, v], t.args["L2_up"][at].rearrange("a p k m -> (a p) k m")).then_inc(loaded[v], 16)
                        sp.dma_start(wd[:, v], t.args["L2_down"][at].rearrange("a p m d -> (a p) m d")).then_inc(loaded[v], 16)

            @block.tensor
            def _(pe):
                pe.sem_inc(down, 2 * GROUPS2)
                with pe.Fori(0, E // 2) as i:
                    for v in range(2):
                        e = 2 * i + v
                        pe.wait_ge(loaded[v], 32 * i + 32)
                        for m_ in range(M):
                            pe.wait_ge(hid_done, M * e + m_ + 1)
                            for k in range(2):
                                last = nc.tensor.matmul(t.bank[m_ % 2][:, :], wu[:, v, k, 128 * m_:128 * (m_ + 1)],
                                                        taken[:, k, bass.ds(e, 1), :, :].rearrange("p a g c -> p (a g c)"),
                                                        start=(k == 0), stop=(k == 1))
                            last.then_inc(up_done, 1)
                    for v in range(2):
                        e = 2 * i + v
                        pe.wait_ge(hid_done, M * e + M + 2)
                        for g in range(GROUPS2):
                            pe.wait_ge(given_done, GROUPS2 * e + g + 1)
                            for m_ in range(M):
                                last = nc.tensor.matmul(t.bank[2 + g % 4][SLOTS2 * v:SLOTS2 * (v + 1), 0:DIM],
                                                        hid[:, v, m_, SLOTS2 * g:SLOTS2 * (g + 1)], wd[:, v, m_, :],
                                                        start=(m_ == 0), stop=(m_ == M - 1))
                            last.then_inc(down, 1)
                        pe.drain().then_inc(used[v], 1)

            @block.scalar
            def _(act):
                act.sem_inc(hid_done, 2)
                with act.Fori(0, E // 2) as i:
                    for v in range(2):
                        e = 2 * i + v
                        for m_ in range(M):
                            act.wait_ge(up_done, M * e + m_ + 1)
                            if m_ == 0:
                                act.wait_ge(down, GROUPS2 * e + GROUPS2)
                            nc.scalar.activation(hid[:, v, m_, :], t.bank[m_ % 2][:, :], ACT.Relu).then_inc(hid_done, 1)

            @block.vector
            def _(dve):
                dve.sem_inc(given_done, 4)
                with dve.Fori(0, E // 2) as i:
                    for v in range(2):
                        for g in range(GROUPS2):
                            dve.wait_ge(down, GROUPS2 * (2 * i + v) + g + 1 + 2 * GROUPS2)
                            rows = slice(SLOTS2 * v, SLOTS2 * (v + 1))
                            nc.vector.tensor_copy(given[rows, bass.ds(i, 1), g:g + 1, :].rearrange("p a g d -> p (a g) d"),
                                                  t.bank[2 + g % 4][rows, 0:DIM].unsqueeze(1)).then_inc(given_done, 1)
        inner.close()
        add_back(t, combine, t.h, lambda b, i: given[:, b, bass.ds(i, 1), :])


INNER = 2 * DIM
TAPS = 4


def layer3_mixer(t):
    nc, w = t.nc, t.w
    G = INNER // 128
    normalise(t, t.h, 1e-5, keep=t.x, feature_major=False)
    normalise(t, t.x, 1e-6, centred=False, gain=w["L3_g"])
    with ExitStack() as st:
        xc, sz, rate, u = (t.sbuf(n, [128, G, TOKENS], st) for n in ("xc", "sz", "rate3", "u3"))
        bc = t.sbuf("bc3", [2 * STATES + 1, TOKENS], st)
        coef = t.sbuf("coef3", [128, G, STATES], st)
        with ExitStack() as inner:
            xs, cv = t.sbuf("xs3", [128, G, CHUNK], inner), t.sbuf("cv", [128, G, CHUNK], inner)
            up, xs_done, conv_step, conv_done, xc_done, mixed, bc_done, stepped, rate_done = (
                t.sem(n) for n in ("up", "xs_done", "conv_step", "conv_done", "xc_done", "mixed", "bc_done", "stepped", "rate_done"))
            with t.block() as block:
                @block.tensor
                def _(pe):
                    pe.sem_inc(rate_done, G)
                    with pe.Fori(0, CHUNKS) as c:
                        at = bass.ds(CHUNK * c, CHUNK)
                        pe.wait_ge(rate_done, G * c + G)
                        for m in range(2 * G):
                            for k in range(2):
                                last = nc.tensor.matmul(t.bank[m][:, 0:CHUNK], w["L3_in"][:, k, 128 * m:128 * (m + 1)],
                                                        t.xT[0:HALF, k, at], start=(k == 0), stop=(k == 1))
                            last.then_inc(up, 1)
                        pe.wait_ge(xc_done, c + 1)
                        for g in range(G):
                            last = nc.tensor.matmul(t.bank[6][0:2 * STATES + 1, 0:CHUNK], w["L3_xproj"][:, g, :], xc[:, g, at],
                                                    start=(g == 0), stop=(g == G - 1))
                        last.then_inc(mixed, 1)
                        pe.wait_ge(bc_done, c + 1)
                        pe.sem_inc(t.passed, 1)
                        for g in range(G):
                            last = nc.tensor.matmul(t.bank[(7, 0, 1)[g]][:, 0:CHUNK], w["L3_dt"][:, 128 * g:128 * (g + 1)], bc[:, at],
                                                    start=True, stop=True)
                        last.then_inc(stepped, 1)

                @block.scalar
                def _(act):
                    nc.scalar.preload_act_table(ACT.Silu)
                    with act.Fori(0, CHUNKS) as c:
                        at = bass.ds(CHUNK * c, CHUNK)
                        for g in range(G):
                            act.wait_ge(up, 2 * G * c + g + 1)
                            nc.scalar.activation(xs[:, g, :], t.bank[g][:, 0:CHUNK], ACT.Identity).then_inc(xs_done, 1)
                        for g in range(G):
                            act.wait_ge(up, 2 * G * c + G + g + 1)
                            act.sem_inc(t.passed, 1)
                            nc.scalar.activation(sz[:, g, at], t.bank[G + g][:, 0:CHUNK], ACT.Silu)
                        act.wait_ge(conv_done, G * c + G)
                        act.sem_inc(t.passed, 1)
                        nc.scalar.activation(xc[:, :, at], cv[:], ACT.Silu).then_inc(xc_done, 1)
                        act.wait_ge(mixed, c + 1)
                        act.sem_inc(t.passed, 1)
                        nc.scalar.activation(bc[:, at], t.bank[6][0:2 * STATES + 1, 0:CHUNK], ACT.Identity).then_inc(bc_done, 1)

                @block.vector
                def _(dve):
                    one = Steps(dve, conv_step)
                    with dve.Fori(0, CHUNKS) as c:
                        one.enter(c, (TAPS - 1) * G)
                        at = bass.ds(CHUNK * c, CHUNK)
                        for g in range(G):
                            dve.wait_ge(xs_done, G * c + g + 1)
                            x_ = xs[:, g, :].rearrange("p (b t) -> p b t", t=SEQ)
                            y_ = cv[:, g, :].rearrange("p (b t) -> p b t", t=SEQ)
                            tap = lambda k: w["L3_conv"][:, g, k:k + 1]
                            one(nc.vector.tensor_scalar(cv[:, g, :], xs[:, g, :], tap(TAPS - 1), w["L3_conv_b"][:, g:g + 1], ALU.mult, ALU.add))
                            for back in range(1, TAPS):
                                ins = nc.vector.scalar_tensor_tensor(y_[:, :, back:], x_[:, :, 0:SEQ - back], tap(TAPS - 1 - back),
                                                                     y_[:, :, back:], ALU.mult, ALU.add)
                                if back < TAPS - 1:
                                    one(ins)
                                else:
                                    ins.then_inc(conv_done, 1)
                        dve.wait_ge(stepped, c + 1)
                        for g in range(G):
                            nc.vector.tensor_scalar(rate[:, g, at], t.bank[(7, 0, 1)[g]][:, 0:CHUNK], w["L3_b_dt"][:, g:g + 1], None,
                                                    ALU.add).then_inc(rate_done, 1)
                    one.leave(CHUNKS)
            softplus(t, rate)
            exp_done = t.sem("exp_done")
            with t.block() as block:
                @block.scalar
                def _(act):
                    nc.scalar.activation(coef[:], w["L3_A_log"][:], ACT.Exp).then_inc(exp_done, 1)

                @block.vector
                def _(dve):
                    nc.vector.tensor_tensor(flat(u[:]), flat(rate[:]), flat(xc[:]), ALU.mult)
                    dve.wait_ge(exp_done, 1)
                    nc.vector.tensor_scalar(coef[:], coef[:], -1.0, None, ALU.mult)
        scan(t, u, rate, coef, bc, xc, w["L3_D"], xc, bilinear=False)
        with t.block() as block:
            @block.vector
            def _(dve):
                nc.vector.tensor_tensor(flat(xc[:]), flat(xc[:]), flat(sz[:]), ALU.mult)
        add_back(t, xc, t.x, lambda g, i: w["L3_out"][:, g, :])
    normalise(t, t.x, 1e-6, centred=False)
    with ExitStack() as st:
        gate = t.sbuf("gate3", [HALF, 2, 8], st)
        share = t.sbuf("share3", [TILE, TILES, 8], st)
        whole = t.sbuf("whole", [TILE, TILES], st)
        with t.block() as block:
            @block.vector
            def _(dve):
                for k in range(2):
                    nc.vector.tensor_scalar(gate[:, k, :], w["L3_router"][:, k, :], w["L3_g_moe"][:, k:k + 1], None, ALU.mult)
        route(t, xT_tile(t, HALF), gates(t, gate, HALF), 8, 2, weights=share)
        summed = t.sem("summed")
        with t.block() as block:
            @block.vector
            def _(dve):
                nc.vector.tensor_reduce(whole[:], share[:], AX.X, ALU.add).then_inc(summed, 1)
                dve.wait_ge(summed, 1)
                with dve.Fori(0, TILES // 4) as i:
                    for v in range(4):
                        at = bass.ds(4 * i + v, 1)
                        nc.vector.scalar_tensor_tensor(t.h[:, at, :], t.x[:, at, :], whole[:, at], t.h[:, at, :], ALU.mult, ALU.add)
        experts(t, "L3m", t.h, share, 8, HALF, ACT.Silu, gated=True, row_gain=w["L3_g_exp"])


def layer3_ffn(t):
    normalise(t, t.h, 1e-5)
    with ExitStack() as st:
        share = t.sbuf("share16", [TILE, TILES, 16], st)
        route(t, xT_tile(t, HALF), gates(t, t.w["L3f_gate"], HALF), 16, 4, weights=share)
        experts(t, "L3f", t.h, share, 16, HALF, ACT.Silu, gated=True)


def tower(nc, args, out):
    with ExitStack() as stack:
        t = Tower(nc, stack, args)
        embed(t)
        layer0_mixer(t)
        layer0_ffn(t)
        layer1_mixer(t)
        layer1_ffn(t)
        layer2_mixer(t)
        layer2_ffn(t)
        layer3_mixer(t)
        layer3_ffn(t)
        store(t, out, t.h)


def halves(w, bias=None):
    a = w.reshape(2, HALF, -1).transpose(1, 0, 2)
    if bias is None:
        return np.ascontiguousarray(a)
    extra = np.zeros((1, 2, a.shape[2]), np.float32)
    extra[0, 0] = bias.reshape(-1)
    return np.concatenate([a, extra], axis=0)


def columns(v, parts=HALF):
    return np.ascontiguousarray(v.reshape(-1, parts).T)


def stacked(parts):
    return np.ascontiguousarray(np.stack(parts))


def rows128(w):
    return np.ascontiguousarray(w.reshape(-1, 128, w.shape[1]).transpose(1, 0, 2))


def windows():
    inner = range(PATCH)
    spots = [(y, x) for y in inner for x in inner]
    spots += [(-1, x) for x in inner] + [(PATCH, x) for x in inner] + [(y, -1) for y in inner] + [(y, PATCH) for y in inner]
    return [(c, y, x) for c in range(CHANNELS) for y, x in spots]


READS = ((0, 0), (0, -1), (0, 1), (-1, 0), (1, 0))


def layout(inputs):
    f = {k: np.asarray(v) for k, v in inputs.items()}
    a = {}
    spots = windows()
    c, y, x = (np.array(v) for v in zip(*spots))
    padded = np.pad(f["x"], ((0, 0), (0, 0), (1, 1), (1, 1)))
    rows = PATCH * np.arange(GRID)
    px = padded[:, c[:, None, None], (y[:, None] + rows + 1)[:, :, None], (x[:, None] + rows + 1)[:, None, :]]
    seq = np.zeros((IMAGES, WINDOW, SEQ), np.float32)
    seq[:, :, 1:] = px.reshape(IMAGES, WINDOW, SEQ - 1)
    a["pixels"] = np.ascontiguousarray(seq.reshape(TILES, 2, WCHUNKS, WROWS, SEQ).transpose(0, 3, 2, 1, 4)
                                       .reshape(TILES, WROWS, WCHUNKS, TILE))
    wide = np.zeros((SHIFTS, WINDOW, DIM + 2), np.float32)
    stack = np.concatenate([f["L0_tok_proj_weight"], f["L0_tok_ln_weight"][None], f["L0_tok_ln_bias"][None]])
    stack = stack.reshape(DIM + 2, PATCH, PATCH, SHIFTS, CHANNELS)
    count = np.zeros(WINDOW, np.float32)
    for s, (dy, dx) in enumerate(READS):
        ys, xs = y - dy, x - dx
        ok = (ys >= 0) & (ys < PATCH) & (xs >= 0) & (xs < PATCH)
        wide[s, ok] = stack[:, ys[ok], xs[ok], s, c[ok]].T
        count[ok] += 1
    wide = wide.reshape(SHIFTS, WCHUNKS, WROWS, DIM + 2).transpose(2, 1, 0, 3)
    a["w_patch"] = np.ascontiguousarray(wide[..., :DIM])
    a["ln_gain"] = np.ascontiguousarray(wide[..., DIM:].transpose(0, 3, 1, 2))
    a["share"] = np.ascontiguousarray((count / PATCH_DIM).astype(np.float32).reshape(WCHUNKS, WROWS).T)
    a["patch_bias"] = f["L0_tok_proj_bias"].reshape(1, DIM)
    a["cls"] = f["cls_tok"].reshape(1, 1, DIM)
    a["c_ident"] = np.eye(128, dtype=np.float32)
    a["c_minus_one"] = np.full((128, 1), -1.0, np.float32)
    a["c_mean"] = np.full((HALF, HALF), 1.0 / DIM, np.float32)
    a["c_clamp"] = np.full((128, 1), -CENTRE / REACH, np.float32)
    for name in ("W_bc", "W_dt"):
        a["c_L0_" + name] = halves(f["L0_attn_" + name])
    a["c_L0_W_dtp"] = f["L0_attn_W_dtp"]
    a["c_L0_A_log"] = halves(f["L0_attn_A_log"])
    for name, key in (("b_dt", "b_dt"), ("rms", "rms_scale"), ("D", "D_param")):
        a["c_L0_" + name] = columns(f["L0_attn_" + key])
    a["c_first"] = np.tile(np.arange(16, 0, -1, dtype=np.float32), (128, 1))
    own = np.arange(TILE) // SEQ
    a["c_mask"] = np.where(own[:, None] == own[None, :], 0.0, MASKED).astype(np.float32)
    a["c_L0_enc"] = halves(f["L0_ffn_enc_w"], f["L0_ffn_enc_b"])
    a["c_L0_switch"] = np.concatenate([f["L0_ffn_sw_w"], f["L0_ffn_sw_b"][None]])
    a["c_L0_w1"] = halves(f["L0_ffn_w1"].transpose(1, 0, 2).reshape(DIM, -1))
    a["c_L0_b1"] = columns(f["L0_ffn_b1"], 128)
    a["c_L0_w2"] = np.ascontiguousarray(f["L0_ffn_w2"].reshape(L0_GROUPS, 128, DIM).transpose(1, 0, 2))
    a["c_L0_b2"] = f["L0_ffn_b2"].reshape(L0_EXPERTS, 1, DIM)
    row = np.arange(L0_GROUPS * 128).reshape(L0_GROUPS, 128) // L0_CODE
    a["c_L0_pair"] = (row[None] == np.arange(L0_EXPERTS)[:, None, None]).astype(np.float32)
    wq, wk, wv = (f["L1_attn_W" + x] for x in "qkv")
    a["c_L1_wqk"] = halves(np.concatenate([wq.T, wk.T], 1), np.concatenate([f["L1_attn_bq"], f["L1_attn_bk"]]))
    a["c_L1_wv"] = halves(wv.T, f["L1_attn_bv"])
    for name in ("ln1_g", "ln1_b", "ln2_g", "ln2_b"):
        a["c_L1_" + name] = columns(f["L1_ffn_" + name])
    a["c_L1_qkv"] = halves(f["L1_ffn_qkv_w"].T, np.zeros(3 * DIM, np.float32))
    a["c_L1_proj"] = halves(f["L1_ffn_proj_w"].T, f["L1_ffn_proj_b"])
    a["c_L1_gate"] = halves(f["L1_ffn_gate_w"].T, f["L1_ffn_gate_b"])
    a["c_L1_b2"] = f["L1_ffn_b2"].reshape(8, 1, DIM)
    a["L1_up"] = stacked([halves(f["L1_ffn_w1"][e].T, f["L1_ffn_b1"][e]) for e in range(8)])
    a["L1_down"] = stacked([rows128(f["L1_ffn_w2"][e].T) for e in range(8)])
    a["c_L2_qkv"] = halves(np.concatenate([f["L2_attn_Wq"], f["L2_attn_Wkv"]], 1), np.concatenate([f["L2_attn_bq"], f["L2_attn_bkv"]]))
    a["c_L2_proj"] = halves(f["L2_attn_Wproj"], f["L2_attn_bproj"])
    a["c_L2_scale"] = np.tile(f["L2_attn_scale"].reshape(1, HEADS), (TILE, 1))
    token = np.arange(TILE)
    a["c_before"] = (token[:, None] < token[None, :]).astype(np.float32)
    a["c_all"] = np.ones((TILE, TILE), np.float32)
    a["c_slot"] = np.tile(np.where(np.arange(SLOTS2) < CAPACITY, np.arange(SLOTS2), -5), (TILE, 1)).astype(np.float32)
    a["c_L2_gate"] = halves(f["L2_ffn_w_router"])
    a["L2_up"] = stacked([halves(x) for x in f["L2_ffn_wi"]])
    a["L2_down"] = stacked([rows128(x) for x in f["L2_ffn_wo"]])
    a["c_L3_g"] = columns(f["L3_attn_g_mamba"])
    a["c_L3_in"] = halves(f["L3_attn_w_in"])
    a["c_L3_conv"] = rows128(f["L3_attn_conv_w"])
    a["c_L3_conv_b"] = columns(f["L3_attn_conv_b"], 128)
    a["c_L3_xproj"] = rows128(f["L3_attn_w_xproj"])
    a["c_L3_dt"] = np.concatenate([np.zeros((2 * STATES, INNER), np.float32), f["L3_attn_w_dt"]])
    a["c_L3_b_dt"] = columns(f["L3_attn_b_dt"], 128)
    a["c_L3_A_log"] = rows128(f["L3_attn_A_log"])
    a["c_L3_D"] = columns(f["L3_attn_D_skip"], 128)
    a["c_L3_out"] = rows128(f["L3_attn_w_out"])
    a["c_L3_router"] = halves(f["L3_attn_w_router"])
    a["c_L3_g_moe"] = columns(f["L3_attn_g_moe"])
    a["c_L3_g_exp"] = halves(f["L3_attn_g_exp"].T)
    a["L3m_up"] = stacked([halves(x) for x in f["L3_attn_w1"]])
    a["L3m_gate"] = stacked([halves(x) for x in f["L3_attn_w3"]])
    a["L3m_down"] = stacked([rows128(x) for x in f["L3_attn_w2"]])
    a["c_L3f_gate"] = halves(f["L3_ffn_router_w"].T)
    a["L3f_up"] = stacked([halves(x.T) for x in f["L3_ffn_w1"]])
    a["L3f_gate"] = stacked([halves(x.T) for x in f["L3_ffn_v1"]])
    a["L3f_down"] = stacked([rows128(x.T) for x in f["L3_ffn_w2"]])
    return a


def kernel(**inputs):
    import concourse.bacc as _bacc
    from concourse.bass_utils import run_bass_kernel_spmd as _run

    nc = _bacc.Bacc("TRN2", target_bir_lowering=False, num_devices=1)
    arrays = layout(inputs)
    args = {k: nc.dram_tensor(k, v.shape, F32, kind="ExternalInput").ap() for k, v in arrays.items()}
    out = nc.dram_tensor("out", (TOKENS, DIM), F32, kind="ExternalOutput").ap()
    tower(nc, args, out)
    r = _run(nc, [arrays], core_ids=[0])
    return r.results[0]["out"].reshape(IMAGES, SEQ, DIM)
```

```python
from contextlib import ExitStack, contextmanager

import numpy as np

import concourse.bass as bass
from concourse import mybir

F32 = mybir.dt.float32
BF16 = mybir.dt.bfloat16
ALU = mybir.AluOpType
ACT = mybir.ActivationFunctionType
AX = mybir.AxisListType

IMAGES, SEQ, DIM = 32, 50, 192
TOKENS = IMAGES * SEQ
TILE = 2 * SEQ
TILES = TOKENS // TILE
HALF = DIM // 2
CHUNK = 4 * TILE
CHUNKS = TOKENS // CHUNK
PATCH, CHANNELS, SHIFTS, GRID = 16, 3, 5, 7
PATCH_DIM = PATCH * PATCH * CHANNELS * SHIFTS
WINDOW = CHANNELS * (PATCH * PATCH + 4 * PATCH)
WROWS = 120
WCHUNKS = WINDOW // WROWS
HEADS, HEAD = 12, 16
HIDDEN = 768
MASKED = -1.0e30


class Steps:

    def __init__(self, engine, sem):
        self.engine, self.sem, self.done, self.offset = engine, sem, 0, None

    def __call__(self, instruction):
        instruction.then_inc(self.sem, 1)
        self.done += 1
        self.engine.wait_ge(self.sem, self.done if self.offset is None else self.offset + self.done)

    def enter(self, index, per):
        self.per, self.start, self.offset = per, self.done, index * per
        return self

    def leave(self, count):
        assert self.done - self.start == self.per, (self.done - self.start, self.per)
        self.done, self.offset = self.start + count * self.per, None


class Tower:

    def __init__(self, nc, stack, args):
        self.nc, self.stack, self.args, self.sems, self.tensors = nc, stack, args, 0, 0
        sb = self.sbuf
        self.h = sb("h", [TILE, TILES, DIM])
        self.x = sb("x", [TILE, TILES, DIM])
        self.xT = sb("xT", [HALF + 1, 2, TOKENS + TILE])
        self.bank = [stack.enter_context(nc.psum_tensor(f"bank{i}", [128, 512], F32)) for i in range(8)]
        self.old, self.theirs, self.new, self.mine = ExitStack(), [], ExitStack(), []
        self.loaded = self.sem("constants_loaded", lasting=True)
        self.loads = []
        self.passed = self.sem("passed", lasting=True)
        self.zeros = sb("zeros", [128, DIM])
        self.slots = nc.dram_tensor("slots", (MOST_BLOCKS + 1, SUBS, 128, DIM), F32, kind="Internal").ap()
        self.results = nc.dram_tensor("results", (MOST_BLOCKS, SUBS, 128, DIM), F32, kind="Internal").ap()
        self.w = {}
        for name, ap in args.items():
            if name.startswith("c_"):
                self.w[name[2:]] = t = sb(name, list(ap.shape))
                self.loads.append((t, ap))

    def sbuf(self, name, shape, stack=None, dtype=F32):
        self.tensors += 1
        return (stack or self.stack).enter_context(self.nc.sbuf_tensor(f"{name}_{self.tensors}", shape, dtype))

    def sem(self, name, lasting=False):
        self.sems += 1
        stack = self.stack if lasting else self.new
        sem = stack.enter_context(self.nc.semaphore(f"{name}_{self.sems}"))
        if not lasting:
            self.mine.append(sem)
        return sem

    @contextmanager
    def block(self):
        with self.nc.Block() as block:
            if self.theirs:
                @block.sync
                def _(sp):
                    for sem in self.theirs:
                        sp.sem_clear(sem)
            yield block
        self.old.close()
        self.old, self.theirs = self.new, self.mine
        self.new, self.mine = ExitStack(), []


def flat(ap):
    return ap.rearrange("p a b -> p (a b)")


def embed(t):
    nc = t.nc
    with ExitStack() as st:
        pixels = t.sbuf("pixels", [WROWS, 2, WCHUNKS, TILE], st)
        squares = t.sbuf("squares", [WROWS, 2, WCHUNKS, TILE], st)
        wshift = t.sbuf("wshift", [WROWS, WCHUNKS, SHIFTS, DIM], st)
        wsum = t.sbuf("wsum", [WROWS, WCHUNKS, DIM + 1], st)
        gain = t.sbuf("gain", [WROWS, 2, WCHUNKS, SHIFTS], st)
        share = t.sbuf("share", [WROWS, WCHUNKS], st)
        lift = t.sbuf("lift", [WROWS, 2, TILE], st)
        onesr = t.sbuf("onesr", [WROWS, TILE], st)
        zero = t.sbuf("zero", [1, DIM], st)
        pbias = t.sbuf("pbias", [1, DIM], st)
        rows = t.sbuf("rows", [TILE, 2, DIM], st)
        stats = t.sbuf("pstats", [TILE, TILES, 2], st)
        var = t.sbuf("pvar", [TILE, 4, TILES], st)
        weights_in, pixels_in, cls_in = t.sem("weights_in"), [t.sem("pixels_even"), t.sem("pixels_odd")], t.sem("cls_in")
        wsum_done, squared, multiplied, stored = t.sem("wsum_done"), t.sem("squared"), t.sem("multiplied"), t.sem("stored")
        bias_done, rows_done, lifted, lift_used = t.sem("bias_done"), t.sem("rows_done"), t.sem("lifted"), t.sem("lift_used")
        step, var_done, root_done, h_done = t.sem("step"), t.sem("var_done"), t.sem("root_done"), t.sem("h_done")
        raw, fixed = t.bank[0:2], t.bank[2:4]
        args = t.args

        with t.block() as block:
            @block.sync
            def _(sp):
                sp.dma_start(gain[:], args["ln_gain"]).then_inc(weights_in, 16)
                sp.dma_start(wshift[:], args["w_patch"]).then_inc(weights_in, 16)
                sp.dma_start(share[:], args["share"]).then_inc(weights_in, 16)
                sp.dma_start(pbias[:], args["patch_bias"]).then_inc(weights_in, 16)
                for u in range(2):
                    sp.dma_start(pixels[:, u], args["pixels"][u]).then_inc(pixels_in[u], 16)
                with sp.Fori(0, TILES // 2 - 1) as i:
                    for u in range(2):
                        sp.wait_ge(multiplied, 2 * i + u + 1)
                        sp.dma_start(pixels[:, u], args["pixels"][bass.ds(2 * i + u + 2, 1)]
                                     .rearrange("a p c n -> p (a c) n")).then_inc(pixels_in[u], 16)
                for dst, src in t.loads:
                    sp.dma_start(dst[:], src).then_inc(t.loaded, 16)
                sp.wait_ge(h_done, TILES)
                for image in range(2):
                    sp.dma_start(t.h[SEQ * image:SEQ * image + 1, :, :],
                                 args["cls"].to_broadcast([1, TILES, DIM])).then_inc(cls_in, 16)
                sp.wait_ge(cls_in, 32)
                sp.wait_ge(t.loaded, 16 * len(t.loads))

            @block.vector
            def _(dve):
                one = Steps(dve, step)
                one(nc.vector.memset(zero[:], 0.0))
                nc.vector.memset(onesr[:], 1.0).then_inc(wsum_done, 1)
                one(nc.vector.memset(t.xT[:, :, TOKENS:], 0.0))
                one(nc.vector.memset(t.xT[HALF:HALF + 1, :, :], 1.0))
                dve.wait_ge(weights_in, 64)
                for c in range(WCHUNKS):
                    for s in range(SHIFTS):
                        if s == 0:
                            one(nc.vector.tensor_scalar(wsum[:, c, 0:DIM], wshift[:, c, s, :],
                                                        gain[:, 0, c, s:s + 1], None, ALU.mult))
                        else:
                            one(nc.vector.scalar_tensor_tensor(
                                wsum[:, c, 0:DIM], wshift[:, c, s, :], gain[:, 0, c, s:s + 1],
                                wsum[:, c, 0:DIM], ALU.mult, ALU.add))
                nc.vector.tensor_copy(wsum[:, :, DIM:DIM + 1], share[:].unsqueeze(2)).then_inc(wsum_done, 1)
                with dve.Fori(0, WCHUNKS * SHIFTS // 4) as i:
                    for u in range(4):
                        dve.wait_ge(lift_used, 4 * i + u + 1)
                        nc.vector.tensor_scalar(
                            lift[:, u % 2, :], onesr[:],
                            gain[:, 1, :, :].rearrange("p c s -> p (c s)")[:, bass.ds(4 * i + u, 1)],
                            None, ALU.mult).then_inc(lifted, 1)
                dve.wait_ge(bias_done, 1)
                nc.vector.tensor_copy(rows[:, 0, :], fixed[0][0:TILE, 0:DIM])
                one(nc.vector.tensor_copy(rows[:, 1, :], fixed[1][0:TILE, 0:DIM]))
                with dve.Fori(0, TILES // 2) as i:
                    for u in range(2):
                        dve.wait_ge(multiplied, 2 * i + u + 1)
                        nc.vector.tensor_copy(t.h[:, bass.ds(2 * i + u, 1), :],
                                              raw[u][0:TILE, 0:DIM].unsqueeze(1))
                        nc.vector.tensor_copy(stats[:, bass.ds(2 * i + u, 1), :],
                                              raw[u][0:TILE, DIM:DIM + 2].unsqueeze(1)).then_inc(stored, 1)
                dve.wait_ge(stored, TILES + 2)
                mean, second = stats[:, :, 0], stats[:, :, 1]
                one(nc.vector.tensor_tensor(var[:, 0, :], mean, mean, ALU.mult))
                one(nc.vector.tensor_tensor(var[:, 1, :], second, var[:, 0, :], ALU.subtract))
                nc.vector.tensor_scalar(var[:, 2, :], var[:, 1, :], 0.0, 1e-5, ALU.max, ALU.add).then_inc(var_done, 1)
                dve.wait_ge(root_done, 1)
                one(nc.vector.reciprocal(var[:, 1, :], var[:, 3, :]))
                one(nc.vector.tensor_scalar(var[:, 0, :], mean, -1.0, None, ALU.mult))
                with dve.Fori(0, TILES // 2) as i:
                    one.enter(i, 2)
                    for u in range(2):
                        tile = t.h[:, bass.ds(2 * i + u, 1), :]
                        one(nc.vector.scalar_tensor_tensor(tile, rows[:, 0:1, :], var[:, 0, bass.ds(2 * i + u, 1)],
                                                           tile, ALU.mult, ALU.add))
                        nc.vector.scalar_tensor_tensor(tile, tile, var[:, 1, bass.ds(2 * i + u, 1)],
                                                       rows[:, 1:2, :], ALU.mult, ALU.add).then_inc(h_done, 1)
                one.leave(TILES // 2)

            @block.scalar
            def _(act):
                with act.Fori(0, TILES // 2) as i:
                    for u in range(2):
                        act.wait_ge(pixels_in[u], 16 * i + 16)
                        nc.scalar.activation(squares[:, u], pixels[:, u], ACT.Square).then_inc(squared, 1)
                act.wait_ge(var_done, 1)
                nc.scalar.activation(var[:, 3, :], var[:, 2, :], ACT.Sqrt).then_inc(root_done, 1)

            @block.tensor
            def _(pe):
                pe.sem_inc(stored, 2)
                pe.sem_inc(lift_used, 2)
                pe.wait_ge(wsum_done, 2)
                for c in range(WCHUNKS):
                    nc.tensor.matmul(fixed[0][0:TILE, 0:DIM], onesr[:], wsum[:, c, 0:DIM],
                                     start=(c == 0), stop=(c == WCHUNKS - 1))
                nc.tensor.matmul(fixed[1][0:TILE, 0:DIM], onesr[0:1, :], pbias[:], start=True, stop=False)
                flat_w = wshift[:].rearrange("p c s d -> p (c s) d")
                with pe.Fori(0, WCHUNKS * SHIFTS // 4) as i:
                    for u in range(4):
                        pe.wait_ge(lifted, 4 * i + u + 1)
                        nc.tensor.matmul(fixed[1][0:TILE, 0:DIM], lift[:, u % 2, :],
                                         flat_w[:, bass.ds(4 * i + u, 1), :], start=False, stop=False).then_inc(lift_used, 1)
                nc.tensor.matmul(fixed[1][0:TILE, 0:DIM], onesr[0:1, :], zero[:], start=False, stop=True).then_inc(bias_done, 1)
                with pe.Fori(0, TILES // 2) as i:
                    for u in range(2):
                        pe.wait_ge(squared, 2 * i + u + 1)
                        pe.wait_ge(stored, 2 * i + u + 1)
                        for c in range(WCHUNKS):
                            nc.tensor.matmul(raw[u][0:TILE, 0:DIM + 1], pixels[:, u, c, :], wsum[:, c, :],
                                             start=(c == 0), stop=(c == WCHUNKS - 1))
                        for c in range(WCHUNKS):
                            last = nc.tensor.matmul(raw[u][0:TILE, DIM + 1:DIM + 2], squares[:, u, c, :],
                                                    share[:, c:c + 1], start=(c == 0), stop=(c == WCHUNKS - 1))
                        last.then_inc(multiplied, 1)


def normalise(t, src, eps, *, keep=None, centred=True, gain=None, bias=None, feature_major=True):
    nc = t.nc
    with ExitStack() as st:
        bn = t.sbuf("bn", [TILE, TILES, 6], st)
        mv = t.sbuf("mv", [TILE, TILES, 2], st)
        sd = t.sbuf("sd", [TILE, 4, TILES], st)
        xs = t.sbuf("xs", [TILE, 2, DIM], st)
        bn_done, mv_done, step = t.sem("bn_done"), t.sem("mv_done"), t.sem("step")
        var_done, root_done = t.sem("var_done"), t.sem("root_done")
        scaled, turned, kept, copied = t.sem("scaled"), t.sem("turned"), t.sem("kept"), t.sem("copied")
        ident = t.w["ident"]

        with t.block() as block:
            @block.vector
            def _(dve):
                one = Steps(dve, step)
                with dve.Fori(0, TILES // 4) as i:
                    for u in range(4):
                        nc.vector.bn_stats(bn[:, bass.ds(4 * i + u, 1), :],
                                           src[:, bass.ds(4 * i + u, 1), :]).then_inc(bn_done, 1)
                dve.wait_ge(bn_done, TILES)
                for i in range(TILES):
                    nc.vector.bn_aggr(mv[:, i, :], bn[:, i, :]).then_inc(mv_done, 1)
                dve.wait_ge(mv_done, TILES)
                mean, var = mv[:, :, 0], mv[:, :, 1]
                if not centred:
                    one(nc.vector.tensor_tensor(sd[:, 2, :], mean, mean, ALU.mult))
                    one(nc.vector.tensor_tensor(sd[:, 3, :], sd[:, 2, :], var, ALU.add))
                    var = sd[:, 3, :]
                nc.vector.tensor_scalar(sd[:, 0, :], var, eps, None, ALU.add).then_inc(var_done, 1)
                dve.wait_ge(root_done, 1)
                one(nc.vector.reciprocal(sd[:, 2, :], sd[:, 1, :]))
                with dve.Fori(0, TILES // 2) as i:
                    for u in range(2):
                        if feature_major:
                            dve.wait_ge(turned, 2 * i + u + 1)
                        if keep is not None:
                            dve.wait_ge(kept, 2 * i + u + 1)
                        at = bass.ds(2 * i + u, 1)
                        if centred:
                            nc.vector.tensor_scalar(xs[:, u:u + 1, :], src[:, at, :], mv[:, at, 0:1], sd[:, 2, at],
                                                    ALU.subtract, ALU.mult).then_inc(scaled, 1)
                        else:
                            nc.vector.tensor_scalar(xs[:, u:u + 1, :], src[:, at, :], sd[:, 2, at], None,
                                                    ALU.mult).then_inc(scaled, 1)

            @block.gpsimd
            def _(pool):
                if keep is not None:
                    pool.sem_inc(kept, 2)
                    with pool.Fori(0, TILES // 2) as i:
                        for u in range(2):
                            pool.wait_ge(scaled, 2 * i + u + 1)
                            pool.sem_inc(t.passed, 1)
                            nc.gpsimd.tensor_copy(keep[:, bass.ds(2 * i + u, 1), :], xs[:, u:u + 1, :]).then_inc(kept, 1)

            @block.scalar
            def _(act):
                act.wait_ge(var_done, 1)
                nc.scalar.activation(sd[:, 1, :], sd[:, 0, :], ACT.Sqrt).then_inc(root_done, 1)
                if feature_major:
                    act.sem_inc(copied, 2)
                    with act.Fori(0, TILES // 2) as i:
                        for u in range(2):
                            act.wait_ge(turned, 2 * i + u + 3)
                            at = bass.ds(TILE * (2 * i + u), TILE)
                            from_psum = t.bank[u][0:HALF, 0:2 * TILE].rearrange("p (k n) -> p k n", k=2)
                            if gain is None:
                                act.sem_inc(t.passed, 1)
                                nc.scalar.activation(t.xT[0:HALF, :, at], from_psum, ACT.Identity).then_inc(copied, 1)
                            else:
                                for k in range(2):
                                    act.sem_inc(t.passed, 1)
                                    last = nc.scalar.activation(
                                        t.xT[0:HALF, k:k + 1, at], from_psum[:, k:k + 1, :], ACT.Identity,
                                        scale=gain[0:HALF, k:k + 1], bias=bias[0:HALF, k:k + 1] if bias is not None else 0.0)
                                last.then_inc(copied, 1)

            @block.tensor
            def _(pe):
                if feature_major:
                    pe.sem_inc(turned, 2)
                    with pe.Fori(0, TILES // 2) as i:
                        for u in range(2):
                            pe.wait_ge(scaled, 2 * i + u + 1)
                            pe.wait_ge(copied, 2 * i + u + 1)
                            for k in range(2):
                                last = nc.tensor.transpose(t.bank[u][0:HALF, TILE * k:TILE * (k + 1)],
                                                           xs[:, u, HALF * k:HALF * (k + 1)], ident[0:TILE, 0:TILE])
                            last.then_inc(turned, 1)


def store(t, out, src):
    nc = t.nc
    stored = t.sem("out_stored")
    with t.block() as block:
        @block.sync
        def _(sp):
            sp.dma_start(out.rearrange("(t p) d -> p t d", p=TILE), src[:]).then_inc(stored, 16)
            sp.wait_ge(stored, 16)

def softplus(t, z):
    nc = t.nc
    parts, groups = z.shape[0], z.shape[1]
    with ExitStack() as st:
        e, w, l, d = (t.sbuf(n, [parts, groups, CHUNK], st) for n in ("sp_e", "sp_w", "sp_ln", "sp_d"))
        abs_done, exp_done, w_done, ln_done = t.sem("abs_done"), t.sem("exp_done"), t.sem("w_done"), t.sem("ln_done")
        step, out_done = t.sem("step"), t.sem("out_done")
        with t.block() as block:
            @block.scalar
            def _(act):
                nc.scalar.preload_act_table_set("natural_log_exp_and_others")
                with act.Fori(0, CHUNKS) as c:
                    act.wait_ge(out_done, c + 1)
                    act.sem_inc(t.passed, 1)
                    nc.scalar.activation(d[:], z[:, :, bass.ds(CHUNK * c, CHUNK)], ACT.Abs).then_inc(abs_done, 1)
                    act.wait_ge(abs_done, c + 1)
                    nc.scalar.activation(e[:], d[:], ACT.Exp, scale=-1.0).then_inc(exp_done, 1)
                    act.wait_ge(w_done, c + 1)
                    nc.scalar.activation(l[:], w[:], ACT.Ln).then_inc(ln_done, 1)

            @block.vector
            def _(dve):
                one = Steps(dve, step)
                dve.sem_inc(out_done, 1)
                with dve.Fori(0, CHUNKS) as c:
                    one.enter(c, 4)
                    zc = z[:, :, bass.ds(CHUNK * c, CHUNK)]
                    dve.wait_ge(exp_done, c + 1)
                    nc.vector.tensor_scalar(w[:], e[:], 1.0, 1.0 + 2.0 ** -23, ALU.add, ALU.max).then_inc(w_done, 1)
                    dve.wait_ge(w_done, c + 1)
                    one(nc.vector.tensor_scalar(d[:], w[:], -1.0, None, ALU.add))
                    one(nc.vector.reciprocal(d[:], d[:]))
                    one(nc.vector.tensor_tensor(d[:], d[:], e[:], ALU.mult))
                    dve.wait_ge(ln_done, c + 1)
                    one(nc.vector.tensor_tensor(d[:], d[:], l[:], ALU.mult))
                    nc.vector.scalar_tensor_tensor(zc, zc, 0.0, d[:], ALU.max, ALU.add).then_inc(out_done, 1)
                one.leave(CHUNKS)


STATES = 16


def scan(t, u, rate, coef, bc, direct, gain, y, bilinear):
    nc = t.nc
    parts, groups = u.shape[0], u.shape[1]
    jobs = STATES * groups
    SLOTS = 4
    with ExitStack() as st:
        thirds = t.sbuf("thirds", [6 * STATES, TOKENS], st, BF16)
        select = t.sbuf("select", [6 * STATES, 2 * STATES], st, BF16)
        with ExitStack() as inner:
            rest = t.sbuf("rest", [2 * STATES, TOKENS], inner)
            part = t.sbuf("part", [2 * STATES, TOKENS], inner, BF16)
            step = t.sem("step")
            with t.block() as block:
                @block.vector
                def _(dve):
                    one = Steps(dve, step)
                    nc.vector.tensor_copy(select[:], t.w["select"][:])
                    one(nc.vector.tensor_copy(thirds[0:2 * STATES, :], bc[0:2 * STATES, :]))
                    one(nc.vector.tensor_tensor(rest[:], bc[0:2 * STATES, :], thirds[0:2 * STATES, :], ALU.subtract))
                    one(nc.vector.tensor_copy(part[:], rest[:]))
                    nc.vector.tensor_copy(thirds[2 * STATES:4 * STATES, :], part[:])
                    one(nc.vector.tensor_tensor(rest[:], rest[:], part[:], ALU.subtract))
                    nc.vector.tensor_copy(thirds[4 * STATES:6 * STATES, :], rest[:])
        den_done, r_done, a_done, w1_done = t.sem("den_done"), t.sem("r_done"), t.sem("a_done"), t.sem("w1_done")
        w2_done, s_done, g_done, summed = t.sem("w2_done"), t.sem("s_done"), t.sem("g_done"), t.sem("summed")
        spread, y_done, a_zero = t.sem("spread"), t.sem("y_done"), t.sem("a_zero")
        a = t.sbuf("a", [parts, SLOTS, CHUNK // SEQ, SEQ], st)
        w2, s, g_ = (t.sbuf(n, [parts, SLOTS, CHUNK], st) for n in ("w2", "s", "g"))
        if bilinear:
            den, r, w1 = (t.sbuf(n, [parts, SLOTS, CHUNK], st) for n in ("den", "r", "w1"))
        bankB, bankC, acc = t.bank[0:2], t.bank[2:4], t.bank[4:4 + groups]
        ident = t.w["ident"]

        with t.block() as block:
            @block.tensor
            def _(pe):
                pe.sem_inc(summed, SLOTS)
                with pe.Fori(0, CHUNKS) as c:
                    at = bass.ds(CHUNK * c, CHUNK)

                    def sum_states(j):
                        n, g = divmod(j, groups)
                        if j == 0:
                            pe.wait_ge(y_done, c + 1)
                        pe.wait_ge(g_done, c * jobs + j + 1 + SLOTS)
                        nc.tensor.matmul(acc[g][0:parts, 0:CHUNK], ident[0:parts, 0:parts], g_[:, j % SLOTS, :],
                                         start=(n == 0), stop=(n == STATES - 1)).then_inc(summed, 1)

                    for n in range(STATES):
                        pe.wait_ge(g_done, c * jobs + (n - 1) * groups + SLOTS)
                        pe.sem_inc(t.passed, 1)
                        for bank, row in ((bankB[n % 2], n), (bankC[n % 2], STATES + n)):
                            last = nc.tensor.matmul(bank[0:parts, 0:CHUNK],
                                                    select[:, row:row + 1].to_broadcast([6 * STATES, parts]),
                                                    thirds[:, at], start=True, stop=True)
                        last.then_inc(spread, 1)
                        if n:
                            for g in range(groups):
                                sum_states((n - 1) * groups + g)
                    for g in range(groups):
                        sum_states((STATES - 1) * groups + g)

            @block.scalar
            def _(act):
                act.wait_ge(a_zero, 1)
                for sem in (den_done, r_done, a_done):
                    act.sem_inc(sem, SLOTS)
                nc.scalar.preload_act_table_set("natural_log_exp_and_others")
                with act.Fori(0, CHUNKS) as c:
                    at = bass.ds(CHUNK * c, CHUNK)

                    def logarithm(j):
                        n, g = divmod(j, groups)
                        act.wait_ge(r_done, c * jobs + j + 1)
                        act.sem_inc(t.passed, 1)
                        nc.scalar.activation(den[:, j % SLOTS, :], rate[:, g, at], ACT.Ln,
                                             scale=coef[:, g, n:n + 1], bias=1.0).then_inc(den_done, 1)

                    def invert(j):
                        act.wait_ge(den_done, c * jobs + j + 1 + SLOTS)
                        act.wait_ge(a_done, c * jobs + j + 1)
                        act.wait_ge(w1_done, c * jobs + j + 1)
                        nc.scalar.activation(r[:, j % SLOTS, :], den[:, j % SLOTS, :], ACT.Exp, scale=-1.0).then_inc(r_done, 1)

                    def decay(j):
                        n, g = divmod(j, groups)
                        act.wait_ge(s_done, c * jobs + j + 1)
                        rest = a[:, j % SLOTS, :, 1:SEQ]
                        if bilinear:
                            act.wait_ge(r_done, c * jobs + j + 1 + SLOTS)
                            nc.scalar.activation(rest, r[:, j % SLOTS, :].rearrange("p (b t) -> p b t", t=SEQ)[:, :, 1:SEQ],
                                                 ACT.Identity, scale=2.0, bias=t.w["minus_one"][0:parts, :]).then_inc(a_done, 1)
                        else:
                            act.sem_inc(t.passed, 1)
                            nc.scalar.activation(rest, rate[:, g, at].rearrange("p (b t) -> p b t", t=SEQ)[:, :, 1:SEQ],
                                                 ACT.Exp, scale=coef[:, g, n:n + 1]).then_inc(a_done, 1)

                    if bilinear:
                        for j in range(jobs + 2):
                            if j < jobs:
                                logarithm(j)
                            if 0 < j <= jobs:
                                invert(j - 1)
                            if j >= 2:
                                decay(j - 2)
                    else:
                        for j in range(jobs):
                            decay(j)

            @block.gpsimd
            def _(pool):
                if bilinear:
                    pool.sem_inc(w1_done, SLOTS)
                    with pool.Fori(0, CHUNKS) as c:
                        at = bass.ds(CHUNK * c, CHUNK)
                        for j in range(jobs):
                            pool.wait_ge(r_done, c * jobs + j + 1 + SLOTS)
                            pool.wait_ge(w2_done, c * jobs + j + 1)
                            pool.sem_inc(t.passed, 1)
                            nc.gpsimd.tensor_tensor(w1[:, j % SLOTS, :], u[:, j % groups, at], r[:, j % SLOTS, :],
                                                    ALU.mult).then_inc(w1_done, 1)

            @block.vector
            def _(dve):
                nc.vector.memset(a[:], 0.0).then_inc(a_zero, 1)
                for sem in (w2_done, s_done, g_done):
                    dve.sem_inc(sem, SLOTS)
                dve.sem_inc(y_done, 1)
                with dve.Fori(0, CHUNKS) as c:
                    at = bass.ds(CHUNK * c, CHUNK)

                    def weigh(j):
                        dve.wait_ge(summed, c * jobs + j + 1)
                        if bilinear:
                            dve.wait_ge(w1_done, c * jobs + j + 1 + SLOTS)
                        n, g = divmod(j, groups)
                        dve.wait_ge(spread, c * STATES + n + 1)
                        src = w1[:, j % SLOTS, :] if bilinear else u[:, g, at]
                        nc.vector.tensor_tensor(w2[:, j % SLOTS, :], src, bankB[n % 2][0:parts, 0:CHUNK],
                                                ALU.mult).then_inc(w2_done, 1)

                    def recur(j):
                        dve.wait_ge(w2_done, c * jobs + j + 1 + SLOTS)
                        dve.wait_ge(a_done, c * jobs + j + 1 + SLOTS)
                        nc.vector.tensor_tensor_scan(s[:, j % SLOTS, :], a[:, j % SLOTS, :, :].rearrange("p b t -> p (b t)"),
                                                     w2[:, j % SLOTS, :], 0.0, ALU.mult, ALU.add).then_inc(s_done, 1)

                    def read(j):
                        dve.wait_ge(s_done, c * jobs + j + 1 + SLOTS)
                        nc.vector.tensor_tensor(g_[:, j % SLOTS, :], s[:, j % SLOTS, :],
                                                bankC[(j // groups) % 2][0:parts, 0:CHUNK], ALU.mult).then_inc(g_done, 1)

                    for j in range(jobs):
                        weigh(j)
                        if j:
                            read(j - 1)
                        recur(j)
                    read(jobs - 1)
                    dve.wait_ge(summed, c * jobs + jobs + SLOTS)
                    for g in range(groups):
                        last = nc.vector.scalar_tensor_tensor(y[:, g, at], direct[0:parts, g, at], gain[0:parts, g:g + 1],
                                                              acc[g][0:parts, 0:CHUNK], ALU.mult, ALU.add)
                    last.then_inc(y_done, 1)


def add_back(t, y, dst, weights=None):
    nc = t.nc
    parts, groups = y.shape[0], y.shape[1]
    with ExitStack() as st:
        ys = t.sbuf("ys", [parts, 2, groups, TILE], st)
        staged, turned, added = t.sem("staged"), t.sem("turned"), t.sem("added")
        with t.block() as block:
            @block.scalar
            def _(act):
                with act.Fori(0, TILES // 2) as i:
                    for v in range(2):
                        act.wait_ge(turned, 2 * i + v + 1)
                        act.sem_inc(t.passed, 1)
                        nc.scalar.activation(ys[:, v], y[:, :, bass.ds(TILE * (2 * i + v), TILE)],
                                             ACT.Identity).then_inc(staged, 1)

            @block.tensor
            def _(pe):
                pe.sem_inc(turned, 2)
                with pe.Fori(0, TILES // 2) as i:
                    for v in range(2):
                        pe.wait_ge(staged, 2 * i + v + 1)
                        pe.wait_ge(added, 2 * i + v + 1)
                        for g in range(groups):
                            if weights is None:
                                last = nc.tensor.transpose(t.bank[v][0:TILE, parts * g:parts * (g + 1)], ys[:, v, g, :],
                                                           t.w["ident"][0:parts, 0:parts])
                            else:
                                last = nc.tensor.matmul(t.bank[v][0:TILE, 0:DIM], ys[:, v, g, :], weights(g, i),
                                                        start=(g == 0), stop=(g == groups - 1))
                        last.then_inc(turned, 1)

            @block.vector
            def _(dve):
                dve.sem_inc(added, 2)
                with dve.Fori(0, TILES // 2) as i:
                    for v in range(2):
                        dve.wait_ge(turned, 2 * i + v + 3)
                        tile = dst[:, bass.ds(2 * i + v, 1), :]
                        nc.vector.tensor_tensor(tile, tile, t.bank[v][0:TILE, 0:DIM].unsqueeze(1), ALU.add).then_inc(added, 1)


CLAMP_LO, CLAMP_HI = 0.0001, 10.0
CENTRE, REACH = (CLAMP_HI + CLAMP_LO) / 2.0, (CLAMP_HI - CLAMP_LO) / 2.0
RANK = 48


def layer0_mixer(t):
    nc, w = t.nc, t.w
    normalise(t, t.h, 1e-5)
    with ExitStack() as st:
        bc = t.sbuf("bc", [2 * STATES, TOKENS], st)
        rate = t.sbuf("rate", [HALF, 2, TOKENS], st)
        u = t.sbuf("u", [HALF, 2, TOKENS], st)
        coef = t.sbuf("coef", [HALF, 2, STATES], st)
        low = t.sbuf("low", [RANK, TOKENS], st)
        mult, low_done, up, biased, coef_done = t.sem("mult"), t.sem("low_done"), t.sem("up"), t.sem("biased"), t.sem("coef_done")
        with t.block() as block:
            @block.tensor
            def _(pe):
                pe.sem_inc(low_done, 1)
                pe.sem_inc(biased, 1)
                with pe.Fori(0, CHUNKS) as c:
                    at = bass.ds(CHUNK * c, CHUNK)
                    pe.wait_ge(low_done, 2 * c + 1)
                    for k in range(2):
                        nc.tensor.matmul(t.bank[0][0:2 * STATES, 0:CHUNK], w["L0_W_bc"][:, k, :], t.xT[0:HALF, k, at],
                                         start=(k == 0), stop=(k == 1))
                    for k in range(2):
                        last = nc.tensor.matmul(t.bank[1][0:RANK, 0:CHUNK], w["L0_W_dt"][:, k, :], t.xT[0:HALF, k, at],
                                                start=(k == 0), stop=(k == 1))
                    last.then_inc(mult, 1)
                    pe.wait_ge(low_done, 2 * c + 3)
                    pe.wait_ge(biased, 2 * c + 1)
                    for k in range(2):
                        last = nc.tensor.matmul(t.bank[2 + k][0:HALF, 0:CHUNK], w["L0_W_dtp"][:, HALF * k:HALF * (k + 1)],
                                                low[:, at], start=True, stop=True)
                    last.then_inc(up, 1)

            @block.scalar
            def _(act):
                act.sem_inc(t.passed, 1)
                nc.scalar.activation(coef[:], w["L0_A_log"][:], ACT.Exp).then_inc(coef_done, 1)
                with act.Fori(0, CHUNKS) as c:
                    at = bass.ds(CHUNK * c, CHUNK)
                    act.wait_ge(mult, c + 1)
                    act.sem_inc(t.passed, 1)
                    nc.scalar.activation(bc[:, at], t.bank[0][0:2 * STATES, 0:CHUNK], ACT.Identity).then_inc(low_done, 1)
                    act.sem_inc(t.passed, 1)
                    nc.scalar.activation(low[:, at], t.bank[1][0:RANK, 0:CHUNK], ACT.Identity).then_inc(low_done, 1)

            @block.vector
            def _(dve):
                dve.wait_ge(coef_done, 1)
                nc.vector.tensor_scalar(coef[:], coef[:], 0.5, None, ALU.mult)
                with dve.Fori(0, CHUNKS) as c:
                    at = bass.ds(CHUNK * c, CHUNK)
                    dve.wait_ge(up, c + 1)
                    for k in range(2):
                        nc.vector.tensor_scalar(rate[:, k, at], t.bank[2 + k][0:HALF, 0:CHUNK],
                                                w["L0_b_dt"][:, k:k + 1], None, ALU.add).then_inc(biased, 1)
        softplus(t, rate)
        with ExitStack() as inner:
            sq = t.sbuf("sq", [HALF, 2, TOKENS], inner)
            rms = t.sbuf("rms", [HALF, 2, CHUNK], inner)
            squared, meant, eps_done, root, inv = t.sem("squared"), t.sem("meant"), t.sem("eps_done"), t.sem("root"), t.sem("inv")
            scaled, tanh_done, clamped, rooted, summed = t.sem("scaled"), t.sem("tanh_done"), t.sem("clamped"), t.sem("rooted"), t.sem("summed")
            with t.block() as block:
                @block.scalar
                def _(act):
                    nc.scalar.preload_act_table(ACT.Sqrt)
                    with act.Fori(0, CHUNKS) as c:
                        at = bass.ds(CHUNK * c, CHUNK)
                        act.sem_inc(t.passed, 1)
                        nc.scalar.activation(sq[:, :, at], rate[:, :, at], ACT.Square).then_inc(squared, 1)
                        act.wait_ge(eps_done, c + 1)
                        nc.scalar.activation(rms[:, 1, :], rms[:, 0, :], ACT.Sqrt).then_inc(root, 1)
                    act.wait_ge(scaled, 2 * CHUNKS)
                    nc.scalar.activation(sq[:], rate[:], ACT.Tanh, scale=1.0 / REACH,
                                         bias=w["clamp"][0:HALF, :]).then_inc(tanh_done, 1)
                    act.wait_ge(clamped, 1)
                    nc.scalar.activation(sq[:], rate[:], ACT.Sqrt).then_inc(rooted, 1)

                @block.tensor
                def _(pe):
                    with pe.Fori(0, CHUNKS) as c:
                        at = bass.ds(CHUNK * c, CHUNK)
                        pe.wait_ge(squared, c + 1)
                        for k in range(2):
                            last = nc.tensor.matmul(t.bank[0][0:HALF, 0:CHUNK], w["mean"][:], sq[:, k, at],
                                                    start=(k == 0), stop=(k == 1))
                        last.then_inc(meant, 1)

                @block.vector
                def _(dve):
                    for k in range(2):
                        xk = t.xT[0:HALF, k, 0:TOKENS].rearrange("p (b t) -> p b t", t=SEQ)
                        uk = u[:, k, :].rearrange("p (b t) -> p b t", t=SEQ)
                        nc.vector.tensor_tensor(uk[:, :, 1:SEQ], xk[:, :, 1:SEQ], xk[:, :, 0:SEQ - 1], ALU.add).then_inc(summed, 1)
                        nc.vector.tensor_copy(uk[:, :, 0:1], xk[:, :, 0:1]).then_inc(summed, 1)
                    with dve.Fori(0, CHUNKS) as c:
                        at = bass.ds(CHUNK * c, CHUNK)
                        dve.wait_ge(meant, c + 1)
                        nc.vector.tensor_scalar(rms[:, 0, :], t.bank[0][0:HALF, 0:CHUNK], 1e-6, None, ALU.add).then_inc(eps_done, 1)
                        dve.wait_ge(root, c + 1)
                        nc.vector.reciprocal(rms[:, 1, :], rms[:, 1, :]).then_inc(inv, 1)
                        dve.wait_ge(inv, c + 1)
                        for k in range(2):
                            nc.vector.scalar_tensor_tensor(rate[:, k, at], rate[:, k, at], w["L0_rms"][:, k:k + 1],
                                                           rms[:, 1, :], ALU.mult, ALU.mult).then_inc(scaled, 1)
                        dve.wait_ge(scaled, 2 * c + 2)
                    dve.wait_ge(tanh_done, 1)
                    nc.vector.tensor_scalar(rate[:], sq[:], REACH, CENTRE, ALU.mult, ALU.add).then_inc(clamped, 1)
                    dve.wait_ge(rooted, 1)
                    dve.wait_ge(summed, 4)
                    nc.vector.scalar_tensor_tensor(flat(u[:]), flat(u[:]), 0.5, flat(sq[:]), ALU.mult, ALU.mult)
        y = rate
        scan(t, u, rate, coef, bc, t.xT, w["L0_D"], y, bilinear=True)
        add_back(t, y, t.h)

def route(t, lhs, gate, experts, picks, masks=None, weights=None, total=None, probs=None):
    nc = t.nc
    size = [TILE, TILES, experts]
    with ExitStack() as st:
        logits, ex, eq, chosen = (t.sbuf(n, size, st) for n in ("logits", "ex", "eq", "chosen"))
        top, best = t.sbuf("top", [TILE, TILES], st), t.sbuf("best", [TILE, TILES], st)
        own = t.sbuf("own", size, st)
        multiplied, shifted, exp_done, step = t.sem("multiplied"), t.sem("shifted"), t.sem("exp_done"), t.sem("step")
        spread = lambda v: v[:].unsqueeze(2).to_broadcast(size)
        first = t.w["first"][0:TILE, 0:experts].unsqueeze(1).to_broadcast(size)
        with t.block() as block:
            @block.tensor
            def _(pe):
                for i in range(TILES):
                    for k in range(len(gate)):
                        last = nc.tensor.matmul(t.bank[0][0:TILE, experts * i:experts * (i + 1)], lhs(i, k), gate[k],
                                                start=(k == 0), stop=(k == len(gate) - 1))
                last.then_inc(multiplied, 1)

            @block.scalar
            def _(act):
                act.wait_ge(shifted, 1)
                nc.scalar.activation(ex[:], own[:], ACT.Exp).then_inc(exp_done, 1)

            @block.vector
            def _(dve):
                one = Steps(dve, step)
                dve.wait_ge(multiplied, 1)
                one(nc.vector.tensor_copy(flat(logits[:]), t.bank[0][0:TILE, 0:TILES * experts]))
                one(nc.vector.tensor_reduce(top[:], logits[:], AX.X, ALU.max))
                nc.vector.tensor_tensor(own[:], logits[:], spread(top), ALU.subtract).then_inc(shifted, 1)
                for j in range(picks):
                    if j:
                        one(nc.vector.scalar_tensor_tensor(flat(logits[:]), flat(mask[:]), MASKED, flat(logits[:]), ALU.mult, ALU.add))
                        one(nc.vector.tensor_reduce(top[:], logits[:], AX.X, ALU.max))
                    mask = masks[j] if masks else (chosen if j == 0 else eq)
                    one(nc.vector.tensor_tensor(eq[:], logits[:], spread(top), ALU.is_equal))
                    one(nc.vector.tensor_tensor(eq[:], eq[:], first, ALU.mult))
                    one(nc.vector.tensor_reduce(best[:], eq[:], AX.X, ALU.max))
                    one(nc.vector.tensor_tensor(mask[:], eq[:], spread(best), ALU.is_equal))
                    if weights is not None and masks and j == 0:
                        one(nc.vector.tensor_copy(chosen[:], mask[:]))
                    elif weights is not None and j:
                        one(nc.vector.tensor_tensor(chosen[:], chosen[:], mask[:], ALU.add))
                dve.wait_ge(exp_done, 1)
                if total is not None:
                    one(nc.vector.tensor_reduce(best[:], ex[:], AX.X, ALU.add))
                    one(nc.vector.reciprocal(total[:], best[:]))
                if probs is not None:
                    one(nc.vector.tensor_tensor(probs[:], ex[:], spread(total), ALU.mult))
                if weights is not None:
                    one(nc.vector.tensor_tensor(ex[:], ex[:], chosen[:], ALU.mult))
                    one(nc.vector.tensor_reduce(best[:], ex[:], AX.X, ALU.add))
                    one(nc.vector.reciprocal(top[:], best[:]))
                    one(nc.vector.tensor_tensor(weights[:], ex[:], spread(top), ALU.mult))


def turn(t, src, dst):
    nc = t.nc
    n = src.shape[2]
    turned = t.sem("turned")
    with t.block() as block:
        @block.tensor
        def _(pe):
            for i in range(TILES):
                nc.tensor.transpose(t.bank[i // 4][0:n, TILE * (i % 4):TILE * (i % 4 + 1)], src[:, i, :],
                                    t.w["ident"][0:TILE, 0:TILE]).then_inc(turned, 1)

        @block.scalar
        def _(act):
            for c in range(CHUNKS):
                act.wait_ge(turned, 4 * c + 4)
                nc.scalar.activation(dst[:, CHUNK * c:CHUNK * (c + 1)], t.bank[c][0:n, 0:CHUNK], ACT.Identity)


L0_CODE, L0_EXPERTS = 64, 8
L0_GROUPS = L0_CODE * L0_EXPERTS // 128


def layer0_ffn(t):
    nc, w = t.nc, t.w
    normalise(t, t.h, 1e-5)
    with ExitStack() as st:
        code = t.sbuf("code", [L0_CODE + 1, TOKENS], st)
        mask = t.sbuf("mask", [TILE, TILES, L0_EXPERTS], st)
        prob = t.sbuf("prob", [TILE, TILES], st)
        gate = t.sbuf("gate", [L0_EXPERTS, 1, TOKENS], st)
        up = t.sbuf("up", [128, L0_GROUPS, CHUNK], st)
        picked = t.sbuf("picked", [128, L0_GROUPS, CHUNK], st)
        ones_done, encoded, code_done = t.sem("ones_done"), t.sem("encoded"), t.sem("code_done")
        with t.block() as block:
            @block.vector
            def _(dve):
                nc.vector.memset(code[L0_CODE:L0_CODE + 1, :], 1.0).then_inc(ones_done, 1)

            @block.tensor
            def _(pe):
                for c in range(CHUNKS):
                    at = slice(CHUNK * c, CHUNK * (c + 1))
                    nc.tensor.matmul(t.bank[c][0:L0_CODE, 0:CHUNK], w["L0_enc"][:, 0, :], t.xT[:, 0, at], start=True, stop=False)
                    nc.tensor.matmul(t.bank[c][0:L0_CODE, 0:CHUNK], w["L0_enc"][0:HALF, 1, :], t.xT[0:HALF, 1, at],
                                     start=False, stop=True).then_inc(encoded, 1)

            @block.scalar
            def _(act):
                for c in range(CHUNKS):
                    act.wait_ge(encoded, c + 1)
                    nc.scalar.activation(code[0:L0_CODE, CHUNK * c:CHUNK * (c + 1)], t.bank[c][0:L0_CODE, 0:CHUNK],
                                         ACT.Identity).then_inc(code_done, 1)
        route(t, lambda i, k: code[:, TILE * i:TILE * (i + 1)], [w["L0_switch"][:]], L0_EXPERTS, 1, masks=[mask], total=prob)
        masked = t.sem("masked")
        with t.block() as block:
            @block.vector
            def _(dve):
                nc.vector.tensor_tensor(mask[:], mask[:], prob[:].unsqueeze(2).to_broadcast([TILE, TILES, L0_EXPERTS]),
                                        ALU.mult).then_inc(masked, 1)
        turn(t, mask, gate[:, 0, :])
        up_done, act_done, spread, pick_done, down, added = (
            t.sem(n) for n in ("up_done", "act_done", "spread", "pick_done", "down", "added"))
        G = L0_GROUPS
        with t.block() as block:
            @block.tensor
            def _(pe):
                pe.sem_inc(down, 4)
                with pe.Fori(0, CHUNKS) as c:
                    at = bass.ds(CHUNK * c, CHUNK)
                    pe.wait_ge(act_done, c * G + G)
                    for m in range(G):
                        for k in range(2):
                            last = nc.tensor.matmul(t.bank[m][:, 0:CHUNK], w["L0_w1"][:, k, 128 * m:128 * (m + 1)],
                                                    t.xT[0:HALF, k, at], start=(k == 0), stop=(k == 1))
                        last.then_inc(up_done, 1)
                    for m in range(G):
                        pe.wait_ge(pick_done, c * G + m + 3)
                        pe.sem_inc(t.passed, 1)
                        nc.tensor.matmul(t.bank[4 + m % 2][:, 0:CHUNK], w["L0_pair"][:, m, :], gate[:, 0, at],
                                         start=True, stop=True).then_inc(spread, 1)
                    pe.wait_ge(pick_done, c * G + G + 4)
                    for j in range(4):
                        pe.wait_ge(added, 4 * c + j + 1)
                        for m in range(G):
                            last = nc.tensor.matmul(t.bank[6 + j % 2][0:TILE, 0:DIM], picked[:, m, TILE * j:TILE * (j + 1)],
                                                    w["L0_w2"][:, m, :], start=(m == 0), stop=(m == G - 1))
                        last.then_inc(down, 1)

            @block.scalar
            def _(act):
                act.sem_inc(act_done, G)
                nc.scalar.preload_act_table(ACT.Gelu)
                with act.Fori(0, CHUNKS) as c:
                    for m in range(G):
                        act.wait_ge(up_done, c * G + m + 1)
                        act.wait_ge(pick_done, c * G + m + 1)
                        nc.scalar.activation(up[:, m, :], t.bank[m][:, 0:CHUNK], ACT.Gelu,
                                             bias=w["L0_b1"][:, m:m + 1]).then_inc(act_done, 1)

            @block.vector
            def _(dve):
                dve.sem_inc(pick_done, G)
                dve.sem_inc(added, 2)
                with dve.Fori(0, CHUNKS) as c:
                    dve.wait_ge(down, 4 * c + 4)
                    for m in range(G):
                        dve.wait_ge(act_done, c * G + m + 1 + G)
                        dve.wait_ge(spread, c * G + m + 1)
                        nc.vector.tensor_tensor(picked[:, m, :], up[:, m, :], t.bank[4 + m % 2][:, 0:CHUNK],
                                                ALU.mult).then_inc(pick_done, 1)
                    for j in range(4):
                        dve.wait_ge(down, 4 * c + j + 1 + 4)
                        tile = t.h[:, bass.ds(4 * c + j, 1), :]
                        nc.vector.tensor_tensor(tile, tile, t.bank[6 + j % 2][0:TILE, 0:DIM].unsqueeze(1), ALU.add).then_inc(added, 1)
        add_back(t, gate, t.h, lambda g, i: w["L0_b2"][:, g, :])


def layer1_mixer(t):
    nc, w = t.nc, t.w
    normalise(t, t.h, 1e-5)
    with ExitStack() as st:
        x = t.sbuf("xtile", [HALF + 1, 2, 2, TILE], st)
        qk = t.sbuf("qk", [HALF, 2, 4, TILE], st)
        v_ = t.sbuf("v", [TILE, 2, DIM], st)
        s = t.sbuf("scores", [TILE, 2, TILE], st)
        p = t.sbuf("probs", [TILE, 2, TILE], st)
        pT = t.sbuf("probsT", [TILE, 2, TILE], st)
        low, tot = t.sbuf("low", [TILE, 2], st), t.sbuf("tot", [TILE, 2], st)
        inv = t.sbuf("inv", [TILE, 2], st)
        staged, projected, qk_done, v_done, scored, masked, low_done, exp_done, turned, pT_done, out_done, inv_done, added = (
            t.sem(n) for n in ("staged", "projected", "qk_done", "v_done", "scored", "masked", "low_done", "exp_done",
                               "turned", "pT_done", "out_done", "inv_done", "added"))
        bankP, bankV, bankS = t.bank[0:2], t.bank[2:4], t.bank[4:6]
        with t.block() as block:
            @block.gpsimd
            def _(pool):
                with pool.Fori(0, TILES // 2) as i:
                    for u in range(2):
                        pool.wait_ge(projected, 2 * i + u + 1)
                        pool.sem_inc(t.passed, 1)
                        nc.gpsimd.tensor_copy(x[:, u], t.xT[:, :, bass.ds(TILE * (2 * i + u), TILE)]).then_inc(staged, 1)

            @block.tensor
            def _(pe):
                pe.sem_inc(projected, 2)
                with pe.Fori(0, TILES // 2) as i:
                    n = lambda u: 2 * i + u + 1
                    for u in range(2):
                        pe.wait_ge(staged, n(u))
                        pe.wait_ge(added, n(u))
                        for m in range(4):
                            nc.tensor.matmul(bankP[u][0:HALF, TILE * m:TILE * (m + 1)], w["L1_wqk"][:, 0, HALF * m:HALF * (m + 1)],
                                             x[:, u, 0, :], start=True, stop=False)
                            nc.tensor.matmul(bankP[u][0:HALF, TILE * m:TILE * (m + 1)], w["L1_wqk"][0:HALF, 1, HALF * m:HALF * (m + 1)],
                                             x[0:HALF, u, 1, :], start=False, stop=True)
                        nc.tensor.matmul(bankV[u][0:TILE, 0:DIM], x[:, u, 0, :], w["L1_wv"][:, 0, :], start=True, stop=False)
                        nc.tensor.matmul(bankV[u][0:TILE, 0:DIM], x[0:HALF, u, 1, :], w["L1_wv"][0:HALF, 1, :],
                                         start=False, stop=True).then_inc(projected, 1)
                    for u in range(2):
                        pe.wait_ge(qk_done, n(u))
                        for k in range(2):
                            last = nc.tensor.matmul(bankS[u][0:TILE, 0:TILE], qk[:, u, k, :], qk[:, u, 2 + k, :],
                                                    start=(k == 0), stop=(k == 1))
                        last.then_inc(scored, 1)
                    for u in range(2):
                        pe.wait_ge(exp_done, n(u))
                        nc.tensor.transpose(bankP[u][0:TILE, 0:TILE], p[:, u, :], w["ident"][0:TILE, 0:TILE]).then_inc(turned, 1)
                    for u in range(2):
                        pe.wait_ge(pT_done, n(u))
                        pe.wait_ge(v_done, n(u))
                        nc.tensor.matmul(bankS[u][0:TILE, TILE:TILE + DIM], pT[:, u, :], v_[:, u, :],
                                         start=True, stop=True).then_inc(out_done, 1)

            @block.scalar
            def _(act):
                nc.scalar.preload_act_table(ACT.Exp)
                with act.Fori(0, TILES // 2) as i:
                    n = lambda u: 2 * i + u + 1
                    for u in range(2):
                        act.wait_ge(projected, n(u) + 2)
                        nc.scalar.activation(qk[:, u], bankP[u][0:HALF, 0:4 * TILE].rearrange("p (m n) -> p m n", m=4),
                                             ACT.Identity).then_inc(qk_done, 1)
                    for u in range(2):
                        act.wait_ge(low_done, n(u))
                        nc.scalar.activation(p[:, u, :], s[:, u, :], ACT.Exp, bias=low[:, u:u + 1],
                                             accum_out=tot[:, u:u + 1]).then_inc(exp_done, 1)
                    for u in range(2):
                        act.wait_ge(turned, n(u))
                        nc.scalar.activation(pT[:, u, :], bankP[u][0:TILE, 0:TILE], ACT.Identity).then_inc(pT_done, 1)

            @block.vector
            def _(dve):
                dve.sem_inc(added, 2)
                with dve.Fori(0, TILES // 2) as i:
                    n = lambda u: 2 * i + u + 1
                    for u in range(2):
                        dve.wait_ge(projected, n(u) + 2)
                        nc.vector.tensor_copy(v_[:, u, :], bankV[u][0:TILE, 0:DIM]).then_inc(v_done, 1)
                    for u in range(2):
                        dve.wait_ge(scored, n(u))
                        nc.vector.scalar_tensor_tensor(s[:, u, :], bankS[u][0:TILE, 0:TILE], DIM ** -0.5,
                                                       w["mask"][:], ALU.mult, ALU.add).then_inc(masked, 1)
                    for u in range(2):
                        dve.wait_ge(masked, n(u))
                        nc.vector.tensor_reduce(low[:, u:u + 1], s[:, u, :], AX.X, ALU.max, negate=True).then_inc(low_done, 1)
                    for u in range(2):
                        dve.wait_ge(exp_done, n(u))
                        nc.vector.reciprocal(inv[:, u:u + 1], tot[:, u:u + 1]).then_inc(inv_done, 1)
                    for u in range(2):
                        dve.wait_ge(inv_done, n(u))
                        dve.wait_ge(out_done, n(u))
                        tile = t.h[:, bass.ds(2 * i + u, 1), :]
                        nc.vector.scalar_tensor_tensor(tile, bankS[u][0:TILE, TILE:TILE + DIM].unsqueeze(1), inv[:, u:u + 1],
                                                       tile, ALU.mult, ALU.add).then_inc(added, 1)


def heads_attention(t, wqkv, wproj, dst, unit):
    nc, w = t.nc, t.w
    GROUPS = HEADS // 4
    with ExitStack() as st:
        x = t.sbuf("xtile", [HALF + 1, 2, 2, TILE], st)
        wide = t.sbuf("wide", [TILE, 2, 2 * HEADS, 2 * HEAD], st)
        sq = t.sbuf("sq", [TILE, 2, 2 * HEADS * HEAD], st)
        norm = t.sbuf("norm", [TILE, 2, 3, 2 * HEADS], st)
        v_ = t.sbuf("v", [TILE, 2, DIM], st)
        qkT = t.sbuf("qkT", [128, 2, 2 * GROUPS, TILE], st)
        s = t.sbuf("scores", [TILE, 2, HEADS, TILE], st)
        pT = t.sbuf("probsT", [TILE, HEADS, TILE], st)
        red = t.sbuf("red", [TILE, 2, 3, HEADS], st)
        a = t.sbuf("a", [TILE, 2, DIM], st)
        aT = t.sbuf("aT", [HALF + 1, 2, 2, TILE], st)
        names = ("zeroed", "ones_done", "staged", "projected", "squared", "summed", "rooted", "q_done", "v_done", "turned", "qkT_done",
                 "scored", "masked", "max_done", "shifted", "exp_done", "probs_turned", "pT_done", "weighed",
                 "a_done", "a_turned", "aT_done", "out_done", "added", "step", "front_step")
        (zeroed, ones_done, staged, projected, squared, summed, rooted, q_done, v_done, turned, qkT_done, scored, masked, max_done,
         shifted, exp_done, probs_turned, pT_done, weighed, a_done, a_turned, aT_done, out_done, added, step, front_step) = (
            t.sem(n) for n in names)
        bankQ, bankV, bankK, bankO, bankS = t.bank[0], t.bank[1], t.bank[2], t.bank[3], t.bank[4:8]
        bankT = (bankQ, bankK)
        ident = w["ident"]
        with t.block() as block:
            @block.gpsimd
            def _(pool):
                nc.gpsimd.memset(wide[:], 0.0).then_inc(zeroed, 1)

                def stage(n, v):
                    nc.gpsimd.tensor_copy(x[:, v], t.xT[:, :, bass.ds(TILE * n, TILE)]).then_inc(staged, 1)

                pool.wait_ge(zeroed, 1)
                stage(0, 0)
                with pool.Fori(0, TILES // 2) as i:
                    for u in range(2):
                        n = 2 * i + u
                        pool.wait_ge(projected, n + 1)
                        pool.sem_inc(t.passed, 1)
                        stage(n + 1, 1 - u)
                        pool.wait_ge(max_done, n + 1)
                        nc.gpsimd.tensor_tensor(s[:, u], s[:, u], red[:, u, 0, :].unsqueeze(2).to_broadcast([TILE, HEADS, TILE]),
                                                ALU.subtract).then_inc(shifted, 1)

            @block.tensor
            def _(pe):
                pe.sem_inc(projected, 1)
                pe.wait_ge(zeroed, 1)
                pe.wait_ge(ones_done, 1)

                def project(v):
                    for bank, lo, hi in ((bankQ, 0, 2 * DIM), (bankV, 2 * DIM, 3 * DIM)):
                        nc.tensor.matmul(bank[0:TILE, 0:hi - lo], x[:, v, 0, :], wqkv[:, 0, lo:hi], start=True, stop=False)
                        last = nc.tensor.matmul(bank[0:TILE, 0:hi - lo], x[0:HALF, v, 1, :], wqkv[0:HALF, 1, lo:hi],
                                                start=False, stop=True)
                    last.then_inc(projected, 1)

                def turn_qk(v):
                    for g in range(2 * GROUPS):
                        last = nc.tensor.transpose(bankT[g // GROUPS][:, TILE * (g % GROUPS):TILE * (g % GROUPS + 1)],
                                                   wide[:, v, 4 * g:4 * g + 4, :].rearrange("p h e -> p (h e)"),
                                                   ident[0:TILE, 0:TILE])
                    last.then_inc(turned, 1)

                pe.wait_ge(staged, 1)
                project(0)
                pe.wait_ge(q_done, 1)
                turn_qk(0)
                with pe.Fori(0, TILES // 2) as i:
                    for u in range(2):
                        n = 2 * i + u
                        pe.wait_ge(qkT_done, n + 1)
                        pe.wait_ge(pT_done, 3 * n + 3)
                        for g in range(GROUPS):
                            for j in range(4):
                                rows = slice(32 * j, 32 * j + HEAD)
                                last = nc.tensor.matmul(bankS[j][0:TILE, TILE * g:TILE * (g + 1)], qkT[rows, u, g, :],
                                                        qkT[rows, u, GROUPS + g, :], start=True, stop=True)
                        last.then_inc(scored, 1)
                        pe.wait_ge(staged, n + 2)
                        pe.wait_ge(v_done, n + 1)
                        project(1 - u)
                        pe.wait_ge(exp_done, n + 1)
                        for g in range(GROUPS):
                            for j in range(4):
                                last = nc.tensor.transpose(bankS[g][0:TILE, TILE * j:TILE * (j + 1)], s[:, u, 4 * g + j, :],
                                                           ident[0:TILE, 0:TILE])
                            last.then_inc(probs_turned, 1)
                        pe.wait_ge(added, n + 1)
                        for g in range(GROUPS):
                            pe.wait_ge(pT_done, 3 * n + 3 + g + 1)
                            for j in range(4):
                                head = slice(HEAD * (4 * g + j), HEAD * (4 * g + j + 1))
                                last = nc.tensor.matmul(bankO[0:TILE, head], pT[:, 4 * g + j, :], v_[:, u, head], start=True, stop=True)
                        last.then_inc(weighed, 1)
                        pe.wait_ge(q_done, n + 2)
                        turn_qk(1 - u)
                        pe.wait_ge(a_done, n + 1)
                        for k in range(2):
                            last = nc.tensor.transpose(bankO[0:HALF, DIM + TILE * k:DIM + TILE * (k + 1)],
                                                       a[:, u, HALF * k:HALF * (k + 1)], ident[0:TILE, 0:TILE])
                        last.then_inc(a_turned, 1)
                        pe.wait_ge(aT_done, n + 1)
                        nc.tensor.matmul(bankO[0:TILE, 0:DIM], aT[:, u, 0, :], wproj[:, 0, :], start=True, stop=False)
                        nc.tensor.matmul(bankO[0:TILE, 0:DIM], aT[0:HALF, u, 1, :], wproj[0:HALF, 1, :],
                                         start=False, stop=True).then_inc(out_done, 1)

            @block.scalar
            def _(act):
                act.sem_inc(pT_done, 3)

                def square(n, v):
                    if unit:
                        act.wait_ge(projected, n + 2)
                        nc.scalar.activation(sq[:, v, :], bankQ[0:TILE, 0:2 * DIM], ACT.Square).then_inc(squared, 1)

                def root(n, v):
                    if unit:
                        act.wait_ge(summed, n + 1)
                        nc.scalar.activation(norm[:, v, 1, :], norm[:, v, 0, :], ACT.Sqrt).then_inc(rooted, 1)

                def take_qkT(n, v):
                    act.wait_ge(turned, n + 1)
                    for half in range(2):
                        last = nc.scalar.activation(qkT[:, v, GROUPS * half:GROUPS * (half + 1), :],
                                                    bankT[half][:, 0:GROUPS * TILE].rearrange("p (g n) -> p g n", g=GROUPS),
                                                    ACT.Identity)
                    last.then_inc(qkT_done, 1)

                square(0, 0)
                root(0, 0)
                take_qkT(0, 0)
                with act.Fori(0, TILES // 2) as i:
                    for u in range(2):
                        n = 2 * i + u
                        square(n + 1, 1 - u)
                        act.wait_ge(shifted, n + 1)
                        nc.scalar.activation(s[:, u], s[:, u], ACT.Exp).then_inc(exp_done, 1)
                        act.wait_ge(weighed, n + 1)
                        for g in range(GROUPS):
                            act.wait_ge(probs_turned, 3 * n + g + 1)
                            nc.scalar.activation(pT[:, 4 * g:4 * g + 4, :], bankS[g][0:TILE, 0:4 * TILE].rearrange("p (j n) -> p j n", j=4),
                                                 ACT.Identity).then_inc(pT_done, 1)
                        root(n + 1, 1 - u)
                        take_qkT(n + 1, 1 - u)
                        act.wait_ge(a_turned, n + 1)
                        nc.scalar.activation(aT[0:HALF, u], bankO[0:HALF, DIM:DIM + 2 * TILE].rearrange("p (k n) -> p k n", k=2),
                                             ACT.Identity).then_inc(aT_done, 1)

            @block.vector
            def _(dve):
                narrow = bankQ[0:TILE, 0:2 * DIM].rearrange("p (h e) -> p h e", e=HEAD)
                dve.sem_inc(added, 1)
                dve.sem_inc(weighed, 1)
                nc.vector.memset(aT[HALF:HALF + 1], 1.0).then_inc(ones_done, 1)
                dve.wait_ge(zeroed, 1)

                def lengths(n, v):
                    if unit:
                        dve.wait_ge(squared, n + 1)
                        nc.vector.tensor_reduce(norm[:, v, 2, :], sq[:, v, :].rearrange("p (h e) -> p h e", e=HEAD),
                                                AX.X, ALU.add).then_inc(front_step, 1)
                        dve.wait_ge(front_step, 3 * n + 1)
                        nc.vector.tensor_scalar(norm[:, v, 0, :], norm[:, v, 2, :], 1e-24, None, ALU.max).then_inc(summed, 1)

                def take_qkv(n, v):
                    if unit:
                        dve.wait_ge(rooted, n + 1)
                        nc.vector.reciprocal(norm[:, v, 2, :], norm[:, v, 1, :]).then_inc(front_step, 1)
                        dve.wait_ge(front_step, 3 * n + 2)
                        nc.vector.tensor_tensor(norm[:, v, 2, 0:HEADS], norm[:, v, 2, 0:HEADS], w["L2_scale"][:],
                                                ALU.mult).then_inc(front_step, 1)
                        dve.wait_ge(front_step, 3 * n + 3)
                        nc.vector.tensor_tensor(wide[:, v, :, 0:HEAD], narrow,
                                                norm[:, v, 2, :].unsqueeze(2).to_broadcast([TILE, 2 * HEADS, HEAD]),
                                                ALU.mult).then_inc(q_done, 1)
                    else:
                        dve.wait_ge(projected, n + 2)
                        nc.vector.tensor_copy(wide[:, v, :, 0:HEAD], narrow).then_inc(q_done, 1)
                    nc.vector.tensor_copy(v_[:, v, :], bankV[0:TILE, 0:DIM]).then_inc(v_done, 1)

                lengths(0, 0)
                take_qkv(0, 0)
                with dve.Fori(0, TILES // 2) as i:
                    for u in range(2):
                        n = 2 * i + u
                        dve.wait_ge(scored, n + 1)
                        for j in range(4):
                            nc.vector.scalar_tensor_tensor(
                                s[:, u].rearrange("p (g j) n -> p j g n", j=4)[:, j], bankS[j][0:TILE, 0:GROUPS * TILE]
                                .rearrange("p (g n) -> p g n", g=GROUPS), 1.0 if unit else HEAD ** -0.5,
                                w["mask"][:].unsqueeze(1).to_broadcast([TILE, GROUPS, TILE]), ALU.mult, ALU.add).then_inc(masked, 1)
                        dve.wait_ge(masked, 4 * n + 4)
                        nc.vector.tensor_reduce(red[:, u, 0, :], s[:, u], AX.X, ALU.max).then_inc(max_done, 1)
                        lengths(n + 1, 1 - u)
                        dve.wait_ge(exp_done, n + 1)
                        nc.vector.tensor_reduce(red[:, u, 1, :], s[:, u], AX.X, ALU.add).then_inc(step, 1)
                        dve.wait_ge(step, 2 * n + 1)
                        nc.vector.reciprocal(red[:, u, 2, :], red[:, u, 1, :]).then_inc(step, 1)
                        take_qkv(n + 1, 1 - u)
                        dve.wait_ge(step, 2 * n + 2)
                        dve.wait_ge(weighed, n + 2)
                        nc.vector.tensor_tensor(a[:, u, :].rearrange("p (h e) -> p h e", e=HEAD),
                                                bankO[0:TILE, 0:DIM].rearrange("p (h e) -> p h e", e=HEAD),
                                                red[:, u, 2, :].unsqueeze(2).to_broadcast([TILE, HEADS, HEAD]),
                                                ALU.mult).then_inc(a_done, 1)
                        dve.wait_ge(out_done, n + 1)
                        tile = dst[:, bass.ds(n, 1), :]
                        nc.vector.tensor_tensor(tile, tile, bankO[0:TILE, 0:DIM].unsqueeze(1), ALU.add).then_inc(added, 1)

BLOCK = 256
SUBS = BLOCK // 128


def block_count(experts, picks):
    return (TOKENS * picks + experts * (BLOCK - 1)) // BLOCK


MOST_BLOCKS = block_count(16, 4)
MOST_OF_ONE = -(-TOKENS // BLOCK)


def clear_slots(t):
    nc = t.nc
    t.cleared = t.sem("cleared", lasting=True)
    zeros_done = t.sem("zeros_done")
    with t.block() as block:
        @block.gpsimd
        def _(pool):
            nc.gpsimd.memset(t.zeros[:], 0.0).then_inc(zeros_done, 1)

        @block.sync
        def _(sp):
            sp.wait_ge(zeros_done, 1)
            sp.dma_start(t.slots.rearrange("a s p d -> p (a s) d"),
                         t.zeros[:].unsqueeze(1).to_broadcast([128, (MOST_BLOCKS + 1) * SUBS, DIM])).then_inc(t.cleared, 16)


def place(t, masks, share, experts, rows, gate, slot, up_row, down_row):
    nc, w = t.nc, t.w
    K, E, B = len(masks), experts, block_count(experts, len(masks)) + 1
    with ExitStack() as st:
        taken = t.sbuf("taken_by", [TILE, TILES, E], st)
        counts, upto, keep = (t.sbuf(n, [128, E, TILES], st) for n in ("counts", "upto", "keep"))
        more = t.sbuf("more", [128, E, MOST_OF_ONE], st)
        blocks, end, ones = (t.sbuf(n, [128, E], st) for n in ("blocks", "end", "ones"))
        over = t.sbuf("over", [128, B, E], st)
        owner = t.sbuf("owner", [128, B], st)
        part = t.sbuf("part", [TILE, TILES, E], st)
        slot_f = t.sbuf("slot_f", [TILE, TILES, K], st)
        taken_done, ranked, step = t.sem("taken_done"), t.sem("ranked"), t.sem("step")
        rank = t.bank[0][0:TILE, 0:TILES * E]
        total = t.bank[1][:, 0:TILES * E]
        with t.block() as block:
            @block.tensor
            def _(pe):
                pe.wait_ge(taken_done, 1)
                nc.tensor.matmul(rank, w["before"][:], flat(taken[:]), start=True, stop=True)
                nc.tensor.matmul(total, w["all"][:], flat(taken[:]), start=True, stop=True).then_inc(ranked, 1)

            @block.vector
            def _(dve):
                one = Steps(dve, step)
                for j in range(1, K):
                    one(nc.vector.tensor_tensor(taken[:], taken[:] if j > 1 else masks[0][:], masks[j][:], ALU.add))
                nc.vector.memset(ones[:], 1.0).then_inc(taken_done, 1)
                one(nc.vector.memset(keep[:], 1.0))
                one(nc.vector.memset(keep[:, :, 0:1], 0.0))
                dve.wait_ge(ranked, 1)
                one(nc.vector.tensor_copy(counts[:], total.rearrange("p (i e) -> p e i", e=E)))
                one(nc.vector.tensor_tensor_scan(flat(upto[:]), flat(keep[:]), flat(counts[:]), 0.0, ALU.mult, ALU.add))
                one(nc.vector.tensor_tensor(more[:], upto[:, :, TILES - 1:TILES].to_broadcast([128, E, MOST_OF_ONE]),
                                            w["full"][:].unsqueeze(1).to_broadcast([128, E, MOST_OF_ONE]), ALU.is_gt))
                one(nc.vector.tensor_reduce(blocks[:], more[:], AX.X, ALU.add))
                one(nc.vector.tensor_tensor_scan(end[:], ones[:], blocks[:], 0.0, ALU.mult, ALU.add))
                one(nc.vector.tensor_tensor(over[:], w["block"][:, 0:B].unsqueeze(2).to_broadcast([128, B, E]),
                                            end[:].unsqueeze(1).to_broadcast([128, B, E]), ALU.is_ge))
                one(nc.vector.tensor_reduce(owner[:], over[:], AX.X, ALU.add))
                one(nc.vector.tensor_scalar(owner[:], owner[:], float(E - 1), None, ALU.min))
                nc.vector.tensor_scalar(up_row[:], owner[:], float(rows), w["lane"][:], ALU.mult, ALU.add)
                nc.vector.tensor_scalar(down_row[:], owner[:], 128.0, w["lane"][:], ALU.mult, ALU.add)
                one(nc.vector.tensor_tensor(blocks[:], end[:], blocks[:], ALU.subtract))
                one(nc.vector.tensor_tensor(upto[:], upto[:], counts[:], ALU.subtract))
                one(nc.vector.scalar_tensor_tensor(upto[:], blocks[:].unsqueeze(2).to_broadcast([128, E, TILES]), float(BLOCK),
                                                   upto[:], ALU.mult, ALU.add))
                one(nc.vector.tensor_tensor(taken[:], upto[0:TILE].rearrange("p e i -> p i e"),
                                            rank.rearrange("p (i e) -> p i e", e=E), ALU.add))
                for j in range(K):
                    one(nc.vector.tensor_tensor(part[:], taken[:], masks[j][:], ALU.mult))
                    one(nc.vector.tensor_reduce(slot_f[:, :, j], part[:], AX.X, ALU.add))
                    one(nc.vector.tensor_tensor(part[:], share[:], masks[j][:], ALU.mult))
                    one(nc.vector.tensor_reduce(gate[:, :, j], part[:], AX.X, ALU.add))
                nc.vector.tensor_copy(slot[:], slot_f[:])


def experts(t, name, src, dst, masks, share, count, rows, func, gated, gain=None, bias=None, expert_gain=None):
    nc, w, args = t.nc, t.w, t.args
    K, B, M = len(masks), block_count(count, len(masks)), HIDDEN // 128
    ups = [args[f"{name}_up"]] + ([args[f"{name}_gate"]] if gated else [])
    ups = [a.rearrange("e p k m -> (e p) (k m)") for a in ups]
    downs = args[f"{name}_down"].rearrange("e p m d -> (e p) (m d)")
    N = len(ups)
    LOADS = N + 1
    U32 = mybir.dt.uint32
    with ExitStack() as st:
        gate = t.sbuf("gate_of", [TILE, TILES, K], st)
        slot = t.sbuf("slot_of", [TILE, TILES, K], st, U32)
        up_row, down_row = (t.sbuf(n, [128, B + 1], st, U32) for n in ("up_row", "down_row"))
        place(t, masks, share, count, rows, gate, slot, up_row, down_row)
        wu = t.sbuf("wu", [rows, 2, N, 2 * HIDDEN], st)
        wd = t.sbuf("wd", [128, 2, M * DIM], st)
        row = t.sbuf("row", [128, 2, 2], st, U32)
        own_gain = t.sbuf("own_gain", [HALF, 2, 2], st)
        tokens = t.sbuf("tokens", [TILE, 2, DIM], st)
        to = t.sbuf("to", [TILE, 2, K], st, U32)
        x = t.sbuf("xblock", [128, 2, SUBS, DIM], st)
        xT = t.sbuf("xTblock", [HALF + 1, 2, 2, BLOCK], st)
        hid = t.sbuf("hid", [128, M, BLOCK], st)
        sa = t.sbuf("sa", [128, 2, BLOCK], st)
        y = t.sbuf("yblock", [128, 2, SUBS, DIM], st)
        bankU, bankX, bankY = t.bank[0:3], t.bank[3], (t.bank[4:6], t.bank[6:8])
        slots_flat = t.slots[0:B].rearrange("a s p d -> (a s p) d")
        results_flat = t.results[0:B].rearrange("a s p d -> (a s p) d")
        ones_done, row_ready, staged = t.sem("ones_done"), t.sem("row_ready"), t.sem("staged")
        loaded, used = [t.sem("loaded_even", lasting=True), t.sem("loaded_odd", lasting=True)], t.sem("used")
        gain_in = [t.sem("gain_in_even", lasting=True), t.sem("gain_in_odd", lasting=True)]
        sorted_ = [t.sem("sorted_even", lasting=True), t.sem("sorted_odd", lasting=True)]
        x_in, stored = [t.sem("x_in_even"), t.sem("x_in_odd")], [t.sem("stored_even"), t.sem("stored_odd")]
        turned, xT_done, up_done, silu_done, hid_done, down, y_done, y_free = (
            t.sem(n) for n in ("turned", "xT_done", "up_done", "silu_done", "hid_done", "down", "y_done", "y_free"))
        with t.block() as block:
            @block.gpsimd
            def _(pool):
                def load(b, v, n):
                    at = bass.ds(b, 1)
                    nc.gpsimd.tensor_copy(row[:, v, 0:1], up_row[:, at])
                    nc.gpsimd.tensor_copy(row[:, v, 1:2], down_row[:, at]).then_inc(row_ready, 1)
                    pool.wait_ge(row_ready, n)
                    pool.sem_inc(t.passed, 1)
                    for i, up in enumerate(ups):
                        nc.gpsimd.indirect_dma_start(wu[:, v, i, :], None, up, bass.IndirectOffsetOnAxis(row[0:rows, v, 0:1], 0)
                                                     ).then_inc(loaded[v], 16)
                    nc.gpsimd.indirect_dma_start(wd[:, v, :], None, downs, bass.IndirectOffsetOnAxis(row[:, v, 1:2], 0)
                                                 ).then_inc(loaded[v], 16)
                    if expert_gain is not None:
                        load_gain(v)

                def load_gain(v):
                    nc.gpsimd.indirect_dma_start(own_gain[:, v, :], None, expert_gain,
                                                 bass.IndirectOffsetOnAxis(row[0:HALF, v, 0:1], 0)).then_inc(gain_in[v], 16)

                for v in range(2):
                    load(v, v, v + 1)
                pool.wait_ge(t.cleared, 16)

                def sort(n, v):
                    nc.gpsimd.tensor_copy(tokens[:, v:v + 1, :], src[:, bass.ds(n, 1), :])
                    nc.gpsimd.tensor_copy(to[:, v:v + 1, :], slot[:, bass.ds(n, 1), :]).then_inc(staged, 1)
                    pool.wait_ge(staged, n + 1)
                    pool.sem_inc(t.passed, 1)
                    for j in range(K):
                        nc.gpsimd.indirect_dma_start(slots_flat, bass.IndirectOffsetOnAxis(to[:, v, j:j + 1], 0),
                                                     tokens[:, v, :], None).then_inc(sorted_[v], 16)

                sort(0, 0)
                sort(1, 1)
                with pool.Fori(1, TILES // 2) as i:
                    for v in range(2):
                        pool.wait_ge(sorted_[v], 16 * K * i)
                        pool.sem_inc(t.passed, 1)
                        sort(2 * i + v, v)
                with pool.Fori(0, B // 2 - 1) as i:
                    for v in range(2):
                        pool.wait_ge(used, 2 * i + v + 1)
                        pool.sem_inc(t.passed, 1)
                        load(2 * i + v + 2, v, 2 * i + v + 3)
                if expert_gain is not None:
                    pool.wait_ge(used, B - 1)
                    nc.gpsimd.tensor_copy(row[:, 0, 0:1], up_row[:, B:B + 1]).then_inc(row_ready, 1)
                    pool.wait_ge(row_ready, B + 1)
                    load_gain(0)

            @block.sync
            def _(sp):
                def load(b, v):
                    sp.dma_start(x[:, v], t.slots[b].rearrange("a s p d -> p (a s) d") if not isinstance(b, int)
                                 else t.slots[b].rearrange("s p d -> p s d")).then_inc(x_in[v], 16)
                for v in range(2):
                    sp.wait_ge(sorted_[v], 16 * K * (TILES // 2))
                load(0, 0)
                with sp.Fori(0, B // 2) as i:
                    for v in range(2):
                        b = 2 * i + v
                        sp.wait_ge(turned, b + 1)
                        load(bass.ds(b + 1, 1), 1 - v)
                        sp.wait_ge(y_done, b + 3)
                        sp.dma_start(t.results[bass.ds(b, 1)].rearrange("a s p d -> p (a s) d"), y[:, v]).then_inc(stored[v], 16)
                        sp.wait_ge(stored[v], 16 * i + 16)
                        sp.sem_inc(y_free, 1)
                sp.wait_ge(x_in[0], 16 * (B // 2) + 16)

            @block.tensor
            def _(pe):
                def turn_(v):
                    for s in range(SUBS):
                        for k in range(2):
                            last = nc.tensor.transpose(bankX[0:HALF, BLOCK * k + 128 * s:BLOCK * k + 128 * (s + 1)],
                                                       x[:, v, s, HALF * k:HALF * (k + 1)], w["ident"][:])
                    last.then_inc(turned, 1)

                if rows > HALF:
                    pe.wait_ge(ones_done, 1)
                pe.wait_ge(x_in[0], 16)
                turn_(0)
                with pe.Fori(0, B // 2) as i:
                    for v in range(2):
                        b = 2 * i + v
                        pe.wait_ge(xT_done, b + 1)
                        pe.wait_ge(loaded[v], 16 * LOADS * i + 16 * LOADS)

                        def up(m):
                            pe.wait_ge(hid_done, b * M + m + 1)
                            for n in range(N):
                                for k in range(2):
                                    part = rows if k == 0 else HALF
                                    last = nc.tensor.matmul(bankU[m % 3][:, BLOCK * n:BLOCK * (n + 1)],
                                                            wu[0:part, v, n, HIDDEN * k + 128 * m:HIDDEN * k + 128 * (m + 1)],
                                                            xT[0:part, v, k, :], start=(k == 0), stop=(k == 1))
                            last.then_inc(up_done, 1)

                        def down_(m):
                            pe.wait_ge(hid_done, b * M + m + 4)
                            if m == 0:
                                pe.wait_ge(y_done, b + 1)
                            for s in range(SUBS):
                                last = nc.tensor.matmul(bankY[v][s][:, 0:DIM], hid[:, m, 128 * s:128 * (s + 1)],
                                                        wd[:, v, DIM * m:DIM * (m + 1)], start=(m == 0), stop=(m == M - 1))
                            last.then_inc(down, 1)

                        up(0)
                        up(1)
                        for m in range(2, M):
                            up(m)
                            down_(m - 2)
                        pe.wait_ge(x_in[1 - v], 16 * i + (16 if v == 0 else 32))
                        turn_(1 - v)
                        down_(M - 2)
                        down_(M - 1)
                        pe.drain().then_inc(used, 1)

            @block.scalar
            def _(act):
                def take_xT(v, n):
                    act.wait_ge(turned, n)
                    for k in range(2):
                        if expert_gain is not None:
                            scale = own_gain[:, v, k:k + 1]
                        else:
                            scale = 1.0 if gain is None else gain[0:HALF, k:k + 1]
                        last = nc.scalar.activation(xT[0:HALF, v, k, :], bankX[0:HALF, BLOCK * k:BLOCK * (k + 1)], ACT.Identity,
                                                    scale=scale, bias=0.0 if bias is None else bias[0:HALF, k:k + 1])
                    last.then_inc(xT_done, 1)

                if not gated:
                    act.sem_inc(hid_done, 3)
                if expert_gain is not None:
                    act.wait_ge(gain_in[0], 16)
                take_xT(0, 1)
                with act.Fori(0, B // 2) as i:
                    for v in range(2):
                        b = 2 * i + v
                        for m in range(M):
                            act.wait_ge(up_done, b * M + m + 1)
                            if gated:
                                act.wait_ge(hid_done, b * M + m + 2)
                                nc.scalar.activation(sa[:, m % 2, :], bankU[m % 3][:, 0:BLOCK], func).then_inc(silu_done, 1)
                            else:
                                act.wait_ge(down, b * M + m + 1)
                                nc.scalar.activation(hid[:, m, :], bankU[m % 3][:, 0:BLOCK], func).then_inc(hid_done, 1)
                        if expert_gain is not None:
                            act.wait_ge(gain_in[1 - v], 16 * i + (32 if v else 16))
                        take_xT(1 - v, b + 2)

            @block.vector
            def _(dve):
                if rows > HALF:
                    nc.vector.memset(xT[HALF:HALF + 1], 1.0).then_inc(ones_done, 1)
                dve.sem_inc(down, M)
                dve.sem_inc(y_done, 2)
                dve.sem_inc(y_free, 2)
                if gated:
                    dve.sem_inc(hid_done, 3)
                with dve.Fori(0, B // 2) as i:
                    for v in range(2):
                        b = 2 * i + v
                        if gated:
                            for m in range(M):
                                dve.wait_ge(silu_done, b * M + m + 1)
                                dve.wait_ge(down, b * M + m + 1)
                                nc.vector.tensor_tensor(hid[:, m, :], sa[:, m % 2, :], bankU[m % 3][:, BLOCK:2 * BLOCK],
                                                        ALU.mult).then_inc(hid_done, 1)
                        dve.wait_ge(down, b * M + 2 * M)
                        dve.wait_ge(y_free, b + 1)
                        for s in range(SUBS):
                            last = nc.vector.tensor_copy(y[:, v, s, :], bankY[v][s][:, 0:DIM])
                        last.then_inc(y_done, 1)

        with ExitStack() as inner:
            back = t.sbuf("back", [TILE, 2, K, DIM], inner)
            here = t.sbuf("here", [TILE, 2, K], inner, U32)
            fetched, staged, summed = [t.sem("fetched_even", lasting=True), t.sem("fetched_odd", lasting=True)], t.sem("staged"), t.sem("summed")
            with t.block() as block:
                @block.gpsimd
                def _(pool):
                    with pool.Fori(0, TILES // 2) as i:
                        for v in range(2):
                            pool.wait_ge(summed, 2 * K * i + K * v + K)
                            pool.sem_inc(t.passed, 1)
                            nc.gpsimd.tensor_copy(here[:, v:v + 1, :], slot[:, bass.ds(2 * i + v, 1), :]).then_inc(staged, 1)
                            pool.wait_ge(staged, 2 * i + v + 1)
                            pool.sem_inc(t.passed, 1)
                            for j in range(K):
                                nc.gpsimd.indirect_dma_start(back[:, v, j, :], None, results_flat,
                                                             bass.IndirectOffsetOnAxis(here[:, v, j:j + 1], 0)
                                                             ).then_inc(fetched[v], 16)

                @block.vector
                def _(dve):
                    dve.sem_inc(summed, 2 * K)
                    with dve.Fori(0, TILES // 2) as i:
                        for v in range(2):
                            tile = dst[:, bass.ds(2 * i + v, 1), :]
                            dve.wait_ge(fetched[v], 16 * K * i + 16 * K)
                            for j in range(K):
                                dve.wait_ge(summed, K * (2 * i + v + 2) + j)
                                nc.vector.scalar_tensor_tensor(tile, back[:, v, j:j + 1, :],
                                                               gate[:, bass.ds(2 * i + v, 1), j:j + 1],
                                                               tile, ALU.mult, ALU.add).then_inc(summed, 1)


def gates(t, w, rows):
    return [w[0:rows, 0, :], w[0:HALF, 1, :]]


def xT_tile(t, rows):
    return lambda i, k: t.xT[0:rows if k == 0 else HALF, k, TILE * i:TILE * (i + 1)]


def add_into(t, dst, src):
    nc = t.nc
    done = t.sem("added_into")
    with t.block() as block:
        @block.vector
        def _(dve):
            nc.vector.tensor_tensor(flat(dst[:]), flat(dst[:]), flat(src[:]), ALU.add).then_inc(done, 1)


def layer1_ffn(t):
    w = t.w
    normalise(t, t.h, 1e-5, keep=t.x, feature_major=False)
    normalise(t, t.x, 1e-5, gain=w["L1_ln1_g"], bias=w["L1_ln1_b"])
    heads_attention(t, w["L1_qkv"], w["L1_proj"], t.x, unit=False)
    add_into(t, t.h, t.x)
    normalise(t, t.x, 1e-5, keep=t.x, gain=w["L1_ln2_g"], bias=w["L1_ln2_b"])
    with ExitStack() as st:
        share = t.sbuf("share8", [TILE, TILES, 8], st)
        shareT = t.sbuf("shareT", [8, 1, TOKENS], st)
        picked = [t.sbuf(f"pick{j}", [TILE, TILES, 8], st) for j in range(2)]
        route(t, xT_tile(t, HALF + 1), gates(t, w["L1_gate"], HALF + 1), 8, 2, masks=picked, weights=share)
        turn(t, share, shareT[:, 0, :])
        add_back(t, shareT, t.h, lambda g, i: w["L1_b2"][:, g, :])
        experts(t, "L1", t.x, t.h, picked, share, 8, HALF + 1, ACT.Gelu, gated=False, gain=w["L1_ln2_g"], bias=w["L1_ln2_b"])


def layer2_mixer(t):
    normalise(t, t.h, 1e-5)
    heads_attention(t, t.w["L2_qkv"], t.w["L2_proj"], t.h, unit=True)

GROUPS2, SLOTS2, CAPACITY = 8, 64, 62
L2_EXPERTS = 8


def layer2_ffn(t):
    nc, w = t.nc, t.w
    E, M = L2_EXPERTS, HIDDEN // 128
    size = [TILE, TILES, E]
    normalise(t, t.h, 1e-5, keep=t.x)
    with ExitStack() as st:
        combine = t.sbuf("combine", [128, E // 2, TOKENS], st)
        taken = t.sbuf("taken", [HALF, 2, E, GROUPS2, SLOTS2], st)
        with ExitStack() as inner:
            m = [t.sbuf(f"choice{j}", size, inner) for j in range(2)]
            prob, chosen, slot, part = (t.sbuf(n, size, inner) for n in ("prob", "chosen", "slot", "part"))
            total = t.sbuf("total", [TILE, TILES], inner)
            route(t, xT_tile(t, HALF), gates(t, w["L2_gate"], HALF), E, 2, masks=m, total=total, probs=prob)
            ranked, step, slots_done = t.sem("ranked"), t.sem("step"), t.sem("slots_done")
            with t.block() as block:
                view = lambda x, par: x[:].rearrange("p (g a) e -> p g a e", a=2)[:, :, par, :]
                rank = lambda b: t.bank[b][0:TILE, 0:GROUPS2 * E]

                @block.tensor
                def _(pe):
                    for j in range(2):
                        for par in range(2):
                            ahead = [(0, 0), (0, 1), (1, 0), (1, 1)][0:2 * j + par]
                            terms = [(w["before"], view(m[j], par))] + [(w["all"], view(m[a], b)) for a, b in ahead]
                            for n, (lhs, rhs) in enumerate(terms):
                                last = nc.tensor.matmul(rank(2 * j + par).rearrange("p (g e) -> p g e", e=E), lhs[:, 0:TILE], rhs,
                                                        start=(n == 0), stop=(n == len(terms) - 1))
                    last.then_inc(ranked, 1)

                @block.vector
                def _(dve):
                    one = Steps(dve, step)
                    one(nc.vector.tensor_tensor(chosen[:], m[0][:], m[1][:], ALU.add))
                    one(nc.vector.tensor_tensor(prob[:], prob[:], chosen[:], ALU.mult))
                    dve.wait_ge(ranked, 1)
                    for j in range(2):
                        for par in range(2):
                            one(nc.vector.tensor_tensor(view((slot, part)[j], par), view(m[j], par),
                                                        rank(2 * j + par).rearrange("p (g e) -> p g e", e=E), ALU.mult))
                    one(nc.vector.tensor_tensor(slot[:], slot[:], part[:], ALU.add))
                    one(nc.vector.tensor_tensor(slot[:], slot[:], chosen[:], ALU.add))
                    nc.vector.tensor_scalar(slot[:], slot[:], -1.0, None, ALU.add).then_inc(slots_done, 1)

            xs = t.sbuf("xs2", [TILE, 2, DIM], inner)
            hot = t.sbuf("hot", [TILE, 2, E, SLOTS2], inner)
            gated = t.sbuf("gated", [TILE, 2, E, SLOTS2], inner)
            staged, hot_done, gated_done, filled, taken_done, turned, combine_done = (
                t.sem(n) for n in ("staged", "hot_done", "gated_done", "filled", "taken_done", "turned", "combine_done"))
            full = [TILE, E, SLOTS2]
            with t.block() as block:
                @block.vector
                def _(dve):
                    with dve.Fori(0, GROUPS2) as g:
                        dve.wait_ge(filled, g + 1)
                        dve.wait_ge(turned, 2 * g + 2)
                        for u in range(2):
                            at = bass.ds(2 * g + u, 1)
                            nc.vector.tensor_tensor(
                                hot[:, u], w["slot"][:].unsqueeze(1).to_broadcast(full),
                                slot[:, at, :].rearrange("p a e -> p (a e)").unsqueeze(2).to_broadcast(full), ALU.is_equal).then_inc(hot_done, 1)
                        for u in range(2):
                            at = bass.ds(2 * g + u, 1)
                            dve.wait_ge(hot_done, 2 * g + u + 1)
                            nc.vector.tensor_tensor(
                                gated[:, u], hot[:, u],
                                prob[:, at, :].rearrange("p a e -> p (a e)").unsqueeze(2).to_broadcast(full), ALU.mult).then_inc(gated_done, 1)

                @block.gpsimd
                def _(pool):
                    with pool.Fori(0, GROUPS2) as g:
                        pool.wait_ge(filled, g + 1)
                        pool.sem_inc(t.passed, 1)
                        nc.gpsimd.tensor_copy(xs[:], t.x[:, bass.ds(2 * g, 2), :]).then_inc(staged, 1)

                @block.tensor
                def _(pe):
                    pe.sem_inc(filled, 1)
                    pe.sem_inc(turned, 2)
                    with pe.Fori(0, GROUPS2) as g:
                        pe.wait_ge(staged, g + 1)
                        pe.wait_ge(hot_done, 2 * g + 2)
                        pe.wait_ge(taken_done, 2 * g + 1)
                        for k in range(2):
                            for u in range(2):
                                last = nc.tensor.matmul(t.bank[k][0:HALF, :], xs[:, u, HALF * k:HALF * (k + 1)],
                                                        hot[:, u].rearrange("p e c -> p (e c)"), start=(u == 0), stop=(u == 1))
                        last.then_inc(filled, 1)
                        for u in range(2):
                            pe.wait_ge(gated_done, 2 * g + u + 1)
                            pe.wait_ge(combine_done, 2 * g + u + 1)
                            for b in range(E // 2):
                                last = nc.tensor.transpose(t.bank[2 + u][:, TILE * b:TILE * (b + 1)],
                                                           gated[:, u, 2 * b:2 * b + 2, :].rearrange("p e c -> p (e c)"),
                                                           w["ident"][0:TILE, 0:TILE])
                            last.then_inc(turned, 1)

                @block.scalar
                def _(act):
                    act.sem_inc(taken_done, 1)
                    act.sem_inc(combine_done, 2)
                    with act.Fori(0, GROUPS2) as g:
                        for k in range(2):
                            act.wait_ge(filled, g + 2)
                            act.sem_inc(t.passed, 1)
                            nc.scalar.activation(taken[:, k, :, bass.ds(g, 1), :].rearrange("p e g c -> p e (g c)"),
                                                 t.bank[k][0:HALF, :].rearrange("p (e c) -> p e c", e=E), ACT.Identity).then_inc(taken_done, 1)
                        for u in range(2):
                            act.wait_ge(turned, 2 * g + u + 3)
                            act.sem_inc(t.passed, 1)
                            nc.scalar.activation(combine[:, :, bass.ds(TILE * (2 * g + u), TILE)],
                                                 t.bank[2 + u][:, 0:4 * TILE].rearrange("p (b n) -> p b n", n=TILE),
                                                 ACT.Identity).then_inc(combine_done, 1)
        given = t.sbuf("given", [128, E // 2, GROUPS2, DIM], st)
        inner = ExitStack()
        wu = t.sbuf("wu2", [HALF, 2, 2, HIDDEN], inner)
        wd = t.sbuf("wd2", [128, 2, M, DIM], inner)
        hid = t.sbuf("hid2", [128, 2, M, GROUPS2 * SLOTS2], inner)
        loaded, used = [t.sem("loaded_even"), t.sem("loaded_odd")], [t.sem("used_even"), t.sem("used_odd")]
        up_done, hid_done, down, given_done = t.sem("up_done"), t.sem("hid_done"), t.sem("down"), t.sem("given_done")
        with t.block() as block:
            @block.sync
            def _(sp):
                for v in range(2):
                    sp.dma_start(wu[:, v], t.args["L2_up"][v]).then_inc(loaded[v], 16)
                    sp.dma_start(wd[:, v], t.args["L2_down"][v]).then_inc(loaded[v], 16)
                with sp.Fori(0, E // 2 - 1) as i:
                    for v in range(2):
                        sp.wait_ge(used[v], i + 1)
                        at = bass.ds(2 * i + v + 2, 1)
                        sp.dma_start(wu[:, v], t.args["L2_up"][at].rearrange("a p k m -> (a p) k m")).then_inc(loaded[v], 16)
                        sp.dma_start(wd[:, v], t.args["L2_down"][at].rearrange("a p m d -> (a p) m d")).then_inc(loaded[v], 16)

            @block.tensor
            def _(pe):
                pe.sem_inc(down, 2 * GROUPS2)
                with pe.Fori(0, E // 2) as i:
                    for v in range(2):
                        e = 2 * i + v
                        pe.wait_ge(loaded[v], 32 * i + 32)
                        for m_ in range(M):
                            pe.wait_ge(hid_done, M * e + m_ + 1)
                            for k in range(2):
                                last = nc.tensor.matmul(t.bank[m_ % 2][:, :], wu[:, v, k, 128 * m_:128 * (m_ + 1)],
                                                        taken[:, k, bass.ds(e, 1), :, :].rearrange("p a g c -> p (a g c)"),
                                                        start=(k == 0), stop=(k == 1))
                            last.then_inc(up_done, 1)
                    for v in range(2):
                        e = 2 * i + v
                        pe.wait_ge(hid_done, M * e + M + 2)
                        for g in range(GROUPS2):
                            pe.wait_ge(given_done, GROUPS2 * e + g + 1)
                            for m_ in range(M):
                                last = nc.tensor.matmul(t.bank[2 + g % 4][SLOTS2 * v:SLOTS2 * (v + 1), 0:DIM],
                                                        hid[:, v, m_, SLOTS2 * g:SLOTS2 * (g + 1)], wd[:, v, m_, :],
                                                        start=(m_ == 0), stop=(m_ == M - 1))
                            last.then_inc(down, 1)
                        pe.drain().then_inc(used[v], 1)

            @block.scalar
            def _(act):
                act.sem_inc(hid_done, 2)
                with act.Fori(0, E // 2) as i:
                    for v in range(2):
                        e = 2 * i + v
                        for m_ in range(M):
                            act.wait_ge(up_done, M * e + m_ + 1)
                            if m_ == 0:
                                act.wait_ge(down, GROUPS2 * e + GROUPS2)
                            nc.scalar.activation(hid[:, v, m_, :], t.bank[m_ % 2][:, :], ACT.Relu).then_inc(hid_done, 1)

            @block.vector
            def _(dve):
                dve.sem_inc(given_done, 4)
                with dve.Fori(0, E // 2) as i:
                    for v in range(2):
                        for g in range(GROUPS2):
                            dve.wait_ge(down, GROUPS2 * (2 * i + v) + g + 1 + 2 * GROUPS2)
                            rows = slice(SLOTS2 * v, SLOTS2 * (v + 1))
                            nc.vector.tensor_copy(given[rows, bass.ds(i, 1), g:g + 1, :].rearrange("p a g d -> p (a g) d"),
                                                  t.bank[2 + g % 4][rows, 0:DIM].unsqueeze(1)).then_inc(given_done, 1)
        inner.close()
        add_back(t, combine, t.h, lambda b, i: given[:, b, bass.ds(i, 1), :])


INNER = 2 * DIM
TAPS = 4


def layer3_mixer(t):
    nc, w = t.nc, t.w
    G = INNER // 128
    normalise(t, t.h, 1e-5, keep=t.x, feature_major=False)
    normalise(t, t.x, 1e-6, centred=False, gain=w["L3_g"])
    with ExitStack() as st:
        xc, sz, rate, u = (t.sbuf(n, [128, G, TOKENS], st) for n in ("xc", "sz", "rate3", "u3"))
        bc = t.sbuf("bc3", [2 * STATES + 1, TOKENS], st)
        coef = t.sbuf("coef3", [128, G, STATES], st)
        with ExitStack() as inner:
            xs, cv = t.sbuf("xs3", [128, G, CHUNK], inner), t.sbuf("cv", [128, G, CHUNK], inner)
            up, xs_done, conv_step, conv_done, xc_done, mixed, bc_done, stepped, rate_done = (
                t.sem(n) for n in ("up", "xs_done", "conv_step", "conv_done", "xc_done", "mixed", "bc_done", "stepped", "rate_done"))
            with t.block() as block:
                @block.tensor
                def _(pe):
                    pe.sem_inc(rate_done, G)
                    with pe.Fori(0, CHUNKS) as c:
                        at = bass.ds(CHUNK * c, CHUNK)
                        pe.wait_ge(rate_done, G * c + G)
                        for m in range(2 * G):
                            for k in range(2):
                                last = nc.tensor.matmul(t.bank[m][:, 0:CHUNK], w["L3_in"][:, k, 128 * m:128 * (m + 1)],
                                                        t.xT[0:HALF, k, at], start=(k == 0), stop=(k == 1))
                            last.then_inc(up, 1)
                        pe.wait_ge(xc_done, c + 1)
                        for g in range(G):
                            last = nc.tensor.matmul(t.bank[6][0:2 * STATES + 1, 0:CHUNK], w["L3_xproj"][:, g, :], xc[:, g, at],
                                                    start=(g == 0), stop=(g == G - 1))
                        last.then_inc(mixed, 1)
                        pe.wait_ge(bc_done, c + 1)
                        pe.sem_inc(t.passed, 1)
                        for g in range(G):
                            last = nc.tensor.matmul(t.bank[(7, 0, 1)[g]][:, 0:CHUNK], w["L3_dt"][:, 128 * g:128 * (g + 1)], bc[:, at],
                                                    start=True, stop=True)
                        last.then_inc(stepped, 1)

                @block.scalar
                def _(act):
                    nc.scalar.preload_act_table(ACT.Silu)
                    with act.Fori(0, CHUNKS) as c:
                        at = bass.ds(CHUNK * c, CHUNK)
                        for g in range(G):
                            act.wait_ge(up, 2 * G * c + g + 1)
                            nc.scalar.activation(xs[:, g, :], t.bank[g][:, 0:CHUNK], ACT.Identity).then_inc(xs_done, 1)
                        for g in range(G):
                            act.wait_ge(up, 2 * G * c + G + g + 1)
                            act.sem_inc(t.passed, 1)
                            nc.scalar.activation(sz[:, g, at], t.bank[G + g][:, 0:CHUNK], ACT.Silu)
                        act.wait_ge(conv_done, G * c + G)
                        act.sem_inc(t.passed, 1)
                        nc.scalar.activation(xc[:, :, at], cv[:], ACT.Silu).then_inc(xc_done, 1)
                        act.wait_ge(mixed, c + 1)
                        act.sem_inc(t.passed, 1)
                        nc.scalar.activation(bc[:, at], t.bank[6][0:2 * STATES + 1, 0:CHUNK], ACT.Identity).then_inc(bc_done, 1)

                @block.vector
                def _(dve):
                    one = Steps(dve, conv_step)
                    with dve.Fori(0, CHUNKS) as c:
                        one.enter(c, (TAPS - 1) * G)
                        at = bass.ds(CHUNK * c, CHUNK)
                        for g in range(G):
                            dve.wait_ge(xs_done, G * c + g + 1)
                            x_ = xs[:, g, :].rearrange("p (b t) -> p b t", t=SEQ)
                            y_ = cv[:, g, :].rearrange("p (b t) -> p b t", t=SEQ)
                            tap = lambda k: w["L3_conv"][:, g, k:k + 1]
                            one(nc.vector.tensor_scalar(cv[:, g, :], xs[:, g, :], tap(TAPS - 1), w["L3_conv_b"][:, g:g + 1], ALU.mult, ALU.add))
                            for back in range(1, TAPS):
                                ins = nc.vector.scalar_tensor_tensor(y_[:, :, back:], x_[:, :, 0:SEQ - back], tap(TAPS - 1 - back),
                                                                     y_[:, :, back:], ALU.mult, ALU.add)
                                if back < TAPS - 1:
                                    one(ins)
                                else:
                                    ins.then_inc(conv_done, 1)
                        dve.wait_ge(stepped, c + 1)
                        for g in range(G):
                            nc.vector.tensor_scalar(rate[:, g, at], t.bank[(7, 0, 1)[g]][:, 0:CHUNK], w["L3_b_dt"][:, g:g + 1], None,
                                                    ALU.add).then_inc(rate_done, 1)
                    one.leave(CHUNKS)
            softplus(t, rate)
            exp_done = t.sem("exp_done")
            with t.block() as block:
                @block.scalar
                def _(act):
                    nc.scalar.activation(coef[:], w["L3_A_log"][:], ACT.Exp).then_inc(exp_done, 1)

                @block.vector
                def _(dve):
                    nc.vector.tensor_tensor(flat(u[:]), flat(rate[:]), flat(xc[:]), ALU.mult)
                    dve.wait_ge(exp_done, 1)
                    nc.vector.tensor_scalar(coef[:], coef[:], -1.0, None, ALU.mult)
        scan(t, u, rate, coef, bc, xc, w["L3_D"], xc, bilinear=False)
        with t.block() as block:
            @block.vector
            def _(dve):
                nc.vector.tensor_tensor(flat(xc[:]), flat(xc[:]), flat(sz[:]), ALU.mult)
        add_back(t, xc, t.x, lambda g, i: w["L3_out"][:, g, :])
    with ExitStack() as st:
        plain = t.sbuf("plain", [TILE, TILES, DIM], st)
        picked = [t.sbuf(f"pick{j}", [TILE, TILES, 8], st) for j in range(2)]
        normalise(t, t.x, 1e-6, keep=plain, centred=False)
        gate = t.sbuf("gate3", [HALF, 2, 8], st)
        share = t.sbuf("share3", [TILE, TILES, 8], st)
        whole = t.sbuf("whole", [TILE, TILES], st)
        with t.block() as block:
            @block.vector
            def _(dve):
                for k in range(2):
                    nc.vector.tensor_scalar(gate[:, k, :], w["L3_router"][:, k, :], w["L3_g_moe"][:, k:k + 1], None, ALU.mult)
        route(t, xT_tile(t, HALF), gates(t, gate, HALF), 8, 2, masks=picked, weights=share)
        summed = t.sem("summed")
        with t.block() as block:
            @block.vector
            def _(dve):
                nc.vector.tensor_reduce(whole[:], share[:], AX.X, ALU.add).then_inc(summed, 1)
                dve.wait_ge(summed, 1)
                with dve.Fori(0, TILES // 4) as i:
                    for v in range(4):
                        at = bass.ds(4 * i + v, 1)
                        nc.vector.scalar_tensor_tensor(t.h[:, at, :], t.x[:, at, :], whole[:, at], t.h[:, at, :], ALU.mult, ALU.add)
        experts(t, "L3m", plain, t.h, picked, share, 8, HALF, ACT.Silu, gated=True,
                expert_gain=t.args["L3_g_exp"])


def layer3_ffn(t):
    normalise(t, t.h, 1e-5, keep=t.x)
    with ExitStack() as st:
        share = t.sbuf("share16", [TILE, TILES, 16], st)
        picked = [t.sbuf(f"pick{j}", [TILE, TILES, 16], st) for j in range(4)]
        route(t, xT_tile(t, HALF), gates(t, t.w["L3f_gate"], HALF), 16, 4, masks=picked, weights=share)
        experts(t, "L3f", t.x, t.h, picked, share, 16, HALF, ACT.Silu, gated=True)


def tower(nc, args, out):
    with ExitStack() as stack:
        t = Tower(nc, stack, args)
        embed(t)
        clear_slots(t)
        layer0_mixer(t)
        layer0_ffn(t)
        layer1_mixer(t)
        layer1_ffn(t)
        layer2_mixer(t)
        layer2_ffn(t)
        layer3_mixer(t)
        layer3_ffn(t)
        store(t, out, t.h)


def halves(w, bias=None):
    a = w.reshape(2, HALF, -1).transpose(1, 0, 2)
    if bias is None:
        return np.ascontiguousarray(a)
    extra = np.zeros((1, 2, a.shape[2]), np.float32)
    extra[0, 0] = bias.reshape(-1)
    return np.concatenate([a, extra], axis=0)


def columns(v, parts=HALF):
    return np.ascontiguousarray(v.reshape(-1, parts).T)


def stacked(parts):
    return np.ascontiguousarray(np.stack(parts))


def rows128(w):
    return np.ascontiguousarray(w.reshape(-1, 128, w.shape[1]).transpose(1, 0, 2))


def windows():
    inner = range(PATCH)
    spots = [(y, x) for y in inner for x in inner]
    spots += [(-1, x) for x in inner] + [(PATCH, x) for x in inner] + [(y, -1) for y in inner] + [(y, PATCH) for y in inner]
    return [(c, y, x) for c in range(CHANNELS) for y, x in spots]


READS = ((0, 0), (0, -1), (0, 1), (-1, 0), (1, 0))


def layout(inputs):
    f = {k: np.asarray(v) for k, v in inputs.items()}
    a = {}
    spots = windows()
    c, y, x = (np.array(v) for v in zip(*spots))
    padded = np.pad(f["x"], ((0, 0), (0, 0), (1, 1), (1, 1)))
    rows = PATCH * np.arange(GRID)
    px = padded[:, c[:, None, None], (y[:, None] + rows + 1)[:, :, None], (x[:, None] + rows + 1)[:, None, :]]
    seq = np.zeros((IMAGES, WINDOW, SEQ), np.float32)
    seq[:, :, 1:] = px.reshape(IMAGES, WINDOW, SEQ - 1)
    a["pixels"] = np.ascontiguousarray(seq.reshape(TILES, 2, WCHUNKS, WROWS, SEQ).transpose(0, 3, 2, 1, 4)
                                       .reshape(TILES, WROWS, WCHUNKS, TILE))
    wide = np.zeros((SHIFTS, WINDOW, DIM + 2), np.float32)
    stack = np.concatenate([f["L0_tok_proj_weight"], f["L0_tok_ln_weight"][None], f["L0_tok_ln_bias"][None]])
    stack = stack.reshape(DIM + 2, PATCH, PATCH, SHIFTS, CHANNELS)
    count = np.zeros(WINDOW, np.float32)
    for s, (dy, dx) in enumerate(READS):
        ys, xs = y - dy, x - dx
        ok = (ys >= 0) & (ys < PATCH) & (xs >= 0) & (xs < PATCH)
        wide[s, ok] = stack[:, ys[ok], xs[ok], s, c[ok]].T
        count[ok] += 1
    wide = wide.reshape(SHIFTS, WCHUNKS, WROWS, DIM + 2).transpose(2, 1, 0, 3)
    a["w_patch"] = np.ascontiguousarray(wide[..., :DIM])
    a["ln_gain"] = np.ascontiguousarray(wide[..., DIM:].transpose(0, 3, 1, 2))
    a["share"] = np.ascontiguousarray((count / PATCH_DIM).astype(np.float32).reshape(WCHUNKS, WROWS).T)
    a["patch_bias"] = f["L0_tok_proj_bias"].reshape(1, DIM)
    a["cls"] = f["cls_tok"].reshape(1, 1, DIM)
    a["c_ident"] = np.eye(128, dtype=np.float32)
    a["c_select"] = np.tile(np.eye(2 * STATES, dtype=np.float32), (3, 1))
    a["c_minus_one"] = np.full((128, 1), -1.0, np.float32)
    a["c_mean"] = np.full((HALF, HALF), 1.0 / DIM, np.float32)
    a["c_clamp"] = np.full((128, 1), -CENTRE / REACH, np.float32)
    for name in ("W_bc", "W_dt"):
        a["c_L0_" + name] = halves(f["L0_attn_" + name])
    a["c_L0_W_dtp"] = f["L0_attn_W_dtp"]
    a["c_L0_A_log"] = halves(f["L0_attn_A_log"])
    for name, key in (("b_dt", "b_dt"), ("rms", "rms_scale"), ("D", "D_param")):
        a["c_L0_" + name] = columns(f["L0_attn_" + key])
    a["c_first"] = np.tile(np.arange(16, 0, -1, dtype=np.float32), (128, 1))
    own = np.arange(TILE) // SEQ
    a["c_mask"] = np.where(own[:, None] == own[None, :], 0.0, MASKED).astype(np.float32)
    a["c_L0_enc"] = halves(f["L0_ffn_enc_w"], f["L0_ffn_enc_b"])
    a["c_L0_switch"] = np.concatenate([f["L0_ffn_sw_w"], f["L0_ffn_sw_b"][None]])
    a["c_L0_w1"] = halves(f["L0_ffn_w1"].transpose(1, 0, 2).reshape(DIM, -1))
    a["c_L0_b1"] = columns(f["L0_ffn_b1"], 128)
    a["c_L0_w2"] = np.ascontiguousarray(f["L0_ffn_w2"].reshape(L0_GROUPS, 128, DIM).transpose(1, 0, 2))
    a["c_L0_b2"] = f["L0_ffn_b2"].reshape(L0_EXPERTS, 1, DIM)
    row = np.arange(L0_GROUPS * 128).reshape(L0_GROUPS, 128) // L0_CODE
    a["c_L0_pair"] = (row[None] == np.arange(L0_EXPERTS)[:, None, None]).astype(np.float32)
    wq, wk, wv = (f["L1_attn_W" + x] for x in "qkv")
    a["c_L1_wqk"] = halves(np.concatenate([wq.T, wk.T], 1), np.concatenate([f["L1_attn_bq"], f["L1_attn_bk"]]))
    a["c_L1_wv"] = halves(wv.T, f["L1_attn_bv"])
    for name in ("ln1_g", "ln1_b", "ln2_g", "ln2_b"):
        a["c_L1_" + name] = columns(f["L1_ffn_" + name])
    a["c_L1_qkv"] = halves(f["L1_ffn_qkv_w"].T, np.zeros(3 * DIM, np.float32))
    a["c_L1_proj"] = halves(f["L1_ffn_proj_w"].T, f["L1_ffn_proj_b"])
    a["c_L1_gate"] = halves(f["L1_ffn_gate_w"].T, f["L1_ffn_gate_b"])
    a["c_L1_b2"] = f["L1_ffn_b2"].reshape(8, 1, DIM)
    a["L1_up"] = stacked([halves(f["L1_ffn_w1"][e].T, f["L1_ffn_b1"][e]) for e in range(8)])
    a["L1_down"] = stacked([rows128(f["L1_ffn_w2"][e].T) for e in range(8)])
    a["c_L2_qkv"] = halves(np.concatenate([f["L2_attn_Wq"], f["L2_attn_Wkv"]], 1), np.concatenate([f["L2_attn_bq"], f["L2_attn_bkv"]]))
    a["c_L2_proj"] = halves(f["L2_attn_Wproj"], f["L2_attn_bproj"])
    a["c_L2_scale"] = np.tile(f["L2_attn_scale"].reshape(1, HEADS), (TILE, 1))
    token = np.arange(TILE)
    a["c_before"] = (token[:, None] < token[None, :]).astype(np.float32)
    a["c_all"] = np.ones((TILE, 128), np.float32)
    a["c_full"] = np.tile(BLOCK * np.arange(MOST_OF_ONE, dtype=np.float32), (128, 1))
    a["c_block"] = np.tile(np.arange(MOST_BLOCKS + 1, dtype=np.float32), (128, 1))
    a["c_lane"] = np.arange(128, dtype=np.float32).reshape(128, 1)
    a["c_slot"] = np.tile(np.where(np.arange(SLOTS2) < CAPACITY, np.arange(SLOTS2), -5), (TILE, 1)).astype(np.float32)
    a["c_L2_gate"] = halves(f["L2_ffn_w_router"])
    a["L2_up"] = stacked([halves(x) for x in f["L2_ffn_wi"]])
    a["L2_down"] = stacked([rows128(x) for x in f["L2_ffn_wo"]])
    a["c_L3_g"] = columns(f["L3_attn_g_mamba"])
    a["c_L3_in"] = halves(f["L3_attn_w_in"])
    a["c_L3_conv"] = rows128(f["L3_attn_conv_w"])
    a["c_L3_conv_b"] = columns(f["L3_attn_conv_b"], 128)
    a["c_L3_xproj"] = rows128(f["L3_attn_w_xproj"])
    a["c_L3_dt"] = np.concatenate([np.zeros((2 * STATES, INNER), np.float32), f["L3_attn_w_dt"]])
    a["c_L3_b_dt"] = columns(f["L3_attn_b_dt"], 128)
    a["c_L3_A_log"] = rows128(f["L3_attn_A_log"])
    a["c_L3_D"] = columns(f["L3_attn_D_skip"], 128)
    a["c_L3_out"] = rows128(f["L3_attn_w_out"])
    a["c_L3_router"] = halves(f["L3_attn_w_router"])
    a["c_L3_g_moe"] = columns(f["L3_attn_g_moe"])
    a["L3_g_exp"] = np.ascontiguousarray(f["L3_attn_g_exp"].reshape(8, 2, HALF).transpose(0, 2, 1).reshape(8 * HALF, 2))
    a["L3m_up"] = stacked([halves(x) for x in f["L3_attn_w1"]])
    a["L3m_gate"] = stacked([halves(x) for x in f["L3_attn_w3"]])
    a["L3m_down"] = stacked([rows128(x) for x in f["L3_attn_w2"]])
    a["c_L3f_gate"] = halves(f["L3_ffn_router_w"].T)
    a["L3f_up"] = stacked([halves(x.T) for x in f["L3_ffn_w1"]])
    a["L3f_gate"] = stacked([halves(x.T) for x in f["L3_ffn_v1"]])
    a["L3f_down"] = stacked([rows128(x.T) for x in f["L3_ffn_w2"]])
    return a


def kernel(**inputs):
    import concourse.bacc as _bacc
    from concourse.bass_utils import run_bass_kernel_spmd as _run

    nc = _bacc.Bacc("TRN2", target_bir_lowering=False, num_devices=1)
    arrays = layout(inputs)
    args = {k: nc.dram_tensor(k, v.shape, F32, kind="ExternalInput").ap() for k, v in arrays.items()}
    out = nc.dram_tensor("out", (TOKENS, DIM), F32, kind="ExternalOutput").ap()
    tower(nc, args, out)
    r = _run(nc, [arrays], core_ids=[0])
    return r.results[0]["out"].reshape(IMAGES, SEQ, DIM)
```

```python
from contextlib import ExitStack, contextmanager

import numpy as np

import concourse.bass as bass
from concourse import mybir

F32 = mybir.dt.float32
BF16 = mybir.dt.bfloat16
ALU = mybir.AluOpType
ACT = mybir.ActivationFunctionType
AX = mybir.AxisListType

IMAGES, SEQ, DIM = 32, 50, 192
TOKENS = IMAGES * SEQ
TILE = 2 * SEQ
TILES = TOKENS // TILE
HALF = DIM // 2
CHUNK = 4 * TILE
CHUNKS = TOKENS // CHUNK
PATCH, CHANNELS, SHIFTS, GRID = 16, 3, 5, 7
PATCH_DIM = PATCH * PATCH * CHANNELS * SHIFTS
WINDOW = CHANNELS * (PATCH * PATCH + 4 * PATCH)
WROWS = 120
WCHUNKS = WINDOW // WROWS
HEADS, HEAD = 12, 16
HIDDEN = 768
MASKED = -1.0e30


class Steps:

    def __init__(self, engine, sem):
        self.engine, self.sem, self.done, self.offset = engine, sem, 0, None

    def __call__(self, instruction):
        instruction.then_inc(self.sem, 1)
        self.done += 1
        self.engine.wait_ge(self.sem, self.done if self.offset is None else self.offset + self.done)

    def enter(self, index, per):
        self.per, self.start, self.offset = per, self.done, index * per
        return self

    def leave(self, count):
        assert self.done - self.start == self.per, (self.done - self.start, self.per)
        self.done, self.offset = self.start + count * self.per, None


class Tower:

    def __init__(self, nc, stack, args):
        self.nc, self.stack, self.args, self.sems, self.tensors = nc, stack, args, 0, 0
        sb = self.sbuf
        self.h = sb("h", [TILE, TILES, DIM])
        self.x = sb("x", [TILE, TILES, DIM])
        self.xT = sb("xT", [HALF + 1, 2, TOKENS + 2 * TILE])
        self.bank = [stack.enter_context(nc.psum_tensor(f"bank{i}", [128, 512], F32)) for i in range(8)]
        self.old, self.theirs, self.new, self.mine = ExitStack(), [], ExitStack(), []
        self.loaded = self.sem("constants_loaded", lasting=True)
        self.loads = []
        self.passed = self.sem("passed", lasting=True)
        self.zeros = sb("zeros", [128, HALF])
        self.slots = nc.dram_tensor("slots", (MOST_BLOCKS + 1, SUBS, 128, DIM), F32, kind="Internal").ap()
        self.results = nc.dram_tensor("results", (MOST_BLOCKS, SUBS, 128, DIM), F32, kind="Internal").ap()
        self.w = {}
        for name, ap in args.items():
            if name.startswith("c_"):
                self.w[name[2:]] = t = sb(name, list(ap.shape))
                self.loads.append((t, ap))

    def sbuf(self, name, shape, stack=None, dtype=F32):
        self.tensors += 1
        return (stack or self.stack).enter_context(self.nc.sbuf_tensor(f"{name}_{self.tensors}", shape, dtype))

    def sem(self, name, lasting=False):
        self.sems += 1
        stack = self.stack if lasting else self.new
        sem = stack.enter_context(self.nc.semaphore(f"{name}_{self.sems}"))
        if not lasting:
            self.mine.append(sem)
        return sem

    @contextmanager
    def block(self):
        with self.nc.Block() as block:
            if self.theirs:
                @block.sync
                def _(sp):
                    for sem in self.theirs:
                        sp.sem_clear(sem)
            yield block
        self.old.close()
        self.old, self.theirs = self.new, self.mine
        self.new, self.mine = ExitStack(), []


def flat(ap):
    return ap.rearrange("p a b -> p (a b)")


def embed(t):
    nc = t.nc
    DEPTH = 4
    with ExitStack() as st:
        pixels = t.sbuf("pixels", [WROWS, DEPTH, WCHUNKS, TILE], st)
        squares = t.sbuf("squares", [WROWS, DEPTH, WCHUNKS, TILE], st)
        wshift = t.sbuf("wshift", [WROWS, WCHUNKS, SHIFTS, DIM], st)
        wsum = t.sbuf("wsum", [WROWS, WCHUNKS, DIM + 1], st)
        gain = t.sbuf("gain", [WROWS, 2, WCHUNKS, SHIFTS], st)
        share = t.sbuf("share", [WROWS, WCHUNKS], st)
        onesr = t.sbuf("onesr", [WROWS, TILE], st)
        pbias = t.sbuf("pbias", [1, DIM], st)
        rows = t.sbuf("rows", [TILE, 2, DIM], st)
        stats = t.sbuf("pstats", [TILE, TILES, 2], st)
        var = t.sbuf("pvar", [TILE, 4, TILES], st)
        weights_in, pixels_in, cls_in = t.sem("weights_in"), [t.sem(f"pixels_{u}") for u in range(DEPTH)], t.sem("cls_in")
        wsum_done, squared, multiplied, stored = t.sem("wsum_done"), t.sem("squared"), t.sem("multiplied"), t.sem("stored")
        bias_done, ones_done = t.sem("bias_done"), t.sem("ones_done")
        step, var_done, root_done, h_done = t.sem("step"), t.sem("var_done"), t.sem("root_done"), t.sem("h_done")
        raw, fixed = t.bank[4:4 + DEPTH], t.bank[2:4]
        args = t.args

        with t.block() as block:
            @block.sync
            def _(sp):
                sp.dma_start(gain[:], args["ln_gain"]).then_inc(weights_in, 16)
                sp.dma_start(wshift[:], args["w_patch"]).then_inc(weights_in, 16)
                sp.dma_start(share[:], args["share"]).then_inc(weights_in, 16)
                sp.dma_start(pbias[:], args["patch_bias"]).then_inc(weights_in, 16)
                for u in range(DEPTH):
                    sp.dma_start(pixels[:, u], args["pixels"][u]).then_inc(pixels_in[u], 16)
                with sp.Fori(0, TILES // DEPTH - 1) as i:
                    for u in range(DEPTH):
                        sp.wait_ge(multiplied, DEPTH * i + u + 1)
                        sp.dma_start(pixels[:, u], args["pixels"][bass.ds(DEPTH * (i + 1) + u, 1)]
                                     .rearrange("a p c n -> p (a c) n")).then_inc(pixels_in[u], 16)
                sp.wait_ge(h_done, TILES)
                for image in range(2):
                    sp.dma_start(t.h[SEQ * image:SEQ * image + 1, :, :],
                                 args["cls"].to_broadcast([1, TILES, DIM])).then_inc(cls_in, 16)
                sp.wait_ge(cls_in, 32)
                sp.wait_ge(t.loaded, 16 * len(t.loads))

            @block.vector
            def _(dve):
                one = Steps(dve, step)
                nc.vector.memset(onesr[:], 1.0).then_inc(ones_done, 1)
                one(nc.vector.memset(t.xT[:, :, TOKENS:], 0.0))
                one(nc.vector.memset(t.xT[HALF:HALF + 1, :, :], 1.0))
                dve.wait_ge(weights_in, 64)
                for s in range(SHIFTS):
                    if s:
                        dve.wait_ge(wsum_done, WCHUNKS * s)
                    for c in range(WCHUNKS):
                        if s == 0:
                            nc.vector.tensor_scalar(wsum[:, c, 0:DIM], wshift[:, c, s, :], gain[:, 0, c, s:s + 1], None,
                                                    ALU.mult).then_inc(wsum_done, 1)
                        else:
                            nc.vector.scalar_tensor_tensor(
                                wsum[:, c, 0:DIM], wshift[:, c, s, :], gain[:, 0, c, s:s + 1],
                                wsum[:, c, 0:DIM], ALU.mult, ALU.add).then_inc(wsum_done, 1)
                nc.vector.tensor_copy(wsum[:, :, DIM:DIM + 1], share[:].unsqueeze(2)).then_inc(wsum_done, 1)
                dve.wait_ge(bias_done, 1)
                nc.vector.tensor_copy(rows[:, 0, :], fixed[0][0:TILE, 0:DIM])
                one(nc.vector.tensor_copy(rows[:, 1, :], fixed[1][0:TILE, 0:DIM]))
                with dve.Fori(0, TILES // DEPTH) as i:
                    for u in range(DEPTH):
                        dve.wait_ge(multiplied, DEPTH * i + u + 1)
                        nc.vector.tensor_copy(t.h[:, bass.ds(DEPTH * i + u, 1), :],
                                              raw[u][0:TILE, 0:DIM].unsqueeze(1))
                        nc.vector.tensor_copy(stats[:, bass.ds(DEPTH * i + u, 1), :],
                                              raw[u][0:TILE, DIM:DIM + 2].unsqueeze(1)).then_inc(stored, 1)
                dve.wait_ge(stored, TILES + DEPTH)
                mean, second = stats[:, :, 0], stats[:, :, 1]
                one(nc.vector.tensor_tensor(var[:, 0, :], mean, mean, ALU.mult))
                one(nc.vector.tensor_tensor(var[:, 1, :], second, var[:, 0, :], ALU.subtract))
                nc.vector.tensor_scalar(var[:, 2, :], var[:, 1, :], 0.0, 1e-5, ALU.max, ALU.add).then_inc(var_done, 1)
                dve.wait_ge(root_done, 1)
                one(nc.vector.reciprocal(var[:, 1, :], var[:, 3, :]))
                one(nc.vector.tensor_scalar(var[:, 0, :], mean, -1.0, None, ALU.mult))
                with dve.Fori(0, TILES // 2) as i:
                    one.enter(i, 2)
                    for u in range(2):
                        tile = t.h[:, bass.ds(2 * i + u, 1), :]
                        one(nc.vector.scalar_tensor_tensor(tile, rows[:, 0:1, :], var[:, 0, bass.ds(2 * i + u, 1)],
                                                           tile, ALU.mult, ALU.add))
                        nc.vector.scalar_tensor_tensor(tile, tile, var[:, 1, bass.ds(2 * i + u, 1)],
                                                       rows[:, 1:2, :], ALU.mult, ALU.add).then_inc(h_done, 1)
                one.leave(TILES // 2)

            @block.scalar
            def _(act):
                for dst, src in t.loads:
                    nc.scalar.dma_start(dst[:], src).then_inc(t.loaded, 16)
                with act.Fori(0, TILES // DEPTH) as i:
                    for u in range(DEPTH):
                        act.wait_ge(pixels_in[u], 16 * i + 16)
                        nc.scalar.activation(squares[:, u], pixels[:, u], ACT.Square).then_inc(squared, 1)
                act.wait_ge(var_done, 1)
                nc.scalar.activation(var[:, 3, :], var[:, 2, :], ACT.Sqrt).then_inc(root_done, 1)

            @block.tensor
            def _(pe):
                pe.sem_inc(stored, DEPTH)
                pe.wait_ge(ones_done, 1)
                pe.wait_ge(weights_in, 64)
                nc.tensor.matmul(fixed[1][0:TILE, 0:DIM], onesr[0:1, :], pbias[:], start=True, stop=False)
                for c in range(WCHUNKS):
                    for s in range(SHIFTS):
                        last = nc.tensor.matmul(fixed[1][0:TILE, 0:DIM], gain[:, 1, c, s:s + 1].to_broadcast([WROWS, TILE]),
                                                wshift[:, c, s, :], start=False, stop=(c == WCHUNKS - 1 and s == SHIFTS - 1))
                pe.wait_ge(wsum_done, WCHUNKS * SHIFTS + 1)
                for c in range(WCHUNKS):
                    last = nc.tensor.matmul(fixed[0][0:TILE, 0:DIM], onesr[:], wsum[:, c, 0:DIM],
                                            start=(c == 0), stop=(c == WCHUNKS - 1))
                last.then_inc(bias_done, 1)
                with pe.Fori(0, TILES // DEPTH) as i:
                    for u in range(DEPTH):
                        pe.wait_ge(squared, DEPTH * i + u + 1)
                        pe.wait_ge(stored, DEPTH * i + u + 1)
                        for c in range(WCHUNKS):
                            nc.tensor.matmul(raw[u][0:TILE, 0:DIM + 1], pixels[:, u, c, :], wsum[:, c, :],
                                             start=(c == 0), stop=(c == WCHUNKS - 1))
                        for c in range(WCHUNKS):
                            last = nc.tensor.matmul(raw[u][0:TILE, DIM + 1:DIM + 2], squares[:, u, c, :],
                                                    share[:, c:c + 1], start=(c == 0), stop=(c == WCHUNKS - 1))
                        last.then_inc(multiplied, 1)


def normalise(t, src, eps, *, keep=None, centred=True, gain=None, bias=None, feature_major=True):
    nc = t.nc
    DEPTH = 4
    with ExitStack() as st:
        bn = t.sbuf("bn", [TILE, TILES, 6], st)
        mv = t.sbuf("mv", [TILE, TILES, 2], st)
        sd = t.sbuf("sd", [TILE, 4, TILES], st)
        xs = t.sbuf("xs", [TILE, DEPTH, DIM], st)
        bn_done, mv_done, step = t.sem("bn_done"), t.sem("mv_done"), t.sem("step")
        var_done, root_done = t.sem("var_done"), t.sem("root_done")
        scaled, turned, kept, copied = t.sem("scaled"), t.sem("turned"), t.sem("kept"), t.sem("copied")
        ident = t.w["ident"]

        with t.block() as block:
            @block.vector
            def _(dve):
                one = Steps(dve, step)
                with dve.Fori(0, TILES // 4) as i:
                    for u in range(4):
                        nc.vector.bn_stats(bn[:, bass.ds(4 * i + u, 1), :],
                                           src[:, bass.ds(4 * i + u, 1), :]).then_inc(bn_done, 1)
                dve.wait_ge(bn_done, TILES)
                for i in range(TILES):
                    nc.vector.bn_aggr(mv[:, i, :], bn[:, i, :]).then_inc(mv_done, 1)
                dve.wait_ge(mv_done, TILES)
                mean, var = mv[:, :, 0], mv[:, :, 1]
                if not centred:
                    one(nc.vector.tensor_tensor(sd[:, 2, :], mean, mean, ALU.mult))
                    one(nc.vector.tensor_tensor(sd[:, 3, :], sd[:, 2, :], var, ALU.add))
                    var = sd[:, 3, :]
                nc.vector.tensor_scalar(sd[:, 0, :], var, eps, None, ALU.add).then_inc(var_done, 1)
                dve.wait_ge(root_done, 1)
                one(nc.vector.reciprocal(sd[:, 2, :], sd[:, 1, :]))
                with dve.Fori(0, TILES // DEPTH) as i:
                    for u in range(DEPTH):
                        if feature_major:
                            dve.wait_ge(turned, DEPTH * i + u + 1)
                        if keep is not None:
                            dve.wait_ge(kept, DEPTH * i + u + 1)
                        at = bass.ds(DEPTH * i + u, 1)
                        if centred:
                            nc.vector.tensor_scalar(xs[:, u:u + 1, :], src[:, at, :], mv[:, at, 0:1], sd[:, 2, at],
                                                    ALU.subtract, ALU.mult).then_inc(scaled, 1)
                        else:
                            nc.vector.tensor_scalar(xs[:, u:u + 1, :], src[:, at, :], sd[:, 2, at], None,
                                                    ALU.mult).then_inc(scaled, 1)

            @block.gpsimd
            def _(pool):
                if keep is not None:
                    pool.sem_inc(kept, DEPTH)
                    with pool.Fori(0, TILES // DEPTH) as i:
                        for u in range(DEPTH):
                            pool.wait_ge(scaled, DEPTH * i + u + 1)
                            pool.sem_inc(t.passed, 1)
                            nc.gpsimd.tensor_copy(keep[:, bass.ds(DEPTH * i + u, 1), :], xs[:, u:u + 1, :]).then_inc(kept, 1)

            @block.scalar
            def _(act):
                act.wait_ge(var_done, 1)
                nc.scalar.activation(sd[:, 1, :], sd[:, 0, :], ACT.Sqrt).then_inc(root_done, 1)
                if feature_major:
                    act.sem_inc(copied, DEPTH)
                    with act.Fori(0, TILES // DEPTH) as i:
                        for u in range(DEPTH):
                            act.wait_ge(turned, DEPTH * (i + 1) + u + 1)
                            at = bass.ds(TILE * (DEPTH * i + u), TILE)
                            from_psum = t.bank[u][0:HALF, 0:2 * TILE].rearrange("p (k n) -> p k n", k=2)
                            if gain is None:
                                act.sem_inc(t.passed, 1)
                                nc.scalar.activation(t.xT[0:HALF, :, at], from_psum, ACT.Identity).then_inc(copied, 1)
                            else:
                                for k in range(2):
                                    act.sem_inc(t.passed, 1)
                                    last = nc.scalar.activation(
                                        t.xT[0:HALF, k:k + 1, at], from_psum[:, k:k + 1, :], ACT.Identity,
                                        scale=gain[0:HALF, k:k + 1], bias=bias[0:HALF, k:k + 1] if bias is not None else 0.0)
                                last.then_inc(copied, 1)

            @block.tensor
            def _(pe):
                if feature_major:
                    pe.sem_inc(turned, DEPTH)
                    with pe.Fori(0, TILES // DEPTH) as i:
                        for u in range(DEPTH):
                            pe.wait_ge(scaled, DEPTH * i + u + 1)
                            pe.wait_ge(copied, DEPTH * i + u + 1)
                            for k in range(2):
                                last = nc.tensor.transpose(t.bank[u][0:HALF, TILE * k:TILE * (k + 1)],
                                                           xs[:, u, HALF * k:HALF * (k + 1)], ident[0:TILE, 0:TILE])
                            last.then_inc(turned, 1)


def store(t, out, src):
    nc = t.nc
    stored = t.sem("out_stored")
    with t.block() as block:
        @block.sync
        def _(sp):
            sp.dma_start(out.rearrange("(t p) d -> p t d", p=TILE), src[:]).then_inc(stored, 16)
            sp.wait_ge(stored, 16)

def softplus(t, z):
    nc = t.nc
    SPAN = 2 * TILE
    SPANS = TOKENS // SPAN
    parts, groups = z.shape[0], z.shape[1]
    with ExitStack() as st:
        e, w, l, d = (t.sbuf(n, [parts, 2, groups, SPAN], st) for n in ("sp_e", "sp_w", "sp_ln", "sp_d"))
        abs_done, exp_done, w_done, ln_done = t.sem("abs_done"), t.sem("exp_done"), t.sem("w_done"), t.sem("ln_done")
        inv_done, step, merged, out_done = t.sem("inv_done"), t.sem("step"), t.sem("merged"), t.sem("out_done")
        with t.block() as block:
            @block.scalar
            def _(act):
                def exponential(c):
                    act.wait_ge(out_done, c + 1)
                    at = slice(SPAN * c, SPAN * (c + 1))
                    nc.scalar.activation(d[:, c % 2], z[:, :, at], ACT.Abs).then_inc(abs_done, 1)
                    act.wait_ge(abs_done, c + 1)
                    nc.scalar.activation(e[:, c % 2], d[:, c % 2], ACT.Exp, scale=-1.0).then_inc(exp_done, 1)

                nc.scalar.preload_act_table_set("natural_log_exp_and_others")
                exponential(0)
                for c in range(SPANS):
                    if c + 1 < SPANS:
                        exponential(c + 1)
                    act.wait_ge(w_done, c + 1)
                    nc.scalar.activation(l[:, c % 2], w[:, c % 2], ACT.Ln).then_inc(ln_done, 1)
                    act.wait_ge(ln_done, c + 1)
                    act.wait_ge(step, 2 * c + 1)
                    nc.scalar.activation(w[:, c % 2], l[:, c % 2], ACT.Exp, scale=-1.0).then_inc(inv_done, 1)

            @block.vector
            def _(dve):
                def widen(c):
                    dve.wait_ge(exp_done, c + 1)
                    v = c % 2
                    nc.vector.tensor_scalar(w[:, v], e[:, v], 1.0, None, ALU.add).then_inc(w_done, 1)
                    dve.wait_ge(w_done, c + 1)
                    nc.vector.scalar_tensor_tensor(d[:, v], w[:, v], -1.0, e[:, v], ALU.add, ALU.subtract).then_inc(step, 1)

                dve.sem_inc(out_done, 2)
                widen(0)
                for c in range(SPANS):
                    v = c % 2
                    zc = z[:, :, SPAN * c:SPAN * (c + 1)]
                    dve.wait_ge(inv_done, c + 1)
                    nc.vector.tensor_tensor(d[:, v], d[:, v], w[:, v], ALU.mult).then_inc(step, 1)
                    if c + 1 < SPANS:
                        widen(c + 1)
                    dve.wait_ge(step, 2 * c + 2)
                    nc.vector.tensor_tensor(l[:, v], l[:, v], d[:, v], ALU.subtract).then_inc(merged, 1)
                    dve.wait_ge(merged, c + 1)
                    nc.vector.scalar_tensor_tensor(zc, zc, 0.0, l[:, v], ALU.max, ALU.add).then_inc(out_done, 1)


STATES = 16


def scan(t, u, rate, coef, bc, direct, gain, y, bilinear):
    nc = t.nc
    parts, groups = u.shape[0], u.shape[1]
    jobs = STATES * groups
    SLOTS = 4
    by_vector = (lambda j: True) if bilinear else (lambda j: j % 12 == 11)
    before = lambda j, vector: sum(by_vector(i) == vector for i in range(j))
    jobs_until = lambda n, vector: before((n + 1) * groups, vector) if n >= 0 else (
        before(jobs + (n + 1) * groups, vector) - before(jobs, vector))
    with ExitStack() as st:
        thirds = t.sbuf("thirds", [6 * STATES, TOKENS], st, BF16)
        select = t.sbuf("select", [6 * STATES, 2 * STATES], st, BF16)
        with ExitStack() as inner:
            rest = t.sbuf("rest", [2 * STATES, TOKENS], inner)
            part = t.sbuf("part", [2 * STATES, TOKENS], inner, BF16)
            step = t.sem("step")
            with t.block() as block:
                @block.vector
                def _(dve):
                    one = Steps(dve, step)
                    nc.vector.tensor_copy(select[:], t.w["select"][:])
                    one(nc.vector.tensor_copy(thirds[0:2 * STATES, :], bc[0:2 * STATES, :]))
                    one(nc.vector.tensor_tensor(rest[:], bc[0:2 * STATES, :], thirds[0:2 * STATES, :], ALU.subtract))
                    one(nc.vector.tensor_copy(part[:], rest[:]))
                    nc.vector.tensor_copy(thirds[2 * STATES:4 * STATES, :], part[:])
                    one(nc.vector.tensor_tensor(rest[:], rest[:], part[:], ALU.subtract))
                    nc.vector.tensor_copy(thirds[4 * STATES:6 * STATES, :], rest[:])
        den_done, r_done, a_done, w1_done = t.sem("den_done"), t.sem("r_done"), t.sem("a_done"), t.sem("w1_done")
        w2_done, s_done, g_done, summed = t.sem("w2_done"), t.sem("s_done"), t.sem("g_done"), t.sem("summed")
        b_spread, spread, y_done, a_zero = t.sem("b_spread"), t.sem("spread"), t.sem("y_done"), t.sem("a_zero")
        a = t.sbuf("a", [parts, SLOTS, CHUNK // SEQ, SEQ], st)
        w2, s, g_ = (t.sbuf(n, [parts, SLOTS, CHUNK], st) for n in ("w2", "s", "g"))
        if bilinear:
            den, r, w1 = (t.sbuf(n, [parts, SLOTS, CHUNK], st) for n in ("den", "r", "w1"))
        else:
            spreadB = t.sbuf("spreadB", [parts, 2, CHUNK], st)
            b_copied, bu_done = t.sem("b_copied"), t.sem("bu_done")
            BACK = before(groups, False) + 1
        bankB, bankC, acc = t.bank[0:2], t.bank[2:4], t.bank[4:4 + groups]
        ident = t.w["ident"]

        with t.block() as block:
            @block.tensor
            def _(pe):
                pe.sem_inc(summed, SLOTS)
                with pe.Fori(0, CHUNKS) as c:
                    at = bass.ds(CHUNK * c, CHUNK)

                    def sum_states(j):
                        n, g = divmod(j, groups)
                        if j == 0:
                            pe.wait_ge(y_done, c + 1)
                        pe.wait_ge(g_done, c * jobs + j + 1 + SLOTS)
                        nc.tensor.matmul(acc[g][0:parts, 0:CHUNK], ident[0:parts, 0:parts], g_[:, j % SLOTS, :],
                                         start=(n == 0), stop=(n == STATES - 1)).then_inc(summed, 1)

                    def spread_row(bank, row):
                        return nc.tensor.matmul(bank[0:parts, 0:CHUNK], select[:, row:row + 1].to_broadcast([6 * STATES, parts]),
                                                thirds[:, at], start=True, stop=True)

                    def spread_b(n):
                        if not bilinear:
                            pe.wait_ge(b_copied, c * STATES + n + 1)
                        pe.wait_ge(w2_done, c * before(jobs, True) + jobs_until(n - 2, True) + SLOTS)
                        pe.sem_inc(t.passed, 1)
                        spread_row(bankB[n % 2], n).then_inc(b_spread, 1)

                    spread_b(0)
                    for n in range(STATES):
                        if n + 1 < STATES:
                            spread_b(n + 1)
                        pe.wait_ge(g_done, c * jobs + (n - 1) * groups + SLOTS)
                        pe.sem_inc(t.passed, 1)
                        spread_row(bankC[n % 2], STATES + n).then_inc(spread, 1)
                        if n:
                            for g in range(groups):
                                sum_states((n - 1) * groups + g)
                    for g in range(groups):
                        sum_states((STATES - 1) * groups + g)

            @block.scalar
            def _(act):
                act.wait_ge(a_zero, 1)
                for sem in (den_done, r_done, a_done):
                    act.sem_inc(sem, SLOTS)
                if not bilinear:
                    act.sem_inc(b_copied, 2)
                nc.scalar.preload_act_table_set("natural_log_exp_and_others")
                with act.Fori(0, CHUNKS) as c:
                    at = bass.ds(CHUNK * c, CHUNK)

                    def logarithm(j):
                        n, g = divmod(j, groups)
                        act.wait_ge(r_done, c * jobs + j + 1)
                        act.sem_inc(t.passed, 1)
                        nc.scalar.activation(den[:, j % SLOTS, :], rate[:, g, at], ACT.Ln,
                                             scale=coef[:, g, n:n + 1], bias=1.0).then_inc(den_done, 1)

                    def invert(j):
                        act.wait_ge(den_done, c * jobs + j + 1 + SLOTS)
                        act.wait_ge(a_done, c * jobs + j + 1)
                        act.wait_ge(w1_done, c * jobs + j + 1)
                        nc.scalar.activation(r[:, j % SLOTS, :], den[:, j % SLOTS, :], ACT.Exp, scale=-1.0).then_inc(r_done, 1)

                    def decay(j):
                        n, g = divmod(j, groups)
                        act.wait_ge(s_done, c * jobs + j + 1)
                        rest = a[:, j % SLOTS, :, 1:SEQ]
                        if bilinear:
                            act.wait_ge(r_done, c * jobs + j + 1 + SLOTS)
                            nc.scalar.activation(rest, r[:, j % SLOTS, :].rearrange("p (b t) -> p b t", t=SEQ)[:, :, 1:SEQ],
                                                 ACT.Identity, scale=2.0, bias=t.w["minus_one"][0:parts, :]).then_inc(a_done, 1)
                        else:
                            act.sem_inc(t.passed, 1)
                            nc.scalar.activation(rest, rate[:, g, at].rearrange("p (b t) -> p b t", t=SEQ)[:, :, 1:SEQ],
                                                 ACT.Exp, scale=coef[:, g, n:n + 1]).then_inc(a_done, 1)

                    if bilinear:
                        for j in range(jobs + 2):
                            if j < jobs:
                                logarithm(j)
                            if 0 < j <= jobs:
                                invert(j - 1)
                            if j >= 2:
                                decay(j - 2)
                    else:
                        def copy_b(n):
                            act.wait_ge(b_spread, c * STATES + n + 1)
                            act.wait_ge(bu_done, c * before(jobs, False) + jobs_until(n - 2, False) + BACK)
                            nc.scalar.activation(spreadB[:, n % 2, :], bankB[n % 2][0:parts, 0:CHUNK], ACT.Identity).then_inc(b_copied, 1)

                        copy_b(0)
                        for j in range(jobs):
                            if (j + 1) % groups == 0 and j + 1 < jobs:
                                copy_b((j + 1) // groups)
                            decay(j)

            @block.gpsimd
            def _(pool):
                if bilinear:
                    pool.sem_inc(w1_done, SLOTS)
                    with pool.Fori(0, CHUNKS) as c:
                        at = bass.ds(CHUNK * c, CHUNK)
                        for j in range(jobs):
                            pool.wait_ge(r_done, c * jobs + j + 1 + SLOTS)
                            pool.wait_ge(w2_done, c * jobs + j + 1)
                            pool.sem_inc(t.passed, 1)
                            nc.gpsimd.tensor_tensor(w1[:, j % SLOTS, :], u[:, j % groups, at], r[:, j % SLOTS, :],
                                                    ALU.mult).then_inc(w1_done, 1)
                else:
                    pool.sem_inc(bu_done, BACK)
                    with pool.Fori(0, CHUNKS) as c:
                        at = bass.ds(CHUNK * c, CHUNK)
                        for j in range(jobs):
                            if by_vector(j):
                                continue
                            n, g = divmod(j, groups)
                            pool.wait_ge(s_done, c * jobs + j + 1)
                            pool.wait_ge(b_copied, c * STATES + n + 3)
                            pool.sem_inc(t.passed, 1)
                            nc.gpsimd.tensor_tensor(w2[:, j % SLOTS, :], u[:, g, at], spreadB[:, n % 2, :],
                                                    ALU.mult).then_inc(bu_done, 1)

            @block.vector
            def _(dve):
                nc.vector.memset(a[:], 0.0).then_inc(a_zero, 1)
                for sem in (w2_done, s_done, g_done):
                    dve.sem_inc(sem, SLOTS)
                dve.sem_inc(y_done, 1)
                with dve.Fori(0, CHUNKS) as c:
                    at = bass.ds(CHUNK * c, CHUNK)

                    def weigh(j):
                        if bilinear:
                            dve.wait_ge(w1_done, c * jobs + j + 1 + SLOTS)
                        dve.wait_ge(b_spread, c * STATES + j // groups + 1)
                        src = w1[:, j % SLOTS, :] if bilinear else u[:, j % groups, at]
                        nc.vector.tensor_tensor(w2[:, j % SLOTS, :], src, bankB[j // groups % 2][0:parts, 0:CHUNK],
                                                ALU.mult).then_inc(w2_done, 1)

                    def recur(j):
                        if by_vector(j):
                            dve.wait_ge(w2_done, c * before(jobs, True) + before(j, True) + 1 + SLOTS)
                        else:
                            dve.wait_ge(bu_done, c * before(jobs, False) + before(j, False) + 1 + BACK)
                        dve.wait_ge(a_done, c * jobs + j + 1 + SLOTS)
                        nc.vector.tensor_tensor_scan(s[:, j % SLOTS, :], a[:, j % SLOTS, :, :].rearrange("p b t -> p (b t)"),
                                                     w2[:, j % SLOTS, :], 0.0, ALU.mult, ALU.add).then_inc(s_done, 1)

                    def read(j):
                        dve.wait_ge(s_done, c * jobs + j + 1 + SLOTS)
                        dve.wait_ge(spread, c * STATES + j // groups + 1)
                        nc.vector.tensor_tensor(g_[:, j % SLOTS, :], s[:, j % SLOTS, :],
                                                bankC[(j // groups) % 2][0:parts, 0:CHUNK], ALU.mult).then_inc(g_done, 1)

                    for j in range(jobs):
                        dve.wait_ge(summed, c * jobs + j + 1)
                        if by_vector(j):
                            weigh(j)
                        if not bilinear:
                            recur(j)
                        if j:
                            read(j - 1)
                        if bilinear:
                            recur(j)
                    read(jobs - 1)
                    dve.wait_ge(summed, c * jobs + jobs + SLOTS)
                    for g in range(groups):
                        last = nc.vector.scalar_tensor_tensor(y[:, g, at], direct[0:parts, g, at], gain[0:parts, g:g + 1],
                                                              acc[g][0:parts, 0:CHUNK], ALU.mult, ALU.add)
                    last.then_inc(y_done, 1)


def add_back(t, y, dst, weights=None):
    nc = t.nc
    parts, groups = y.shape[0], y.shape[1]
    with ExitStack() as st:
        ys = t.sbuf("ys", [parts, 2, groups, TILE], st)
        staged, turned, added = t.sem("staged"), t.sem("turned"), t.sem("added")
        with t.block() as block:
            @block.scalar
            def _(act):
                with act.Fori(0, TILES // 2) as i:
                    for v in range(2):
                        act.wait_ge(turned, 2 * i + v + 1)
                        act.sem_inc(t.passed, 1)
                        nc.scalar.activation(ys[:, v], y[:, :, bass.ds(TILE * (2 * i + v), TILE)],
                                             ACT.Identity).then_inc(staged, 1)

            @block.tensor
            def _(pe):
                pe.sem_inc(turned, 2)
                with pe.Fori(0, TILES // 2) as i:
                    for v in range(2):
                        pe.wait_ge(staged, 2 * i + v + 1)
                        pe.wait_ge(added, 2 * i + v + 1)
                        for g in range(groups):
                            if weights is None:
                                last = nc.tensor.transpose(t.bank[v][0:TILE, parts * g:parts * (g + 1)], ys[:, v, g, :],
                                                           t.w["ident"][0:parts, 0:parts])
                            else:
                                last = nc.tensor.matmul(t.bank[v][0:TILE, 0:DIM], ys[:, v, g, :], weights(g, i),
                                                        start=(g == 0), stop=(g == groups - 1))
                        last.then_inc(turned, 1)

            @block.vector
            def _(dve):
                dve.sem_inc(added, 2)
                with dve.Fori(0, TILES // 2) as i:
                    for v in range(2):
                        dve.wait_ge(turned, 2 * i + v + 3)
                        tile = dst[:, bass.ds(2 * i + v, 1), :]
                        nc.vector.tensor_tensor(tile, tile, t.bank[v][0:TILE, 0:DIM].unsqueeze(1), ALU.add).then_inc(added, 1)


CLAMP_LO, CLAMP_HI = 0.0001, 10.0
CENTRE, REACH = (CLAMP_HI + CLAMP_LO) / 2.0, (CLAMP_HI - CLAMP_LO) / 2.0
RANK = 48


def layer0_mixer(t):
    nc, w = t.nc, t.w
    normalise(t, t.h, 1e-5)
    with ExitStack() as st:
        bc = t.sbuf("bc", [2 * STATES, TOKENS], st)
        rate = t.sbuf("rate", [HALF, 2, TOKENS], st)
        u = t.sbuf("u", [HALF, 2, TOKENS], st)
        coef = t.sbuf("coef", [HALF, 2, STATES], st)
        low = t.sbuf("low", [RANK, TOKENS], st)
        mult, low_done, up, biased, coef_done = t.sem("mult"), t.sem("low_done"), t.sem("up"), t.sem("biased"), t.sem("coef_done")
        with t.block() as block:
            @block.tensor
            def _(pe):
                pe.sem_inc(low_done, 1)
                pe.sem_inc(biased, 1)
                with pe.Fori(0, CHUNKS) as c:
                    at = bass.ds(CHUNK * c, CHUNK)
                    pe.wait_ge(low_done, 2 * c + 1)
                    for k in range(2):
                        nc.tensor.matmul(t.bank[0][0:2 * STATES, 0:CHUNK], w["L0_W_bc"][:, k, :], t.xT[0:HALF, k, at],
                                         start=(k == 0), stop=(k == 1))
                    for k in range(2):
                        last = nc.tensor.matmul(t.bank[1][0:RANK, 0:CHUNK], w["L0_W_dt"][:, k, :], t.xT[0:HALF, k, at],
                                                start=(k == 0), stop=(k == 1))
                    last.then_inc(mult, 1)
                    pe.wait_ge(low_done, 2 * c + 3)
                    pe.wait_ge(biased, 2 * c + 1)
                    for k in range(2):
                        last = nc.tensor.matmul(t.bank[2 + k][0:HALF, 0:CHUNK], w["L0_W_dtp"][:, HALF * k:HALF * (k + 1)],
                                                low[:, at], start=True, stop=True)
                    last.then_inc(up, 1)

            @block.scalar
            def _(act):
                act.sem_inc(t.passed, 1)
                nc.scalar.activation(coef[:], w["L0_A_log"][:], ACT.Exp).then_inc(coef_done, 1)
                with act.Fori(0, CHUNKS) as c:
                    at = bass.ds(CHUNK * c, CHUNK)
                    act.wait_ge(mult, c + 1)
                    act.sem_inc(t.passed, 1)
                    nc.scalar.activation(bc[:, at], t.bank[0][0:2 * STATES, 0:CHUNK], ACT.Identity).then_inc(low_done, 1)
                    act.sem_inc(t.passed, 1)
                    nc.scalar.activation(low[:, at], t.bank[1][0:RANK, 0:CHUNK], ACT.Identity).then_inc(low_done, 1)

            @block.vector
            def _(dve):
                dve.wait_ge(coef_done, 1)
                nc.vector.tensor_scalar(coef[:], coef[:], 0.5, None, ALU.mult)
                with dve.Fori(0, CHUNKS) as c:
                    at = bass.ds(CHUNK * c, CHUNK)
                    dve.wait_ge(up, c + 1)
                    for k in range(2):
                        nc.vector.tensor_scalar(rate[:, k, at], t.bank[2 + k][0:HALF, 0:CHUNK],
                                                w["L0_b_dt"][:, k:k + 1], None, ALU.add).then_inc(biased, 1)
        softplus(t, rate)
        with ExitStack() as inner:
            sq = t.sbuf("sq", [HALF, 2, TOKENS], inner)
            rms = t.sbuf("rms", [HALF, 2, CHUNK], inner)
            squared, meant, eps_done, root, inv = t.sem("squared"), t.sem("meant"), t.sem("eps_done"), t.sem("root"), t.sem("inv")
            scaled, tanh_done, clamped, rooted, summed = t.sem("scaled"), t.sem("tanh_done"), t.sem("clamped"), t.sem("rooted"), t.sem("summed")
            with t.block() as block:
                @block.scalar
                def _(act):
                    nc.scalar.preload_act_table(ACT.Sqrt)
                    with act.Fori(0, CHUNKS) as c:
                        at = bass.ds(CHUNK * c, CHUNK)
                        act.sem_inc(t.passed, 1)
                        nc.scalar.activation(sq[:, :, at], rate[:, :, at], ACT.Square).then_inc(squared, 1)
                        act.wait_ge(eps_done, c + 1)
                        nc.scalar.activation(rms[:, 1, :], rms[:, 0, :], ACT.Sqrt).then_inc(root, 1)
                    act.wait_ge(scaled, 2 * CHUNKS)
                    nc.scalar.activation(sq[:], rate[:], ACT.Tanh, scale=1.0 / REACH,
                                         bias=w["clamp"][0:HALF, :]).then_inc(tanh_done, 1)
                    act.wait_ge(clamped, 1)
                    nc.scalar.activation(sq[:], rate[:], ACT.Sqrt).then_inc(rooted, 1)

                @block.tensor
                def _(pe):
                    with pe.Fori(0, CHUNKS) as c:
                        at = bass.ds(CHUNK * c, CHUNK)
                        pe.wait_ge(squared, c + 1)
                        for k in range(2):
                            last = nc.tensor.matmul(t.bank[0][0:HALF, 0:CHUNK], w["mean"][:], sq[:, k, at],
                                                    start=(k == 0), stop=(k == 1))
                        last.then_inc(meant, 1)

                @block.vector
                def _(dve):
                    for k in range(2):
                        xk = t.xT[0:HALF, k, 0:TOKENS].rearrange("p (b t) -> p b t", t=SEQ)
                        uk = u[:, k, :].rearrange("p (b t) -> p b t", t=SEQ)
                        nc.vector.tensor_tensor(uk[:, :, 1:SEQ], xk[:, :, 1:SEQ], xk[:, :, 0:SEQ - 1], ALU.add).then_inc(summed, 1)
                        nc.vector.tensor_copy(uk[:, :, 0:1], xk[:, :, 0:1]).then_inc(summed, 1)
                    with dve.Fori(0, CHUNKS) as c:
                        at = bass.ds(CHUNK * c, CHUNK)
                        dve.wait_ge(meant, c + 1)
                        nc.vector.tensor_scalar(rms[:, 0, :], t.bank[0][0:HALF, 0:CHUNK], 1e-6, None, ALU.add).then_inc(eps_done, 1)
                        dve.wait_ge(root, c + 1)
                        nc.vector.reciprocal(rms[:, 1, :], rms[:, 1, :]).then_inc(inv, 1)
                        dve.wait_ge(inv, c + 1)
                        for k in range(2):
                            nc.vector.scalar_tensor_tensor(rate[:, k, at], rate[:, k, at], w["L0_rms"][:, k:k + 1],
                                                           rms[:, 1, :], ALU.mult, ALU.mult).then_inc(scaled, 1)
                        dve.wait_ge(scaled, 2 * c + 2)
                    dve.wait_ge(tanh_done, 1)
                    nc.vector.tensor_scalar(rate[:], sq[:], REACH, CENTRE, ALU.mult, ALU.add).then_inc(clamped, 1)
                    dve.wait_ge(rooted, 1)
                    dve.wait_ge(summed, 4)
                    nc.vector.scalar_tensor_tensor(flat(u[:]), flat(u[:]), 0.5, flat(sq[:]), ALU.mult, ALU.mult)
        y = rate
        scan(t, u, rate, coef, bc, t.xT, w["L0_D"], y, bilinear=True)
        add_back(t, y, t.h)

def route(t, lhs, gate, experts, picks, masks=None, weights=None, total=None, probs=None):
    nc = t.nc
    size = [TILE, TILES, experts]
    with ExitStack() as st:
        logits, ex, eq, chosen = (t.sbuf(n, size, st) for n in ("logits", "ex", "eq", "chosen"))
        top, best = t.sbuf("top", [TILE, TILES], st), t.sbuf("best", [TILE, TILES], st)
        own = t.sbuf("own", size, st)
        multiplied, shifted, exp_done, step = t.sem("multiplied"), t.sem("shifted"), t.sem("exp_done"), t.sem("step")
        spread = lambda v: v[:].unsqueeze(2).to_broadcast(size)
        first = t.w["first"][0:TILE, 0:experts].unsqueeze(1).to_broadcast(size)
        with t.block() as block:
            @block.tensor
            def _(pe):
                for i in range(TILES):
                    for k in range(len(gate)):
                        last = nc.tensor.matmul(t.bank[0][0:TILE, experts * i:experts * (i + 1)], lhs(i, k), gate[k],
                                                start=(k == 0), stop=(k == len(gate) - 1))
                last.then_inc(multiplied, 1)

            @block.scalar
            def _(act):
                act.wait_ge(shifted, 1)
                nc.scalar.activation(ex[:], own[:], ACT.Exp).then_inc(exp_done, 1)

            @block.vector
            def _(dve):
                one = Steps(dve, step)
                dve.wait_ge(multiplied, 1)
                one(nc.vector.tensor_copy(flat(logits[:]), t.bank[0][0:TILE, 0:TILES * experts]))
                one(nc.vector.tensor_reduce(top[:], logits[:], AX.X, ALU.max))
                nc.vector.tensor_tensor(own[:], logits[:], spread(top), ALU.subtract).then_inc(shifted, 1)
                for j in range(picks):
                    if j:
                        one(nc.vector.scalar_tensor_tensor(flat(logits[:]), flat(mask[:]), MASKED, flat(logits[:]), ALU.mult, ALU.add))
                        one(nc.vector.tensor_reduce(top[:], logits[:], AX.X, ALU.max))
                    mask = masks[j] if masks else (chosen if j == 0 else eq)
                    one(nc.vector.tensor_tensor(eq[:], logits[:], spread(top), ALU.is_equal))
                    one(nc.vector.tensor_tensor(eq[:], eq[:], first, ALU.mult))
                    one(nc.vector.tensor_reduce(best[:], eq[:], AX.X, ALU.max))
                    one(nc.vector.tensor_tensor(mask[:], eq[:], spread(best), ALU.is_equal))
                    if weights is not None and masks and j == 0:
                        one(nc.vector.tensor_copy(chosen[:], mask[:]))
                    elif weights is not None and j:
                        one(nc.vector.tensor_tensor(chosen[:], chosen[:], mask[:], ALU.add))
                dve.wait_ge(exp_done, 1)
                if total is not None:
                    one(nc.vector.tensor_reduce(best[:], ex[:], AX.X, ALU.add))
                    one(nc.vector.reciprocal(total[:], best[:]))
                if probs is not None:
                    one(nc.vector.tensor_tensor(probs[:], ex[:], spread(total), ALU.mult))
                if weights is not None:
                    one(nc.vector.tensor_tensor(ex[:], ex[:], chosen[:], ALU.mult))
                    one(nc.vector.tensor_reduce(best[:], ex[:], AX.X, ALU.add))
                    one(nc.vector.reciprocal(top[:], best[:]))
                    one(nc.vector.tensor_tensor(weights[:], ex[:], spread(top), ALU.mult))


def turn(t, src, dst):
    nc = t.nc
    n = src.shape[2]
    turned = t.sem("turned")
    with t.block() as block:
        @block.tensor
        def _(pe):
            for i in range(TILES):
                nc.tensor.transpose(t.bank[i // 4][0:n, TILE * (i % 4):TILE * (i % 4 + 1)], src[:, i, :],
                                    t.w["ident"][0:TILE, 0:TILE]).then_inc(turned, 1)

        @block.scalar
        def _(act):
            for c in range(CHUNKS):
                act.wait_ge(turned, 4 * c + 4)
                nc.scalar.activation(dst[:, CHUNK * c:CHUNK * (c + 1)], t.bank[c][0:n, 0:CHUNK], ACT.Identity)


L0_CODE, L0_EXPERTS = 64, 8
L0_GROUPS = L0_CODE * L0_EXPERTS // 128


def layer0_ffn(t):
    nc, w = t.nc, t.w
    normalise(t, t.h, 1e-5)
    with ExitStack() as st:
        code = t.sbuf("code", [L0_CODE + 1, TOKENS], st)
        mask = t.sbuf("mask", [TILE, TILES, L0_EXPERTS], st)
        prob = t.sbuf("prob", [TILE, TILES], st)
        gate = t.sbuf("gate", [L0_EXPERTS, 1, TOKENS], st)
        up = t.sbuf("up", [128, L0_GROUPS, CHUNK], st)
        picked = t.sbuf("picked", [128, L0_GROUPS, CHUNK], st)
        ones_done, encoded, code_done = t.sem("ones_done"), t.sem("encoded"), t.sem("code_done")
        with t.block() as block:
            @block.vector
            def _(dve):
                nc.vector.memset(code[L0_CODE:L0_CODE + 1, :], 1.0).then_inc(ones_done, 1)

            @block.tensor
            def _(pe):
                for c in range(CHUNKS):
                    at = slice(CHUNK * c, CHUNK * (c + 1))
                    nc.tensor.matmul(t.bank[c][0:L0_CODE, 0:CHUNK], w["L0_enc"][:, 0, :], t.xT[:, 0, at], start=True, stop=False)
                    nc.tensor.matmul(t.bank[c][0:L0_CODE, 0:CHUNK], w["L0_enc"][0:HALF, 1, :], t.xT[0:HALF, 1, at],
                                     start=False, stop=True).then_inc(encoded, 1)

            @block.scalar
            def _(act):
                for c in range(CHUNKS):
                    act.wait_ge(encoded, c + 1)
                    nc.scalar.activation(code[0:L0_CODE, CHUNK * c:CHUNK * (c + 1)], t.bank[c][0:L0_CODE, 0:CHUNK],
                                         ACT.Identity).then_inc(code_done, 1)
        route(t, lambda i, k: code[:, TILE * i:TILE * (i + 1)], [w["L0_switch"][:]], L0_EXPERTS, 1, masks=[mask], total=prob)
        masked = t.sem("masked")
        with t.block() as block:
            @block.vector
            def _(dve):
                nc.vector.tensor_tensor(mask[:], mask[:], prob[:].unsqueeze(2).to_broadcast([TILE, TILES, L0_EXPERTS]),
                                        ALU.mult).then_inc(masked, 1)
        turn(t, mask, gate[:, 0, :])
        up_done, act_done, spread, pick_done, down, added = (
            t.sem(n) for n in ("up_done", "act_done", "spread", "pick_done", "down", "added"))
        G = L0_GROUPS
        with t.block() as block:
            @block.tensor
            def _(pe):
                pe.sem_inc(down, 4)
                with pe.Fori(0, CHUNKS) as c:
                    at = bass.ds(CHUNK * c, CHUNK)
                    pe.wait_ge(act_done, c * G + G)
                    for m in range(G):
                        for k in range(2):
                            last = nc.tensor.matmul(t.bank[m][:, 0:CHUNK], w["L0_w1"][:, k, 128 * m:128 * (m + 1)],
                                                    t.xT[0:HALF, k, at], start=(k == 0), stop=(k == 1))
                        last.then_inc(up_done, 1)
                    for m in range(G):
                        pe.wait_ge(pick_done, c * G + m + 3)
                        pe.sem_inc(t.passed, 1)
                        nc.tensor.matmul(t.bank[4 + m % 2][:, 0:CHUNK], w["L0_pair"][:, m, :], gate[:, 0, at],
                                         start=True, stop=True).then_inc(spread, 1)
                    pe.wait_ge(pick_done, c * G + G + 4)
                    for j in range(4):
                        pe.wait_ge(added, 4 * c + j + 1)
                        for m in range(G):
                            last = nc.tensor.matmul(t.bank[6 + j % 2][0:TILE, 0:DIM], picked[:, m, TILE * j:TILE * (j + 1)],
                                                    w["L0_w2"][:, m, :], start=(m == 0), stop=(m == G - 1))
                        last.then_inc(down, 1)

            @block.scalar
            def _(act):
                act.sem_inc(act_done, G)
                nc.scalar.preload_act_table(ACT.Gelu)
                with act.Fori(0, CHUNKS) as c:
                    for m in range(G):
                        act.wait_ge(up_done, c * G + m + 1)
                        act.wait_ge(pick_done, c * G + m + 1)
                        nc.scalar.activation(up[:, m, :], t.bank[m][:, 0:CHUNK], ACT.Gelu,
                                             bias=w["L0_b1"][:, m:m + 1]).then_inc(act_done, 1)

            @block.vector
            def _(dve):
                dve.sem_inc(pick_done, G)
                dve.sem_inc(added, 2)
                with dve.Fori(0, CHUNKS) as c:
                    dve.wait_ge(down, 4 * c + 4)
                    for m in range(G):
                        dve.wait_ge(act_done, c * G + m + 1 + G)
                        dve.wait_ge(spread, c * G + m + 1)
                        nc.vector.tensor_tensor(picked[:, m, :], up[:, m, :], t.bank[4 + m % 2][:, 0:CHUNK],
                                                ALU.mult).then_inc(pick_done, 1)
                    for j in range(4):
                        dve.wait_ge(down, 4 * c + j + 1 + 4)
                        tile = t.h[:, bass.ds(4 * c + j, 1), :]
                        nc.vector.tensor_tensor(tile, tile, t.bank[6 + j % 2][0:TILE, 0:DIM].unsqueeze(1), ALU.add).then_inc(added, 1)
        add_back(t, gate, t.h, lambda g, i: w["L0_b2"][:, g, :])


def layer1_mixer(t):
    nc, w = t.nc, t.w
    normalise(t, t.h, 1e-5)
    with ExitStack() as st:
        x = t.sbuf("xtile", [HALF + 1, 2, 2, TILE], st)
        qk = t.sbuf("qk", [HALF, 2, 4, TILE], st)
        v_ = t.sbuf("v", [TILE, 2, DIM], st)
        s = t.sbuf("scores", [TILE, 2, TILE], st)
        p = t.sbuf("probs", [TILE, 2, TILE], st)
        pT = t.sbuf("probsT", [TILE, 2, TILE], st)
        low, tot = t.sbuf("low", [TILE, 2], st), t.sbuf("tot", [TILE, 2], st)
        inv = t.sbuf("inv", [TILE, 2], st)
        staged, projected, qk_done, v_done, scored, masked, low_done, exp_done, turned, pT_done, out_done, inv_done, added = (
            t.sem(n) for n in ("staged", "projected", "qk_done", "v_done", "scored", "masked", "low_done", "exp_done",
                               "turned", "pT_done", "out_done", "inv_done", "added"))
        bankP, bankV, bankS = t.bank[0:2], t.bank[2:4], t.bank[4:6]
        with t.block() as block:
            @block.gpsimd
            def _(pool):
                with pool.Fori(0, TILES // 2) as i:
                    for u in range(2):
                        pool.wait_ge(projected, 2 * i + u + 1)
                        pool.sem_inc(t.passed, 1)
                        nc.gpsimd.tensor_copy(x[:, u], t.xT[:, :, bass.ds(TILE * (2 * i + u), TILE)]).then_inc(staged, 1)

            @block.tensor
            def _(pe):
                pe.sem_inc(projected, 2)
                with pe.Fori(0, TILES // 2) as i:
                    n = lambda u: 2 * i + u + 1
                    for u in range(2):
                        pe.wait_ge(staged, n(u))
                        pe.wait_ge(added, n(u))
                        for m in range(4):
                            nc.tensor.matmul(bankP[u][0:HALF, TILE * m:TILE * (m + 1)], w["L1_wqk"][:, 0, HALF * m:HALF * (m + 1)],
                                             x[:, u, 0, :], start=True, stop=False)
                            nc.tensor.matmul(bankP[u][0:HALF, TILE * m:TILE * (m + 1)], w["L1_wqk"][0:HALF, 1, HALF * m:HALF * (m + 1)],
                                             x[0:HALF, u, 1, :], start=False, stop=True)
                        nc.tensor.matmul(bankV[u][0:TILE, 0:DIM], x[:, u, 0, :], w["L1_wv"][:, 0, :], start=True, stop=False)
                        nc.tensor.matmul(bankV[u][0:TILE, 0:DIM], x[0:HALF, u, 1, :], w["L1_wv"][0:HALF, 1, :],
                                         start=False, stop=True).then_inc(projected, 1)
                    for u in range(2):
                        pe.wait_ge(qk_done, n(u))
                        for k in range(2):
                            last = nc.tensor.matmul(bankS[u][0:TILE, 0:TILE], qk[:, u, k, :], qk[:, u, 2 + k, :],
                                                    start=(k == 0), stop=(k == 1))
                        last.then_inc(scored, 1)
                    for u in range(2):
                        pe.wait_ge(exp_done, n(u))
                        nc.tensor.transpose(bankP[u][0:TILE, 0:TILE], p[:, u, :], w["ident"][0:TILE, 0:TILE]).then_inc(turned, 1)
                    for u in range(2):
                        pe.wait_ge(pT_done, n(u))
                        pe.wait_ge(v_done, n(u))
                        nc.tensor.matmul(bankS[u][0:TILE, TILE:TILE + DIM], pT[:, u, :], v_[:, u, :],
                                         start=True, stop=True).then_inc(out_done, 1)

            @block.scalar
            def _(act):
                nc.scalar.preload_act_table(ACT.Exp)
                with act.Fori(0, TILES // 2) as i:
                    n = lambda u: 2 * i + u + 1
                    for u in range(2):
                        act.wait_ge(projected, n(u) + 2)
                        nc.scalar.activation(qk[:, u], bankP[u][0:HALF, 0:4 * TILE].rearrange("p (m n) -> p m n", m=4),
                                             ACT.Identity).then_inc(qk_done, 1)
                    for u in range(2):
                        act.wait_ge(low_done, n(u))
                        nc.scalar.activation(p[:, u, :], s[:, u, :], ACT.Exp, bias=low[:, u:u + 1],
                                             accum_out=tot[:, u:u + 1]).then_inc(exp_done, 1)
                    for u in range(2):
                        act.wait_ge(turned, n(u))
                        nc.scalar.activation(pT[:, u, :], bankP[u][0:TILE, 0:TILE], ACT.Identity).then_inc(pT_done, 1)

            @block.vector
            def _(dve):
                dve.sem_inc(added, 2)
                with dve.Fori(0, TILES // 2) as i:
                    n = lambda u: 2 * i + u + 1
                    for u in range(2):
                        dve.wait_ge(projected, n(u) + 2)
                        nc.vector.tensor_copy(v_[:, u, :], bankV[u][0:TILE, 0:DIM]).then_inc(v_done, 1)
                    for u in range(2):
                        dve.wait_ge(scored, n(u))
                        nc.vector.scalar_tensor_tensor(s[:, u, :], bankS[u][0:TILE, 0:TILE], DIM ** -0.5,
                                                       w["mask"][:], ALU.mult, ALU.add).then_inc(masked, 1)
                    for u in range(2):
                        dve.wait_ge(masked, n(u))
                        nc.vector.tensor_reduce(low[:, u:u + 1], s[:, u, :], AX.X, ALU.max, negate=True).then_inc(low_done, 1)
                    for u in range(2):
                        dve.wait_ge(exp_done, n(u))
                        nc.vector.reciprocal(inv[:, u:u + 1], tot[:, u:u + 1]).then_inc(inv_done, 1)
                    for u in range(2):
                        dve.wait_ge(inv_done, n(u))
                        dve.wait_ge(out_done, n(u))
                        tile = t.h[:, bass.ds(2 * i + u, 1), :]
                        nc.vector.scalar_tensor_tensor(tile, bankS[u][0:TILE, TILE:TILE + DIM].unsqueeze(1), inv[:, u:u + 1],
                                                       tile, ALU.mult, ALU.add).then_inc(added, 1)


def heads_attention(t, wqkv, wproj, dst, unit):
    nc, w = t.nc, t.w
    GROUPS = HEADS // 4
    with ExitStack() as st:
        x = t.sbuf("xtile", [HALF + 1, 2, 2, TILE], st)
        wide = t.sbuf("wide", [TILE, 2, 2 * HEADS, 2 * HEAD], st)
        sq = t.sbuf("sq", [TILE, 2, 2 * HEADS * HEAD], st)
        norm = t.sbuf("norm", [TILE, 2, 3, 2 * HEADS], st)
        v_ = t.sbuf("v", [TILE, 2, DIM], st)
        qkT = t.sbuf("qkT", [128, 2, 2 * GROUPS, TILE], st)
        s = t.sbuf("scores", [TILE, 2, HEADS, TILE], st)
        pT = t.sbuf("probsT", [TILE, HEADS, TILE], st)
        red = t.sbuf("red", [TILE, 2, 3, HEADS], st)
        a = t.sbuf("a", [TILE, 2, DIM], st)
        aT = t.sbuf("aT", [HALF + 1, 2, 2, TILE], st)
        names = ("zeroed", "ones_done", "staged", "projected", "squared", "summed", "logged", "rooted", "q_done", "v_done", "turned", "qkT_done",
                 "scored", "masked", "max_done", "shifted", "exp_done", "probs_turned", "pT_done", "weighed",
                 "a_done", "a_turned", "aT_done", "out_done", "added", "step", "front_step")
        (zeroed, ones_done, staged, projected, squared, summed, logged, rooted, q_done, v_done, turned, qkT_done, scored, masked, max_done,
         shifted, exp_done, probs_turned, pT_done, weighed, a_done, a_turned, aT_done, out_done, added, step, front_step) = (
            t.sem(n) for n in names)
        bankQ, bankV, bankK, bankO, bankS = t.bank[0], t.bank[1], t.bank[2], t.bank[3], t.bank[4:8]
        bankT = (bankQ, bankK)
        ident = w["ident"]
        with t.block() as block:
            @block.gpsimd
            def _(pool):
                nc.gpsimd.memset(wide[:], 0.0).then_inc(zeroed, 1)

                def stage(n, v):
                    nc.gpsimd.tensor_copy(x[:, v], t.xT[:, :, bass.ds(TILE * n, TILE)]).then_inc(staged, 1)

                def shift(n, v):
                    pool.wait_ge(max_done, n + 1)
                    nc.gpsimd.tensor_tensor(s[:, v], s[:, v], red[:, v, 0, :].unsqueeze(2).to_broadcast([TILE, HEADS, TILE]),
                                            ALU.subtract).then_inc(shifted, 1)

                pool.wait_ge(zeroed, 1)
                stage(0, 0)
                stage(1, 1)
                shift(0, 0)
                with pool.Fori(0, TILES // 2) as i:
                    for u in range(2):
                        n = 2 * i + u
                        pool.wait_ge(projected, n + 2)
                        pool.sem_inc(t.passed, 1)
                        stage(n + 2, u)
                        shift(n + 1, 1 - u)

            @block.tensor
            def _(pe):
                pe.sem_inc(projected, 1)
                pe.wait_ge(zeroed, 1)
                pe.wait_ge(ones_done, 1)

                def project(v):
                    for bank, lo, hi in ((bankQ, 0, 2 * DIM), (bankV, 2 * DIM, 3 * DIM)):
                        nc.tensor.matmul(bank[0:TILE, 0:hi - lo], x[:, v, 0, :], wqkv[:, 0, lo:hi], start=True, stop=False)
                        last = nc.tensor.matmul(bank[0:TILE, 0:hi - lo], x[0:HALF, v, 1, :], wqkv[0:HALF, 1, lo:hi],
                                                start=False, stop=True)
                    last.then_inc(projected, 1)

                def turn_qk(v):
                    for g in range(2 * GROUPS):
                        last = nc.tensor.transpose(bankT[g // GROUPS][:, TILE * (g % GROUPS):TILE * (g % GROUPS + 1)],
                                                   wide[:, v, 4 * g:4 * g + 4, :].rearrange("p h e -> p (h e)"),
                                                   ident[0:TILE, 0:TILE])
                    last.then_inc(turned, 1)

                def score(v):
                    for g in range(GROUPS):
                        for j in range(4):
                            rows = slice(32 * j, 32 * j + HEAD)
                            last = nc.tensor.matmul(bankS[j][0:TILE, TILE * g:TILE * (g + 1)], qkT[rows, v, g, :],
                                                    qkT[rows, v, GROUPS + g, :], start=True, stop=True)
                    last.then_inc(scored, 1)

                pe.wait_ge(staged, 1)
                project(0)
                pe.wait_ge(q_done, 1)
                turn_qk(0)
                pe.wait_ge(qkT_done, 1)
                score(0)
                pe.wait_ge(staged, 2)
                pe.wait_ge(v_done, 1)
                project(1)
                pe.wait_ge(q_done, 2)
                turn_qk(1)
                with pe.Fori(0, TILES // 2) as i:
                    for u in range(2):
                        n = 2 * i + u
                        pe.wait_ge(qkT_done, n + 2)
                        pe.wait_ge(masked, 4 * n + 4)
                        pe.wait_ge(pT_done, 3 * n + 3)
                        score(1 - u)
                        pe.wait_ge(staged, n + 3)
                        pe.wait_ge(v_done, n + 2)
                        project(u)
                        pe.wait_ge(exp_done, n + 1)
                        pe.wait_ge(masked, 4 * n + 8)
                        for g in range(GROUPS):
                            for j in range(4):
                                last = nc.tensor.transpose(bankS[g][0:TILE, TILE * j:TILE * (j + 1)], s[:, u, 4 * g + j, :],
                                                           ident[0:TILE, 0:TILE])
                            last.then_inc(probs_turned, 1)
                        if not unit:
                            pe.wait_ge(q_done, n + 3)
                            turn_qk(u)
                        pe.wait_ge(added, n + 1)
                        for g in range(GROUPS):
                            pe.wait_ge(pT_done, 3 * n + 3 + g + 1)
                            for j in range(4):
                                head = slice(HEAD * (4 * g + j), HEAD * (4 * g + j + 1))
                                last = nc.tensor.matmul(bankO[0:TILE, head], pT[:, 4 * g + j, :], v_[:, u, head], start=True, stop=True)
                        last.then_inc(weighed, 1)
                        if unit:
                            pe.wait_ge(q_done, n + 3)
                            turn_qk(u)
                        pe.wait_ge(a_done, n + 1)
                        for k in range(2):
                            last = nc.tensor.transpose(bankO[0:HALF, DIM + TILE * k:DIM + TILE * (k + 1)],
                                                       a[:, u, HALF * k:HALF * (k + 1)], ident[0:TILE, 0:TILE])
                        last.then_inc(a_turned, 1)
                        pe.wait_ge(aT_done, n + 1)
                        nc.tensor.matmul(bankO[0:TILE, 0:DIM], aT[:, u, 0, :], wproj[:, 0, :], start=True, stop=False)
                        nc.tensor.matmul(bankO[0:TILE, 0:DIM], aT[0:HALF, u, 1, :], wproj[0:HALF, 1, :],
                                         start=False, stop=True).then_inc(out_done, 1)

            @block.scalar
            def _(act):
                act.sem_inc(pT_done, 3)
                nc.scalar.preload_act_table_set("natural_log_exp_and_others")

                def square(n, v):
                    if unit:
                        act.wait_ge(projected, n + 2)
                        nc.scalar.activation(sq[:, v, :], bankQ[0:TILE, 0:2 * DIM], ACT.Square).then_inc(squared, 1)

                def root(n, v):
                    if unit:
                        act.wait_ge(summed, n + 1)
                        nc.scalar.activation(norm[:, v, 2, :], norm[:, v, 0, :], ACT.Ln).then_inc(logged, 1)
                        act.wait_ge(logged, n + 1)
                        nc.scalar.activation(norm[:, v, 1, :], norm[:, v, 2, :], ACT.Exp, scale=-0.5).then_inc(rooted, 1)

                def take_qkT(n, v):
                    act.wait_ge(turned, n + 1)
                    for half in range(2):
                        last = nc.scalar.activation(qkT[:, v, GROUPS * half:GROUPS * (half + 1), :],
                                                    bankT[half][:, 0:GROUPS * TILE].rearrange("p (g n) -> p g n", g=GROUPS),
                                                    ACT.Identity)
                    last.then_inc(qkT_done, 1)

                def exponents(n, v):
                    act.wait_ge(shifted, n + 1)
                    nc.scalar.activation(s[:, v], s[:, v], ACT.Exp).then_inc(exp_done, 1)

                square(0, 0)
                root(0, 0)
                take_qkT(0, 0)
                square(1, 1)
                root(1, 1)
                take_qkT(1, 1)
                exponents(0, 0)
                with act.Fori(0, TILES // 2) as i:
                    for u in range(2):
                        n = 2 * i + u
                        square(n + 2, u)
                        act.wait_ge(weighed, n + 1)
                        for g in range(GROUPS):
                            act.wait_ge(probs_turned, 3 * n + g + 1)
                            nc.scalar.activation(pT[:, 4 * g:4 * g + 4, :], bankS[g][0:TILE, 0:4 * TILE].rearrange("p (j n) -> p j n", j=4),
                                                 ACT.Identity).then_inc(pT_done, 1)
                        root(n + 2, u)
                        take_qkT(n + 2, u)
                        act.wait_ge(a_turned, n + 1)
                        nc.scalar.activation(aT[0:HALF, u], bankO[0:HALF, DIM:DIM + 2 * TILE].rearrange("p (k n) -> p k n", k=2),
                                             ACT.Identity).then_inc(aT_done, 1)
                        exponents(n + 1, 1 - u)

            @block.vector
            def _(dve):
                narrow = bankQ[0:TILE, 0:2 * DIM].rearrange("p (h e) -> p h e", e=HEAD)
                dve.sem_inc(added, 1)
                dve.sem_inc(weighed, 1)
                nc.vector.memset(aT[HALF:HALF + 1], 1.0).then_inc(ones_done, 1)
                dve.wait_ge(zeroed, 1)

                def lengths(n, v):
                    if unit:
                        dve.wait_ge(squared, n + 1)
                        nc.vector.tensor_reduce(norm[:, v, 2, :], sq[:, v, :].rearrange("p (h e) -> p h e", e=HEAD),
                                                AX.X, ALU.add).then_inc(front_step, 1)
                        dve.wait_ge(front_step, 2 * n + 1)
                        nc.vector.tensor_scalar(norm[:, v, 0, :], norm[:, v, 2, :], 1e-24, None, ALU.max).then_inc(summed, 1)

                def take_qk(n, v):
                    if unit:
                        dve.wait_ge(rooted, n + 1)
                        nc.vector.tensor_tensor(norm[:, v, 1, 0:HEADS], norm[:, v, 1, 0:HEADS], w["L2_scale"][:],
                                                ALU.mult).then_inc(front_step, 1)
                        dve.wait_ge(front_step, 2 * n + 2)
                        nc.vector.tensor_tensor(wide[:, v, :, 0:HEAD], narrow,
                                                norm[:, v, 1, :].unsqueeze(2).to_broadcast([TILE, 2 * HEADS, HEAD]),
                                                ALU.mult).then_inc(q_done, 1)
                    else:
                        dve.wait_ge(projected, n + 2)
                        nc.vector.tensor_copy(wide[:, v, :, 0:HEAD], narrow).then_inc(q_done, 1)

                def take_v(v):
                    nc.vector.tensor_copy(v_[:, v, :], bankV[0:TILE, 0:DIM]).then_inc(v_done, 1)

                def highest(n, v):
                    dve.wait_ge(scored, n + 1)
                    for j in range(4):
                        nc.vector.scalar_tensor_tensor(
                            s[:, v].rearrange("p (g j) n -> p j g n", j=4)[:, j], bankS[j][0:TILE, 0:GROUPS * TILE]
                            .rearrange("p (g n) -> p g n", g=GROUPS), 1.0 if unit else HEAD ** -0.5,
                            w["mask"][:].unsqueeze(1).to_broadcast([TILE, GROUPS, TILE]), ALU.mult, ALU.add).then_inc(masked, 1)
                    dve.wait_ge(masked, 4 * n + 4)
                    nc.vector.tensor_reduce(red[:, v, 0, :], s[:, v], AX.X, ALU.max).then_inc(max_done, 1)

                lengths(0, 0)
                take_qk(0, 0)
                take_v(0)
                highest(0, 0)
                lengths(1, 1)
                take_qk(1, 1)
                take_v(1)
                with dve.Fori(0, TILES // 2) as i:
                    for u in range(2):
                        n = 2 * i + u
                        dve.wait_ge(exp_done, n + 1)
                        nc.vector.tensor_reduce(red[:, u, 1, :], s[:, u], AX.X, ALU.add).then_inc(step, 1)
                        dve.wait_ge(step, 2 * n + 1)
                        nc.vector.reciprocal(red[:, u, 2, :], red[:, u, 1, :]).then_inc(step, 1)
                        highest(n + 1, 1 - u)
                        lengths(n + 2, u)
                        take_qk(n + 2, u)
                        dve.wait_ge(step, 2 * n + 2)
                        dve.wait_ge(weighed, n + 2)
                        nc.vector.tensor_tensor(a[:, u, :].rearrange("p (h e) -> p h e", e=HEAD),
                                                bankO[0:TILE, 0:DIM].rearrange("p (h e) -> p h e", e=HEAD),
                                                red[:, u, 2, :].unsqueeze(2).to_broadcast([TILE, HEADS, HEAD]),
                                                ALU.mult).then_inc(a_done, 1)
                        dve.wait_ge(projected, n + 4)
                        take_v(u)
                        dve.wait_ge(out_done, n + 1)
                        tile = dst[:, bass.ds(n, 1), :]
                        nc.vector.tensor_tensor(tile, tile, bankO[0:TILE, 0:DIM].unsqueeze(1), ALU.add).then_inc(added, 1)

BLOCK = 256
SUBS = BLOCK // 128


def block_count(experts, picks):
    return (TOKENS * picks + experts * (BLOCK - 1)) // BLOCK


MOST_BLOCKS = block_count(16, 4)
MOST_OF_ONE = -(-TOKENS // BLOCK)


def clear_slots(t):
    nc = t.nc
    t.cleared = t.sem("cleared", lasting=True)
    zeros_done = t.sem("zeros_done")
    with t.block() as block:
        @block.gpsimd
        def _(pool):
            nc.gpsimd.memset(t.zeros[:], 0.0).then_inc(zeros_done, 1)

        @block.sync
        def _(sp):
            sp.wait_ge(zeros_done, 1)
            sp.dma_start(t.slots.rearrange("a s p d -> (a s p d)").rearrange("(p n d) -> p n d", p=128, d=HALF),
                         t.zeros[:].unsqueeze(1).to_broadcast([128, (MOST_BLOCKS + 1) * SUBS * 2, HALF])).then_inc(t.cleared, 16)


def place(t, masks, share, experts, rows, gate, slot, up_row, down_row):
    nc, w = t.nc, t.w
    K, E, B = len(masks), experts, block_count(experts, len(masks)) + 1
    with ExitStack() as st:
        taken = t.sbuf("taken_by", [TILE, TILES, E], st)
        counts, upto, keep = (t.sbuf(n, [128, E, TILES], st) for n in ("counts", "upto", "keep"))
        more = t.sbuf("more", [128, E, MOST_OF_ONE], st)
        blocks, end, ones = (t.sbuf(n, [128, E], st) for n in ("blocks", "end", "ones"))
        over = t.sbuf("over", [128, B, E], st)
        owner = t.sbuf("owner", [128, B], st)
        part = t.sbuf("part", [TILE, TILES, E], st)
        slot_f = t.sbuf("slot_f", [TILE, TILES, K], st)
        taken_done, ranked, step = t.sem("taken_done"), t.sem("ranked"), t.sem("step")
        rank = t.bank[0][0:TILE, 0:TILES * E]
        total = t.bank[1][:, 0:TILES * E]
        with t.block() as block:
            @block.tensor
            def _(pe):
                pe.wait_ge(taken_done, 1)
                nc.tensor.matmul(rank, w["before"][:], flat(taken[:]), start=True, stop=True)
                nc.tensor.matmul(total, w["all"][:], flat(taken[:]), start=True, stop=True).then_inc(ranked, 1)

            @block.vector
            def _(dve):
                one = Steps(dve, step)
                for j in range(1, K):
                    one(nc.vector.tensor_tensor(taken[:], taken[:] if j > 1 else masks[0][:], masks[j][:], ALU.add))
                nc.vector.memset(ones[:], 1.0).then_inc(taken_done, 1)
                one(nc.vector.memset(keep[:], 1.0))
                one(nc.vector.memset(keep[:, :, 0:1], 0.0))
                dve.wait_ge(ranked, 1)
                one(nc.vector.tensor_copy(counts[:], total.rearrange("p (i e) -> p e i", e=E)))
                one(nc.vector.tensor_tensor_scan(flat(upto[:]), flat(keep[:]), flat(counts[:]), 0.0, ALU.mult, ALU.add))
                one(nc.vector.tensor_tensor(more[:], upto[:, :, TILES - 1:TILES].to_broadcast([128, E, MOST_OF_ONE]),
                                            w["full"][:].unsqueeze(1).to_broadcast([128, E, MOST_OF_ONE]), ALU.is_gt))
                one(nc.vector.tensor_reduce(blocks[:], more[:], AX.X, ALU.add))
                one(nc.vector.tensor_tensor_scan(end[:], ones[:], blocks[:], 0.0, ALU.mult, ALU.add))
                one(nc.vector.tensor_tensor(over[:], w["block"][:, 0:B].unsqueeze(2).to_broadcast([128, B, E]),
                                            end[:].unsqueeze(1).to_broadcast([128, B, E]), ALU.is_ge))
                one(nc.vector.tensor_reduce(owner[:], over[:], AX.X, ALU.add))
                one(nc.vector.tensor_scalar(owner[:], owner[:], float(E - 1), None, ALU.min))
                nc.vector.tensor_scalar(up_row[:], owner[:], float(rows), w["lane"][:], ALU.mult, ALU.add)
                nc.vector.tensor_scalar(down_row[:], owner[:], 128.0, w["lane"][:], ALU.mult, ALU.add)
                one(nc.vector.tensor_tensor(blocks[:], end[:], blocks[:], ALU.subtract))
                one(nc.vector.tensor_tensor(upto[:], upto[:], counts[:], ALU.subtract))
                one(nc.vector.scalar_tensor_tensor(upto[:], blocks[:].unsqueeze(2).to_broadcast([128, E, TILES]), float(BLOCK),
                                                   upto[:], ALU.mult, ALU.add))
                one(nc.vector.tensor_tensor(taken[:], upto[0:TILE].rearrange("p e i -> p i e"),
                                            rank.rearrange("p (i e) -> p i e", e=E), ALU.add))
                for j in range(K):
                    one(nc.vector.tensor_tensor(part[:], taken[:], masks[j][:], ALU.mult))
                    one(nc.vector.tensor_reduce(slot_f[:, :, j], part[:], AX.X, ALU.add))
                    one(nc.vector.tensor_tensor(part[:], share[:], masks[j][:], ALU.mult))
                    one(nc.vector.tensor_reduce(gate[:, :, j], part[:], AX.X, ALU.add))
                nc.vector.tensor_copy(slot[:], slot_f[:])


def experts(t, name, src, dst, masks, share, count, rows, func, gated, gain=None, bias=None, expert_gain=None):
    nc, w, args = t.nc, t.w, t.args
    K, B, M = len(masks), block_count(count, len(masks)), HIDDEN // 128
    ups = [args[f"{name}_up"]] + ([args[f"{name}_gate"]] if gated else [])
    ups = [a.rearrange("e p k m -> (e p) (k m)") for a in ups]
    downs = args[f"{name}_down"].rearrange("e p m d -> (e p) (m d)")
    N = len(ups)
    LOADS = N + 1
    STAGES = 4
    U32 = mybir.dt.uint32
    with ExitStack() as st:
        gate = t.sbuf("gate_of", [TILE, TILES, K], st)
        slot = t.sbuf("slot_of", [TILE, TILES, K], st, U32)
        up_row, down_row = (t.sbuf(n, [128, B + 1], st, U32) for n in ("up_row", "down_row"))
        place(t, masks, share, count, rows, gate, slot, up_row, down_row)
        wu = t.sbuf("wu", [rows, 2, N, 2 * HIDDEN], st)
        wd = t.sbuf("wd", [128, 2, M * DIM], st)
        row = t.sbuf("row", [128, 2, 2], st, U32)
        own_gain = t.sbuf("own_gain", [HALF, 2, 2], st)
        tokens = t.sbuf("tokens", [TILE, STAGES, DIM], st)
        to = t.sbuf("to", [TILE, STAGES, K], st, U32)
        x = t.sbuf("xblock", [128, 2, SUBS, DIM], st)
        xT = t.sbuf("xTblock", [HALF + 1, 2, 2, BLOCK], st)
        hid = t.sbuf("hid", [128, M, BLOCK], st)
        sa = t.sbuf("sa", [128, 2, BLOCK], st)
        y = t.sbuf("yblock", [128, 2, SUBS, DIM], st)
        bankU, bankX, bankY = t.bank[0:3], t.bank[3], (t.bank[4:6], t.bank[6:8])
        slots_flat = t.slots[0:B].rearrange("a s p d -> (a s p) d")
        results_flat = t.results[0:B].rearrange("a s p d -> (a s p) d")
        ones_done, row_ready, staged = t.sem("ones_done"), t.sem("row_ready"), t.sem("staged")
        loaded, used = [t.sem("loaded_even", lasting=True), t.sem("loaded_odd", lasting=True)], t.sem("used")
        gain_in = [t.sem("gain_in_even", lasting=True), t.sem("gain_in_odd", lasting=True)]
        sorted_ = [t.sem(f"sorted_{v}", lasting=True) for v in range(STAGES)]
        x_in, stored = [t.sem("x_in_even"), t.sem("x_in_odd")], [t.sem("stored_even"), t.sem("stored_odd")]
        turned, xT_done, up_done, silu_done, hid_done, down, y_done, y_free = (
            t.sem(n) for n in ("turned", "xT_done", "up_done", "silu_done", "hid_done", "down", "y_done", "y_free"))
        with t.block() as block:
            @block.gpsimd
            def _(pool):
                def load(b, v, n):
                    at = bass.ds(b, 1)
                    nc.gpsimd.tensor_copy(row[:, v, 0:1], up_row[:, at])
                    nc.gpsimd.tensor_copy(row[:, v, 1:2], down_row[:, at]).then_inc(row_ready, 1)
                    pool.wait_ge(row_ready, n)
                    pool.sem_inc(t.passed, 1)
                    for i, up in enumerate(ups):
                        nc.gpsimd.indirect_dma_start(wu[:, v, i, :], None, up, bass.IndirectOffsetOnAxis(row[0:rows, v, 0:1], 0)
                                                     ).then_inc(loaded[v], 16)
                    nc.gpsimd.indirect_dma_start(wd[:, v, :], None, downs, bass.IndirectOffsetOnAxis(row[:, v, 1:2], 0)
                                                 ).then_inc(loaded[v], 16)
                    if expert_gain is not None:
                        load_gain(v)

                def load_gain(v):
                    nc.gpsimd.indirect_dma_start(own_gain[:, v, :], None, expert_gain,
                                                 bass.IndirectOffsetOnAxis(row[0:HALF, v, 0:1], 0)).then_inc(gain_in[v], 16)

                load(0, 0, 1)
                pool.wait_ge(t.cleared, 16)

                def sort(n, v):
                    nc.gpsimd.tensor_copy(tokens[:, v:v + 1, :], src[:, bass.ds(n, 1), :])
                    nc.gpsimd.tensor_copy(to[:, v:v + 1, :], slot[:, bass.ds(n, 1), :]).then_inc(staged, 1)
                    pool.wait_ge(staged, n + 1)
                    pool.sem_inc(t.passed, 1)
                    for j in range(K):
                        nc.gpsimd.indirect_dma_start(slots_flat, bass.IndirectOffsetOnAxis(to[:, v, j:j + 1], 0),
                                                     tokens[:, v, :], None).then_inc(sorted_[v], 16)

                for v in range(STAGES):
                    sort(v, v)
                with pool.Fori(1, TILES // STAGES) as i:
                    for v in range(STAGES):
                        pool.wait_ge(sorted_[v], 16 * K * i)
                        pool.sem_inc(t.passed, 1)
                        sort(STAGES * i + v, v)
                load(1, 1, 2)
                with pool.Fori(0, B // 2 - 1) as i:
                    for v in range(2):
                        pool.wait_ge(used, 2 * i + v + 1)
                        pool.sem_inc(t.passed, 1)
                        load(2 * i + v + 2, v, 2 * i + v + 3)
                if expert_gain is not None:
                    pool.wait_ge(used, B - 1)
                    nc.gpsimd.tensor_copy(row[:, 0, 0:1], up_row[:, B:B + 1]).then_inc(row_ready, 1)
                    pool.wait_ge(row_ready, B + 1)
                    load_gain(0)

            @block.sync
            def _(sp):
                def load(b, v):
                    sp.dma_start(x[:, v], t.slots[b].rearrange("a s p d -> p (a s) d") if not isinstance(b, int)
                                 else t.slots[b].rearrange("s p d -> p s d")).then_inc(x_in[v], 16)
                for v in range(STAGES):
                    sp.wait_ge(sorted_[v], 16 * K * (TILES // STAGES))
                load(0, 0)
                with sp.Fori(0, B // 2) as i:
                    for v in range(2):
                        b = 2 * i + v
                        sp.wait_ge(turned, b + 1)
                        load(bass.ds(b + 1, 1), 1 - v)
                        sp.wait_ge(y_done, b + 3)
                        sp.dma_start(t.results[bass.ds(b, 1)].rearrange("a s p d -> p (a s) d"), y[:, v]).then_inc(stored[v], 16)
                        sp.wait_ge(stored[v], 16 * i + 16)
                        sp.sem_inc(y_free, 1)
                sp.wait_ge(x_in[0], 16 * (B // 2) + 16)

            @block.tensor
            def _(pe):
                def turn_(v):
                    for s in range(SUBS):
                        for k in range(2):
                            last = nc.tensor.transpose(bankX[0:HALF, BLOCK * k + 128 * s:BLOCK * k + 128 * (s + 1)],
                                                       x[:, v, s, HALF * k:HALF * (k + 1)], w["ident"][:])
                    last.then_inc(turned, 1)

                if rows > HALF:
                    pe.wait_ge(ones_done, 1)
                pe.wait_ge(x_in[0], 16)
                turn_(0)
                with pe.Fori(0, B // 2) as i:
                    for v in range(2):
                        b = 2 * i + v
                        pe.wait_ge(xT_done, b + 1)
                        pe.wait_ge(loaded[v], 16 * LOADS * i + 16 * LOADS)

                        def up(m):
                            pe.wait_ge(hid_done, b * M + m + 1)
                            for n in range(N):
                                for k in range(2):
                                    part = rows if k == 0 else HALF
                                    last = nc.tensor.matmul(bankU[m % 3][:, BLOCK * n:BLOCK * (n + 1)],
                                                            wu[0:part, v, n, HIDDEN * k + 128 * m:HIDDEN * k + 128 * (m + 1)],
                                                            xT[0:part, v, k, :], start=(k == 0), stop=(k == 1))
                            last.then_inc(up_done, 1)

                        def down_(m):
                            pe.wait_ge(hid_done, b * M + m + 4)
                            if m == 0:
                                pe.wait_ge(y_done, b + 1)
                            for s in range(SUBS):
                                last = nc.tensor.matmul(bankY[v][s][:, 0:DIM], hid[:, m, 128 * s:128 * (s + 1)],
                                                        wd[:, v, DIM * m:DIM * (m + 1)], start=(m == 0), stop=(m == M - 1))
                            last.then_inc(down, 1)

                        up(0)
                        up(1)
                        for m in range(2, M):
                            up(m)
                            down_(m - 2)
                        pe.wait_ge(x_in[1 - v], 16 * i + (16 if v == 0 else 32))
                        turn_(1 - v)
                        down_(M - 2)
                        down_(M - 1)
                        pe.drain().then_inc(used, 1)

            @block.scalar
            def _(act):
                def take_xT(v, n):
                    act.wait_ge(turned, n)
                    for k in range(2):
                        if expert_gain is not None:
                            scale = own_gain[:, v, k:k + 1]
                        else:
                            scale = 1.0 if gain is None else gain[0:HALF, k:k + 1]
                        last = nc.scalar.activation(xT[0:HALF, v, k, :], bankX[0:HALF, BLOCK * k:BLOCK * (k + 1)], ACT.Identity,
                                                    scale=scale, bias=0.0 if bias is None else bias[0:HALF, k:k + 1])
                    last.then_inc(xT_done, 1)

                if not gated:
                    act.sem_inc(hid_done, 3)
                if expert_gain is not None:
                    act.wait_ge(gain_in[0], 16)
                take_xT(0, 1)
                with act.Fori(0, B // 2) as i:
                    for v in range(2):
                        b = 2 * i + v
                        for m in range(M):
                            act.wait_ge(up_done, b * M + m + 1)
                            if gated:
                                act.wait_ge(hid_done, b * M + m + 2)
                                nc.scalar.activation(sa[:, m % 2, :], bankU[m % 3][:, 0:BLOCK], func).then_inc(silu_done, 1)
                            else:
                                act.wait_ge(down, b * M + m + 1)
                                nc.scalar.activation(hid[:, m, :], bankU[m % 3][:, 0:BLOCK], func).then_inc(hid_done, 1)
                        if expert_gain is not None:
                            act.wait_ge(gain_in[1 - v], 16 * i + (32 if v else 16))
                        take_xT(1 - v, b + 2)

            @block.vector
            def _(dve):
                if rows > HALF:
                    nc.vector.memset(xT[HALF:HALF + 1], 1.0).then_inc(ones_done, 1)
                dve.sem_inc(down, M)
                dve.sem_inc(y_done, 2)
                dve.sem_inc(y_free, 2)
                if gated:
                    dve.sem_inc(hid_done, 3)
                with dve.Fori(0, B // 2) as i:
                    for v in range(2):
                        b = 2 * i + v
                        if gated:
                            for m in range(M):
                                dve.wait_ge(silu_done, b * M + m + 1)
                                dve.wait_ge(down, b * M + m + 1)
                                nc.vector.tensor_tensor(hid[:, m, :], sa[:, m % 2, :], bankU[m % 3][:, BLOCK:2 * BLOCK],
                                                        ALU.mult).then_inc(hid_done, 1)
                        dve.wait_ge(down, b * M + 2 * M)
                        dve.wait_ge(y_free, b + 1)
                        for s in range(SUBS):
                            last = nc.vector.tensor_copy(y[:, v, s, :], bankY[v][s][:, 0:DIM])
                        last.then_inc(y_done, 1)

        with ExitStack() as inner:
            back = t.sbuf("back", [TILE, STAGES, K, DIM], inner)
            here = t.sbuf("here", [TILE, STAGES, K], inner, U32)
            fetched, staged, summed = [t.sem(f"fetched_{v}", lasting=True) for v in range(STAGES)], t.sem("staged"), t.sem("summed")
            with t.block() as block:
                @block.gpsimd
                def _(pool):
                    with pool.Fori(0, TILES // STAGES) as i:
                        for v in range(STAGES):
                            pool.wait_ge(summed, K * (STAGES * i + v + 1))
                            pool.sem_inc(t.passed, 1)
                            nc.gpsimd.tensor_copy(here[:, v:v + 1, :], slot[:, bass.ds(STAGES * i + v, 1), :]).then_inc(staged, 1)
                            pool.wait_ge(staged, STAGES * i + v + 1)
                            pool.sem_inc(t.passed, 1)
                            for j in range(K):
                                nc.gpsimd.indirect_dma_start(back[:, v, j, :], None, results_flat,
                                                             bass.IndirectOffsetOnAxis(here[:, v, j:j + 1], 0)
                                                             ).then_inc(fetched[v], 16)

                @block.vector
                def _(dve):
                    dve.sem_inc(summed, STAGES * K)
                    with dve.Fori(0, TILES // STAGES) as i:
                        for v in range(STAGES):
                            tile = dst[:, bass.ds(STAGES * i + v, 1), :]
                            dve.wait_ge(fetched[v], 16 * K * i + 16 * K)
                            for j in range(K):
                                dve.wait_ge(summed, K * (STAGES * (i + 1) + v) + j)
                                nc.vector.scalar_tensor_tensor(tile, back[:, v, j:j + 1, :],
                                                               gate[:, bass.ds(STAGES * i + v, 1), j:j + 1],
                                                               tile, ALU.mult, ALU.add).then_inc(summed, 1)


def gates(t, w, rows):
    return [w[0:rows, 0, :], w[0:HALF, 1, :]]


def xT_tile(t, rows):
    return lambda i, k: t.xT[0:rows if k == 0 else HALF, k, TILE * i:TILE * (i + 1)]


def add_into(t, dst, src):
    nc = t.nc
    done = t.sem("added_into")
    with t.block() as block:
        @block.vector
        def _(dve):
            nc.vector.tensor_tensor(flat(dst[:]), flat(dst[:]), flat(src[:]), ALU.add).then_inc(done, 1)


def layer1_ffn(t):
    w = t.w
    normalise(t, t.h, 1e-5, keep=t.x, feature_major=False)
    normalise(t, t.x, 1e-5, gain=w["L1_ln1_g"], bias=w["L1_ln1_b"])
    heads_attention(t, w["L1_qkv"], w["L1_proj"], t.x, unit=False)
    add_into(t, t.h, t.x)
    normalise(t, t.x, 1e-5, keep=t.x, gain=w["L1_ln2_g"], bias=w["L1_ln2_b"])
    with ExitStack() as st:
        share = t.sbuf("share8", [TILE, TILES, 8], st)
        shareT = t.sbuf("shareT", [8, 1, TOKENS], st)
        picked = [t.sbuf(f"pick{j}", [TILE, TILES, 8], st) for j in range(2)]
        route(t, xT_tile(t, HALF + 1), gates(t, w["L1_gate"], HALF + 1), 8, 2, masks=picked, weights=share)
        turn(t, share, shareT[:, 0, :])
        add_back(t, shareT, t.h, lambda g, i: w["L1_b2"][:, g, :])
        experts(t, "L1", t.x, t.h, picked, share, 8, HALF + 1, ACT.Gelu, gated=False, gain=w["L1_ln2_g"], bias=w["L1_ln2_b"])


def layer2_mixer(t):
    normalise(t, t.h, 1e-5)
    heads_attention(t, t.w["L2_qkv"], t.w["L2_proj"], t.h, unit=True)

GROUPS2, SLOTS2, CAPACITY = 8, 64, 62
L2_EXPERTS = 8


def layer2_ffn(t):
    nc, w = t.nc, t.w
    E, M = L2_EXPERTS, HIDDEN // 128
    size = [TILE, TILES, E]
    normalise(t, t.h, 1e-5, keep=t.x)
    with ExitStack() as st:
        combine = t.sbuf("combine", [128, E // 2, TOKENS], st)
        taken = t.sbuf("taken", [HALF, 2, E, GROUPS2, SLOTS2], st)
        with ExitStack() as inner:
            m = [t.sbuf(f"choice{j}", size, inner) for j in range(2)]
            prob, chosen, slot, part = (t.sbuf(n, size, inner) for n in ("prob", "chosen", "slot", "part"))
            total = t.sbuf("total", [TILE, TILES], inner)
            route(t, xT_tile(t, HALF), gates(t, w["L2_gate"], HALF), E, 2, masks=m, total=total, probs=prob)
            ranked, step, slots_done = t.sem("ranked"), t.sem("step"), t.sem("slots_done")
            with t.block() as block:
                view = lambda x, par: x[:].rearrange("p (g a) e -> p g a e", a=2)[:, :, par, :]
                rank = lambda b: t.bank[b][0:TILE, 0:GROUPS2 * E]

                @block.tensor
                def _(pe):
                    for j in range(2):
                        for par in range(2):
                            ahead = [(0, 0), (0, 1), (1, 0), (1, 1)][0:2 * j + par]
                            terms = [(w["before"], view(m[j], par))] + [(w["all"], view(m[a], b)) for a, b in ahead]
                            for n, (lhs, rhs) in enumerate(terms):
                                last = nc.tensor.matmul(rank(2 * j + par).rearrange("p (g e) -> p g e", e=E), lhs[:, 0:TILE], rhs,
                                                        start=(n == 0), stop=(n == len(terms) - 1))
                    last.then_inc(ranked, 1)

                @block.vector
                def _(dve):
                    one = Steps(dve, step)
                    one(nc.vector.tensor_tensor(chosen[:], m[0][:], m[1][:], ALU.add))
                    one(nc.vector.tensor_tensor(prob[:], prob[:], chosen[:], ALU.mult))
                    dve.wait_ge(ranked, 1)
                    for j in range(2):
                        for par in range(2):
                            one(nc.vector.tensor_tensor(view((slot, part)[j], par), view(m[j], par),
                                                        rank(2 * j + par).rearrange("p (g e) -> p g e", e=E), ALU.mult))
                    one(nc.vector.tensor_tensor(slot[:], slot[:], part[:], ALU.add))
                    one(nc.vector.tensor_tensor(slot[:], slot[:], chosen[:], ALU.add))
                    nc.vector.tensor_scalar(slot[:], slot[:], -1.0, None, ALU.add).then_inc(slots_done, 1)

            xs = t.sbuf("xs2", [TILE, 2, DIM], inner)
            hot = t.sbuf("hot", [TILE, 2, E, SLOTS2], inner)
            gated = t.sbuf("gated", [TILE, 2, E, SLOTS2], inner)
            staged, hot_done, gated_done, filled, taken_done, turned, combine_done = (
                t.sem(n) for n in ("staged", "hot_done", "gated_done", "filled", "taken_done", "turned", "combine_done"))
            full = [TILE, E, SLOTS2]
            with t.block() as block:
                @block.vector
                def _(dve):
                    with dve.Fori(0, GROUPS2) as g:
                        dve.wait_ge(filled, g + 1)
                        dve.wait_ge(turned, 2 * g + 2)
                        for u in range(2):
                            at = bass.ds(2 * g + u, 1)
                            nc.vector.tensor_tensor(
                                hot[:, u], w["slot"][:].unsqueeze(1).to_broadcast(full),
                                slot[:, at, :].rearrange("p a e -> p (a e)").unsqueeze(2).to_broadcast(full), ALU.is_equal).then_inc(hot_done, 1)
                        for u in range(2):
                            at = bass.ds(2 * g + u, 1)
                            dve.wait_ge(hot_done, 2 * g + u + 1)
                            nc.vector.tensor_tensor(
                                gated[:, u], hot[:, u],
                                prob[:, at, :].rearrange("p a e -> p (a e)").unsqueeze(2).to_broadcast(full), ALU.mult).then_inc(gated_done, 1)

                @block.gpsimd
                def _(pool):
                    with pool.Fori(0, GROUPS2) as g:
                        pool.wait_ge(filled, g + 1)
                        pool.sem_inc(t.passed, 1)
                        nc.gpsimd.tensor_copy(xs[:], t.x[:, bass.ds(2 * g, 2), :]).then_inc(staged, 1)

                @block.tensor
                def _(pe):
                    pe.sem_inc(filled, 1)
                    pe.sem_inc(turned, 2)
                    with pe.Fori(0, GROUPS2) as g:
                        pe.wait_ge(staged, g + 1)
                        pe.wait_ge(hot_done, 2 * g + 2)
                        pe.wait_ge(taken_done, 2 * g + 1)
                        for k in range(2):
                            for u in range(2):
                                last = nc.tensor.matmul(t.bank[k][0:HALF, :], xs[:, u, HALF * k:HALF * (k + 1)],
                                                        hot[:, u].rearrange("p e c -> p (e c)"), start=(u == 0), stop=(u == 1))
                        last.then_inc(filled, 1)
                        for u in range(2):
                            pe.wait_ge(gated_done, 2 * g + u + 1)
                            pe.wait_ge(combine_done, 2 * g + u + 1)
                            for b in range(E // 2):
                                last = nc.tensor.transpose(t.bank[2 + u][:, TILE * b:TILE * (b + 1)],
                                                           gated[:, u, 2 * b:2 * b + 2, :].rearrange("p e c -> p (e c)"),
                                                           w["ident"][0:TILE, 0:TILE])
                            last.then_inc(turned, 1)

                @block.scalar
                def _(act):
                    act.sem_inc(taken_done, 1)
                    act.sem_inc(combine_done, 2)
                    with act.Fori(0, GROUPS2) as g:
                        for k in range(2):
                            act.wait_ge(filled, g + 2)
                            act.sem_inc(t.passed, 1)
                            nc.scalar.activation(taken[:, k, :, bass.ds(g, 1), :].rearrange("p e g c -> p e (g c)"),
                                                 t.bank[k][0:HALF, :].rearrange("p (e c) -> p e c", e=E), ACT.Identity).then_inc(taken_done, 1)
                        for u in range(2):
                            act.wait_ge(turned, 2 * g + u + 3)
                            act.sem_inc(t.passed, 1)
                            nc.scalar.activation(combine[:, :, bass.ds(TILE * (2 * g + u), TILE)],
                                                 t.bank[2 + u][:, 0:4 * TILE].rearrange("p (b n) -> p b n", n=TILE),
                                                 ACT.Identity).then_inc(combine_done, 1)
        given = t.sbuf("given", [128, E // 2, GROUPS2, DIM], st)
        inner = ExitStack()
        wu = t.sbuf("wu2", [HALF, 2, 2, HIDDEN], inner)
        wd = t.sbuf("wd2", [128, 2, M, DIM], inner)
        hid = t.sbuf("hid2", [128, 2, M, GROUPS2 * SLOTS2], inner)
        loaded, used = [t.sem("loaded_even"), t.sem("loaded_odd")], [t.sem("used_even"), t.sem("used_odd")]
        up_done, hid_done, down, given_done = t.sem("up_done"), t.sem("hid_done"), t.sem("down"), t.sem("given_done")
        with t.block() as block:
            @block.sync
            def _(sp):
                for v in range(2):
                    sp.dma_start(wu[:, v], t.args["L2_up"][v]).then_inc(loaded[v], 16)
                    sp.dma_start(wd[:, v], t.args["L2_down"][v]).then_inc(loaded[v], 16)
                with sp.Fori(0, E // 2 - 1) as i:
                    for v in range(2):
                        sp.wait_ge(used[v], i + 1)
                        at = bass.ds(2 * i + v + 2, 1)
                        sp.dma_start(wu[:, v], t.args["L2_up"][at].rearrange("a p k m -> (a p) k m")).then_inc(loaded[v], 16)
                        sp.dma_start(wd[:, v], t.args["L2_down"][at].rearrange("a p m d -> (a p) m d")).then_inc(loaded[v], 16)

            @block.tensor
            def _(pe):
                pe.sem_inc(down, 2 * GROUPS2)
                with pe.Fori(0, E // 2) as i:
                    for v in range(2):
                        e = 2 * i + v
                        pe.wait_ge(loaded[v], 32 * i + 32)
                        for m_ in range(M):
                            pe.wait_ge(hid_done, M * e + m_ + 1)
                            for k in range(2):
                                last = nc.tensor.matmul(t.bank[m_ % 2][:, :], wu[:, v, k, 128 * m_:128 * (m_ + 1)],
                                                        taken[:, k, bass.ds(e, 1), :, :].rearrange("p a g c -> p (a g c)"),
                                                        start=(k == 0), stop=(k == 1))
                            last.then_inc(up_done, 1)
                    for v in range(2):
                        e = 2 * i + v
                        pe.wait_ge(hid_done, M * e + M + 2)
                        for g in range(GROUPS2):
                            pe.wait_ge(given_done, GROUPS2 * e + g + 1)
                            for m_ in range(M):
                                last = nc.tensor.matmul(t.bank[2 + g % 4][SLOTS2 * v:SLOTS2 * (v + 1), 0:DIM],
                                                        hid[:, v, m_, SLOTS2 * g:SLOTS2 * (g + 1)], wd[:, v, m_, :],
                                                        start=(m_ == 0), stop=(m_ == M - 1))
                            last.then_inc(down, 1)
                        pe.drain().then_inc(used[v], 1)

            @block.scalar
            def _(act):
                act.sem_inc(hid_done, 2)
                with act.Fori(0, E // 2) as i:
                    for v in range(2):
                        e = 2 * i + v
                        for m_ in range(M):
                            act.wait_ge(up_done, M * e + m_ + 1)
                            if m_ == 0:
                                act.wait_ge(down, GROUPS2 * e + GROUPS2)
                            nc.scalar.activation(hid[:, v, m_, :], t.bank[m_ % 2][:, :], ACT.Relu).then_inc(hid_done, 1)

            @block.vector
            def _(dve):
                dve.sem_inc(given_done, 4)
                with dve.Fori(0, E // 2) as i:
                    for v in range(2):
                        for g in range(GROUPS2):
                            dve.wait_ge(down, GROUPS2 * (2 * i + v) + g + 1 + 2 * GROUPS2)
                            rows = slice(SLOTS2 * v, SLOTS2 * (v + 1))
                            nc.vector.tensor_copy(given[rows, bass.ds(i, 1), g:g + 1, :].rearrange("p a g d -> p (a g) d"),
                                                  t.bank[2 + g % 4][rows, 0:DIM].unsqueeze(1)).then_inc(given_done, 1)
        inner.close()
        add_back(t, combine, t.h, lambda b, i: given[:, b, bass.ds(i, 1), :])


INNER = 2 * DIM
TAPS = 4


def layer3_mixer(t):
    nc, w = t.nc, t.w
    G = INNER // 128
    normalise(t, t.h, 1e-5, keep=t.x, feature_major=False)
    normalise(t, t.x, 1e-6, centred=False, gain=w["L3_g"])
    with ExitStack() as st:
        xc, sz, rate, u = (t.sbuf(n, [128, G, TOKENS], st) for n in ("xc", "sz", "rate3", "u3"))
        bc = t.sbuf("bc3", [2 * STATES + 1, TOKENS], st)
        coef = t.sbuf("coef3", [128, G, STATES], st)
        with ExitStack() as inner:
            xs, cv = t.sbuf("xs3", [128, G, CHUNK], inner), t.sbuf("cv", [128, G, CHUNK], inner)
            up, xs_done, conv_step, conv_done, xc_done, mixed, bc_done, stepped, rate_done = (
                t.sem(n) for n in ("up", "xs_done", "conv_step", "conv_done", "xc_done", "mixed", "bc_done", "stepped", "rate_done"))
            with t.block() as block:
                @block.tensor
                def _(pe):
                    pe.sem_inc(rate_done, G)
                    with pe.Fori(0, CHUNKS) as c:
                        at = bass.ds(CHUNK * c, CHUNK)
                        pe.wait_ge(rate_done, G * c + G)
                        for m in range(2 * G):
                            for k in range(2):
                                last = nc.tensor.matmul(t.bank[m][:, 0:CHUNK], w["L3_in"][:, k, 128 * m:128 * (m + 1)],
                                                        t.xT[0:HALF, k, at], start=(k == 0), stop=(k == 1))
                            last.then_inc(up, 1)
                        pe.wait_ge(xc_done, c + 1)
                        for g in range(G):
                            last = nc.tensor.matmul(t.bank[6][0:2 * STATES + 1, 0:CHUNK], w["L3_xproj"][:, g, :], xc[:, g, at],
                                                    start=(g == 0), stop=(g == G - 1))
                        last.then_inc(mixed, 1)
                        pe.wait_ge(bc_done, c + 1)
                        pe.sem_inc(t.passed, 1)
                        for g in range(G):
                            last = nc.tensor.matmul(t.bank[(7, 0, 1)[g]][:, 0:CHUNK], w["L3_dt"][:, 128 * g:128 * (g + 1)], bc[:, at],
                                                    start=True, stop=True)
                        last.then_inc(stepped, 1)

                @block.scalar
                def _(act):
                    nc.scalar.preload_act_table(ACT.Silu)
                    with act.Fori(0, CHUNKS) as c:
                        at = bass.ds(CHUNK * c, CHUNK)
                        for g in range(G):
                            act.wait_ge(up, 2 * G * c + g + 1)
                            nc.scalar.activation(xs[:, g, :], t.bank[g][:, 0:CHUNK], ACT.Identity).then_inc(xs_done, 1)
                        for g in range(G):
                            act.wait_ge(up, 2 * G * c + G + g + 1)
                            act.sem_inc(t.passed, 1)
                            nc.scalar.activation(sz[:, g, at], t.bank[G + g][:, 0:CHUNK], ACT.Silu)
                        act.wait_ge(conv_done, G * c + G)
                        act.sem_inc(t.passed, 1)
                        nc.scalar.activation(xc[:, :, at], cv[:], ACT.Silu).then_inc(xc_done, 1)
                        act.wait_ge(mixed, c + 1)
                        act.sem_inc(t.passed, 1)
                        nc.scalar.activation(bc[:, at], t.bank[6][0:2 * STATES + 1, 0:CHUNK], ACT.Identity).then_inc(bc_done, 1)

                @block.vector
                def _(dve):
                    one = Steps(dve, conv_step)
                    with dve.Fori(0, CHUNKS) as c:
                        one.enter(c, (TAPS - 1) * G)
                        at = bass.ds(CHUNK * c, CHUNK)
                        for g in range(G):
                            dve.wait_ge(xs_done, G * c + g + 1)
                            x_ = xs[:, g, :].rearrange("p (b t) -> p b t", t=SEQ)
                            y_ = cv[:, g, :].rearrange("p (b t) -> p b t", t=SEQ)
                            tap = lambda k: w["L3_conv"][:, g, k:k + 1]
                            one(nc.vector.tensor_scalar(cv[:, g, :], xs[:, g, :], tap(TAPS - 1), w["L3_conv_b"][:, g:g + 1], ALU.mult, ALU.add))
                            for back in range(1, TAPS):
                                ins = nc.vector.scalar_tensor_tensor(y_[:, :, back:], x_[:, :, 0:SEQ - back], tap(TAPS - 1 - back),
                                                                     y_[:, :, back:], ALU.mult, ALU.add)
                                if back < TAPS - 1:
                                    one(ins)
                                else:
                                    ins.then_inc(conv_done, 1)
                        dve.wait_ge(stepped, c + 1)
                        for g in range(G):
                            nc.vector.tensor_scalar(rate[:, g, at], t.bank[(7, 0, 1)[g]][:, 0:CHUNK], w["L3_b_dt"][:, g:g + 1], None,
                                                    ALU.add).then_inc(rate_done, 1)
                    one.leave(CHUNKS)
            softplus(t, rate)
            exp_done = t.sem("exp_done")
            with t.block() as block:
                @block.scalar
                def _(act):
                    nc.scalar.activation(coef[:], w["L3_A_log"][:], ACT.Exp).then_inc(exp_done, 1)

                @block.vector
                def _(dve):
                    nc.vector.tensor_tensor(flat(u[:]), flat(rate[:]), flat(xc[:]), ALU.mult)
                    dve.wait_ge(exp_done, 1)
                    nc.vector.tensor_scalar(coef[:], coef[:], -1.0, None, ALU.mult)
        scan(t, u, rate, coef, bc, xc, w["L3_D"], xc, bilinear=False)
        with t.block() as block:
            @block.vector
            def _(dve):
                nc.vector.tensor_tensor(flat(xc[:]), flat(xc[:]), flat(sz[:]), ALU.mult)
        add_back(t, xc, t.x, lambda g, i: w["L3_out"][:, g, :])
    with ExitStack() as st:
        plain = t.sbuf("plain", [TILE, TILES, DIM], st)
        picked = [t.sbuf(f"pick{j}", [TILE, TILES, 8], st) for j in range(2)]
        normalise(t, t.x, 1e-6, keep=plain, centred=False)
        gate = t.sbuf("gate3", [HALF, 2, 8], st)
        share = t.sbuf("share3", [TILE, TILES, 8], st)
        whole = t.sbuf("whole", [TILE, TILES], st)
        with t.block() as block:
            @block.vector
            def _(dve):
                for k in range(2):
                    nc.vector.tensor_scalar(gate[:, k, :], w["L3_router"][:, k, :], w["L3_g_moe"][:, k:k + 1], None, ALU.mult)
        route(t, xT_tile(t, HALF), gates(t, gate, HALF), 8, 2, masks=picked, weights=share)
        summed = t.sem("summed")
        with t.block() as block:
            @block.vector
            def _(dve):
                nc.vector.tensor_reduce(whole[:], share[:], AX.X, ALU.add).then_inc(summed, 1)
                dve.wait_ge(summed, 1)
                with dve.Fori(0, TILES // 4) as i:
                    for v in range(4):
                        at = bass.ds(4 * i + v, 1)
                        nc.vector.scalar_tensor_tensor(t.h[:, at, :], t.x[:, at, :], whole[:, at], t.h[:, at, :], ALU.mult, ALU.add)
        experts(t, "L3m", plain, t.h, picked, share, 8, HALF, ACT.Silu, gated=True,
                expert_gain=t.args["L3_g_exp"])


def layer3_ffn(t):
    normalise(t, t.h, 1e-5, keep=t.x)
    with ExitStack() as st:
        share = t.sbuf("share16", [TILE, TILES, 16], st)
        picked = [t.sbuf(f"pick{j}", [TILE, TILES, 16], st) for j in range(4)]
        route(t, xT_tile(t, HALF), gates(t, t.w["L3f_gate"], HALF), 16, 4, masks=picked, weights=share)
        experts(t, "L3f", t.x, t.h, picked, share, 16, HALF, ACT.Silu, gated=True)


def tower(nc, args, out):
    with ExitStack() as stack:
        t = Tower(nc, stack, args)
        embed(t)
        clear_slots(t)
        layer0_mixer(t)
        layer0_ffn(t)
        layer1_mixer(t)
        layer1_ffn(t)
        layer2_mixer(t)
        layer2_ffn(t)
        layer3_mixer(t)
        layer3_ffn(t)
        store(t, out, t.h)


def halves(w, bias=None):
    a = w.reshape(2, HALF, -1).transpose(1, 0, 2)
    if bias is None:
        return np.ascontiguousarray(a)
    extra = np.zeros((1, 2, a.shape[2]), np.float32)
    extra[0, 0] = bias.reshape(-1)
    return np.concatenate([a, extra], axis=0)


def columns(v, parts=HALF):
    return np.ascontiguousarray(v.reshape(-1, parts).T)


def stacked(parts):
    return np.ascontiguousarray(np.stack(parts))


def rows128(w):
    return np.ascontiguousarray(w.reshape(-1, 128, w.shape[1]).transpose(1, 0, 2))


def windows():
    inner = range(PATCH)
    spots = [(y, x) for y in inner for x in inner]
    spots += [(-1, x) for x in inner] + [(PATCH, x) for x in inner] + [(y, -1) for y in inner] + [(y, PATCH) for y in inner]
    return [(c, y, x) for c in range(CHANNELS) for y, x in spots]


READS = ((0, 0), (0, -1), (0, 1), (-1, 0), (1, 0))


def layout(inputs):
    f = {k: np.asarray(v) for k, v in inputs.items()}
    a = {}
    spots = windows()
    c, y, x = (np.array(v) for v in zip(*spots))
    padded = np.pad(f["x"], ((0, 0), (0, 0), (1, 1), (1, 1)))
    rows = PATCH * np.arange(GRID)
    px = padded[:, c[:, None, None], (y[:, None] + rows + 1)[:, :, None], (x[:, None] + rows + 1)[:, None, :]]
    seq = np.zeros((IMAGES, WINDOW, SEQ), np.float32)
    seq[:, :, 1:] = px.reshape(IMAGES, WINDOW, SEQ - 1)
    a["pixels"] = np.ascontiguousarray(seq.reshape(TILES, 2, WCHUNKS, WROWS, SEQ).transpose(0, 3, 2, 1, 4)
                                       .reshape(TILES, WROWS, WCHUNKS, TILE))
    wide = np.zeros((SHIFTS, WINDOW, DIM + 2), np.float32)
    stack = np.concatenate([f["L0_tok_proj_weight"], f["L0_tok_ln_weight"][None], f["L0_tok_ln_bias"][None]])
    stack = stack.reshape(DIM + 2, PATCH, PATCH, SHIFTS, CHANNELS)
    count = np.zeros(WINDOW, np.float32)
    for s, (dy, dx) in enumerate(READS):
        ys, xs = y - dy, x - dx
        ok = (ys >= 0) & (ys < PATCH) & (xs >= 0) & (xs < PATCH)
        wide[s, ok] = stack[:, ys[ok], xs[ok], s, c[ok]].T
        count[ok] += 1
    wide = wide.reshape(SHIFTS, WCHUNKS, WROWS, DIM + 2).transpose(2, 1, 0, 3)
    a["w_patch"] = np.ascontiguousarray(wide[..., :DIM])
    a["ln_gain"] = np.ascontiguousarray(wide[..., DIM:].transpose(0, 3, 1, 2))
    a["share"] = np.ascontiguousarray((count / PATCH_DIM).astype(np.float32).reshape(WCHUNKS, WROWS).T)
    a["patch_bias"] = f["L0_tok_proj_bias"].reshape(1, DIM)
    a["cls"] = f["cls_tok"].reshape(1, 1, DIM)
    a["c_ident"] = np.eye(128, dtype=np.float32)
    a["c_select"] = np.tile(np.eye(2 * STATES, dtype=np.float32), (3, 1))
    a["c_minus_one"] = np.full((128, 1), -1.0, np.float32)
    a["c_mean"] = np.full((HALF, HALF), 1.0 / DIM, np.float32)
    a["c_clamp"] = np.full((128, 1), -CENTRE / REACH, np.float32)
    for name in ("W_bc", "W_dt"):
        a["c_L0_" + name] = halves(f["L0_attn_" + name])
    a["c_L0_W_dtp"] = f["L0_attn_W_dtp"]
    a["c_L0_A_log"] = halves(f["L0_attn_A_log"])
    for name, key in (("b_dt", "b_dt"), ("rms", "rms_scale"), ("D", "D_param")):
        a["c_L0_" + name] = columns(f["L0_attn_" + key])
    a["c_first"] = np.tile(np.arange(16, 0, -1, dtype=np.float32), (128, 1))
    own = np.arange(TILE) // SEQ
    a["c_mask"] = np.where(own[:, None] == own[None, :], 0.0, MASKED).astype(np.float32)
    a["c_L0_enc"] = halves(f["L0_ffn_enc_w"], f["L0_ffn_enc_b"])
    a["c_L0_switch"] = np.concatenate([f["L0_ffn_sw_w"], f["L0_ffn_sw_b"][None]])
    a["c_L0_w1"] = halves(f["L0_ffn_w1"].transpose(1, 0, 2).reshape(DIM, -1))
    a["c_L0_b1"] = columns(f["L0_ffn_b1"], 128)
    a["c_L0_w2"] = np.ascontiguousarray(f["L0_ffn_w2"].reshape(L0_GROUPS, 128, DIM).transpose(1, 0, 2))
    a["c_L0_b2"] = f["L0_ffn_b2"].reshape(L0_EXPERTS, 1, DIM)
    row = np.arange(L0_GROUPS * 128).reshape(L0_GROUPS, 128) // L0_CODE
    a["c_L0_pair"] = (row[None] == np.arange(L0_EXPERTS)[:, None, None]).astype(np.float32)
    wq, wk, wv = (f["L1_attn_W" + x] for x in "qkv")
    a["c_L1_wqk"] = halves(np.concatenate([wq.T, wk.T], 1), np.concatenate([f["L1_attn_bq"], f["L1_attn_bk"]]))
    a["c_L1_wv"] = halves(wv.T, f["L1_attn_bv"])
    for name in ("ln1_g", "ln1_b", "ln2_g", "ln2_b"):
        a["c_L1_" + name] = columns(f["L1_ffn_" + name])
    a["c_L1_qkv"] = halves(f["L1_ffn_qkv_w"].T, np.zeros(3 * DIM, np.float32))
    a["c_L1_proj"] = halves(f["L1_ffn_proj_w"].T, f["L1_ffn_proj_b"])
    a["c_L1_gate"] = halves(f["L1_ffn_gate_w"].T, f["L1_ffn_gate_b"])
    a["c_L1_b2"] = f["L1_ffn_b2"].reshape(8, 1, DIM)
    a["L1_up"] = stacked([halves(f["L1_ffn_w1"][e].T, f["L1_ffn_b1"][e]) for e in range(8)])
    a["L1_down"] = stacked([rows128(f["L1_ffn_w2"][e].T) for e in range(8)])
    a["c_L2_qkv"] = halves(np.concatenate([f["L2_attn_Wq"], f["L2_attn_Wkv"]], 1), np.concatenate([f["L2_attn_bq"], f["L2_attn_bkv"]]))
    a["c_L2_proj"] = halves(f["L2_attn_Wproj"], f["L2_attn_bproj"])
    a["c_L2_scale"] = np.tile(f["L2_attn_scale"].reshape(1, HEADS), (TILE, 1))
    token = np.arange(TILE)
    a["c_before"] = (token[:, None] < token[None, :]).astype(np.float32)
    a["c_all"] = np.ones((TILE, 128), np.float32)
    a["c_full"] = np.tile(BLOCK * np.arange(MOST_OF_ONE, dtype=np.float32), (128, 1))
    a["c_block"] = np.tile(np.arange(MOST_BLOCKS + 1, dtype=np.float32), (128, 1))
    a["c_lane"] = np.arange(128, dtype=np.float32).reshape(128, 1)
    a["c_slot"] = np.tile(np.where(np.arange(SLOTS2) < CAPACITY, np.arange(SLOTS2), -5), (TILE, 1)).astype(np.float32)
    a["c_L2_gate"] = halves(f["L2_ffn_w_router"])
    a["L2_up"] = stacked([halves(x) for x in f["L2_ffn_wi"]])
    a["L2_down"] = stacked([rows128(x) for x in f["L2_ffn_wo"]])
    a["c_L3_g"] = columns(f["L3_attn_g_mamba"])
    a["c_L3_in"] = halves(f["L3_attn_w_in"])
    a["c_L3_conv"] = rows128(f["L3_attn_conv_w"])
    a["c_L3_conv_b"] = columns(f["L3_attn_conv_b"], 128)
    a["c_L3_xproj"] = rows128(f["L3_attn_w_xproj"])
    a["c_L3_dt"] = np.concatenate([np.zeros((2 * STATES, INNER), np.float32), f["L3_attn_w_dt"]])
    a["c_L3_b_dt"] = columns(f["L3_attn_b_dt"], 128)
    a["c_L3_A_log"] = rows128(f["L3_attn_A_log"])
    a["c_L3_D"] = columns(f["L3_attn_D_skip"], 128)
    a["c_L3_out"] = rows128(f["L3_attn_w_out"])
    a["c_L3_router"] = halves(f["L3_attn_w_router"])
    a["c_L3_g_moe"] = columns(f["L3_attn_g_moe"])
    a["L3_g_exp"] = np.ascontiguousarray(f["L3_attn_g_exp"].reshape(8, 2, HALF).transpose(0, 2, 1).reshape(8 * HALF, 2))
    a["L3m_up"] = stacked([halves(x) for x in f["L3_attn_w1"]])
    a["L3m_gate"] = stacked([halves(x) for x in f["L3_attn_w3"]])
    a["L3m_down"] = stacked([rows128(x) for x in f["L3_attn_w2"]])
    a["c_L3f_gate"] = halves(f["L3_ffn_router_w"].T)
    a["L3f_up"] = stacked([halves(x.T) for x in f["L3_ffn_w1"]])
    a["L3f_gate"] = stacked([halves(x.T) for x in f["L3_ffn_v1"]])
    a["L3f_down"] = stacked([rows128(x.T) for x in f["L3_ffn_w2"]])
    return a


def kernel(**inputs):
    import concourse.bacc as _bacc
    from concourse.bass_utils import run_bass_kernel_spmd as _run

    nc = _bacc.Bacc("TRN2", target_bir_lowering=False, num_devices=1)
    arrays = layout(inputs)
    args = {k: nc.dram_tensor(k, v.shape, F32, kind="ExternalInput").ap() for k, v in arrays.items()}
    out = nc.dram_tensor("out", (TOKENS, DIM), F32, kind="ExternalOutput").ap()
    tower(nc, args, out)
    r = _run(nc, [arrays], core_ids=[0])
    return r.results[0]["out"].reshape(IMAGES, SEQ, DIM)
```
